# Optimizing a Trainium2 kernel written in Bass

```python
import numpy as np
import jax
import jax.numpy as jnp

def _softmax(x, axis=-1):
    return jax.nn.softmax(x, axis=axis)

def _gelu(x):
    return jax.nn.gelu(x, approximate=True)

def _silu(x):
    return jax.nn.silu(x)

def _sigmoid(x):
    return jax.nn.sigmoid(x)

def _layernorm(x, axis=-1, eps=1e-05):
    m = jnp.mean(x, axis=axis, keepdims=True)
    v = jnp.var(x, axis=axis, keepdims=True)
    return (x - m) / jnp.sqrt(v + eps)

def _scatter_add(tgt, idx, src, axis=0):
    return tgt.at[idx].add(src)

def _segment_sum(src, seg, n):
    return jax.ops.segment_sum(src, seg, n)
kernel_name = 'mk_gnn_resnorm_d4_gnn_r64_6934a2'

def setup_inputs(seed: int=0):
    np.random.seed(seed)
    _w = jnp.asarray

    def _rec_inputs():
        import jax
        import jax.numpy as jnp
        _gk = jax.random.key(seed)
        x = -0.000202 + 1 * jax.random.normal(jax.random.fold_in(_gk, 1), (100000, 64), jnp.float32)
        src = jax.random.randint(jax.random.fold_in(_gk, 2), (50000,), 0, 100000, jnp.int32)
        dst = jnp.minimum((100000 * jax.random.uniform(jax.random.fold_in(_gk, 3), (50000,)) ** 2.0).astype(jnp.int32), 99999)
        _o = jnp.argsort(dst, stable=True)
        src = src[_o]
        dst = dst[_o]
        edge_weight = jax.random.uniform(jax.random.fold_in(_gk, 12), (50000,), jnp.float32, 0.0, 0.999999)
        edge_weight1 = jax.random.uniform(jax.random.fold_in(_gk, 13), (50000, 1), jnp.float32, 0.0, 0.999998)
        return (x, src, dst, edge_weight, edge_weight1)
    x, src, dst, edge_weight, edge_weight1 = _rec_inputs()

    def _L0_gnn_setup():
        import jax, jax.numpy as jnp
        import numpy as np
        N_NODES = 100000
        N_EDGES = 25000
        K = 5
        F_IN, F_HID, F_OUT = (64, 128, 64)

        def _gcn_norm(edge_weight, row, col):
            deg = jax.ops.segment_sum(edge_weight, col, num_segments=N_NODES)
            safe_deg = jnp.where(deg > 0, deg, 1.0)
            dis = jnp.where(deg > 0, jax.lax.rsqrt(safe_deg), 0.0)
            return dis[row] * edge_weight * dis[col]

        def _tag_conv(x, row, col, norm, W, b):
            out = x @ W[0]
            h = x
            for k in range(1, K + 1):
                msg = h[row] * norm[:, None]
                h = jax.ops.segment_sum(msg, col, num_segments=N_NODES)
                out = out + h @ W[k]
            return out + b
        key = jax.random.key(seed)
        ks = jax.random.split(key, 6)
        x = jax.random.normal(ks[0], (N_NODES, F_IN), dtype=jnp.float32)
        edge_index = jax.random.randint(ks[1], (2, N_EDGES), 0, N_NODES, dtype=jnp.int32)
        edge_weight = jax.random.uniform(ks[2], (N_EDGES,), dtype=jnp.float32)
        W0 = jax.random.normal(ks[3], (K + 1, F_IN, F_HID), dtype=jnp.float32) * 0.05
        b0 = jnp.zeros((F_HID,), dtype=jnp.float32)
        W1 = jax.random.normal(ks[4], (K + 1, F_HID, F_OUT), dtype=jnp.float32) * 0.05
        b1 = jnp.zeros((F_OUT,), dtype=jnp.float32)
        return {'x': x, 'edge_index': edge_index, 'edge_weight': edge_weight, 'W0': W0, 'b0': b0, 'W1': W1, 'b1': b1}
    _L0_gnn_all = _L0_gnn_setup()
    _L0_gnn_in = {k: v for k, v in _L0_gnn_all.items() if k in ('W0', 'b0', 'W1', 'b1')}
    del _L0_gnn_all

    def _L1_gnn_setup():
        import jax, jax.numpy as jnp
        import numpy as np
        N, E, D_IN, D, H = (50000, 12500, 64, 64, 4)
        key = jax.random.key(seed)
        ks = jax.random.split(key, 14)
        s = 0.05
        x = jax.random.normal(ks[0], (N, D_IN), jnp.float32)
        edge_index = jax.random.randint(ks[1], (2, E), 0, N, jnp.int32)
        return {'x': x, 'edge_index': edge_index, 'W_sl': jax.random.normal(ks[2], (D_IN, D), jnp.float32) * s, 'b_sl': jnp.zeros((D,), jnp.float32), 'W_sr': jax.random.normal(ks[3], (D_IN, D), jnp.float32) * s, 'Wg_l': jax.random.normal(ks[4], (D, H * D), jnp.float32) * s, 'bg_l': jnp.zeros((H * D,), jnp.float32), 'Wg_r': jax.random.normal(ks[5], (D, H * D), jnp.float32) * s, 'bg_r': jnp.zeros((H * D,), jnp.float32), 'att': jax.random.normal(ks[6], (H, D), jnp.float32) * s, 'b_gat': jnp.zeros((D,), jnp.float32), 'gamma': jnp.ones((D,), jnp.float32), 'beta': jnp.zeros((D,), jnp.float32)}
    _L1_gnn_all = _L1_gnn_setup()
    _L1_gnn_in = {k: v for k, v in _L1_gnn_all.items() if k in ('W_sl', 'b_sl', 'W_sr', 'Wg_l', 'bg_l', 'Wg_r', 'bg_r', 'att', 'b_gat', 'gamma', 'beta')}
    del _L1_gnn_all

    def _L2_gnn_setup():
        import jax, jax.numpy as jnp
        import numpy as np
        N_NODES = 50000
        N_EDGES = 12500
        C_IN = 64
        C_HID = 64
        key = jax.random.key(seed)
        k1, k2, k3, k4, k5 = jax.random.split(key, 5)
        x = jax.random.normal(k1, (N_NODES, C_IN), dtype=jnp.float32)
        edge_index = jax.random.randint(k2, (2, N_EDGES), 0, N_NODES, dtype=jnp.int64)
        edge_attr = jax.random.uniform(k3, (N_EDGES, 1), dtype=jnp.float32)
        W = jax.random.normal(k4, (C_IN, C_HID), dtype=jnp.float32) * (1.0 / np.sqrt(C_IN))
        root = jax.random.normal(k5, (C_IN, C_HID), dtype=jnp.float32) * (1.0 / np.sqrt(C_IN))
        bias = jnp.zeros((C_HID,), dtype=jnp.float32)
        return {'x': x, 'edge_index': edge_index, 'edge_attr': edge_attr, 'W': W, 'root': root, 'bias': bias}
    _L2_gnn_all = _L2_gnn_setup()
    _L2_gnn_in = {k: v for k, v in _L2_gnn_all.items() if k in ('W', 'root', 'bias')}
    del _L2_gnn_all

    def _L3_gnn_setup():
        import jax, jax.numpy as jnp
        import numpy as np
        N_NODES = 50000
        DIM = 64
        HEADS = 4
        N_EDGES = 12500
        NEG_SLOPE = 0.2
        key = jax.random.key(seed)
        ks = jax.random.split(key, 8)
        H, C = (HEADS, DIM)
        embedding = jax.random.normal(ks[0], (N_NODES, DIM), dtype=jnp.float32)
        graph = jax.random.randint(ks[1], (2, N_EDGES), 0, N_NODES, dtype=jnp.int64)
        s = 1.0 / np.sqrt(DIM)
        W = jax.random.normal(ks[2], (DIM, H * C), dtype=jnp.float32) * s
        att_src = jax.random.normal(ks[3], (H, C), dtype=jnp.float32) * s
        att_dst = jax.random.normal(ks[4], (H, C), dtype=jnp.float32) * s
        bias = jnp.zeros((H * C,), dtype=jnp.float32)
        dense_w = jax.random.normal(ks[5], (H * C, DIM), dtype=jnp.float32) / np.sqrt(H * C)
        dense_b = jnp.zeros((DIM,), dtype=jnp.float32)
        return {'embedding': embedding, 'graph': graph, 'W': W, 'att_src': att_src, 'att_dst': att_dst, 'bias': bias, 'dense_w': dense_w, 'dense_b': dense_b}
    _L3_gnn_all = _L3_gnn_setup()
    _L3_gnn_in = {k: v for k, v in _L3_gnn_all.items() if k in ('W', 'att_src', 'att_dst', 'bias', 'dense_w', 'dense_b')}
    del _L3_gnn_all
    return {'x': x, 'src': src, 'dst': dst, 'edge_weight': edge_weight, 'edge_weight1': edge_weight1, 'L0_gnn_W0': _L0_gnn_in['W0'], 'L0_gnn_b0': _L0_gnn_in['b0'], 'L0_gnn_W1': _L0_gnn_in['W1'], 'L0_gnn_b1': _L0_gnn_in['b1'], 'L1_gnn_W_sl': _L1_gnn_in['W_sl'], 'L1_gnn_b_sl': _L1_gnn_in['b_sl'], 'L1_gnn_W_sr': _L1_gnn_in['W_sr'], 'L1_gnn_Wg_l': _L1_gnn_in['Wg_l'], 'L1_gnn_bg_l': _L1_gnn_in['bg_l'], 'L1_gnn_Wg_r': _L1_gnn_in['Wg_r'], 'L1_gnn_bg_r': _L1_gnn_in['bg_r'], 'L1_gnn_att': _L1_gnn_in['att'], 'L1_gnn_b_gat': _L1_gnn_in['b_gat'], 'L1_gnn_gamma': _L1_gnn_in['gamma'], 'L1_gnn_beta': _L1_gnn_in['beta'], 'L2_gnn_W': _L2_gnn_in['W'], 'L2_gnn_root': _L2_gnn_in['root'], 'L2_gnn_bias': _L2_gnn_in['bias'], 'L3_gnn_W': _L3_gnn_in['W'], 'L3_gnn_att_src': _L3_gnn_in['att_src'], 'L3_gnn_att_dst': _L3_gnn_in['att_dst'], 'L3_gnn_bias': _L3_gnn_in['bias'], 'L3_gnn_dense_w': _L3_gnn_in['dense_w'], 'L3_gnn_dense_b': _L3_gnn_in['dense_b']}

def reference(x, src, dst, edge_weight, edge_weight1, L0_gnn_W0, L0_gnn_b0, L0_gnn_W1, L0_gnn_b1, L1_gnn_W_sl, L1_gnn_b_sl, L1_gnn_W_sr, L1_gnn_Wg_l, L1_gnn_bg_l, L1_gnn_Wg_r, L1_gnn_bg_r, L1_gnn_att, L1_gnn_b_gat, L1_gnn_gamma, L1_gnn_beta, L2_gnn_W, L2_gnn_root, L2_gnn_bias, L3_gnn_W, L3_gnn_att_src, L3_gnn_att_dst, L3_gnn_bias, L3_gnn_dense_w, L3_gnn_dense_b):
    import jax
    import jax.numpy as jnp

    def _L0_gnn_ref(x, edge_index, edge_weight, W0, b0, W1, b1):
        import jax, jax.numpy as jnp
        import numpy as np
        N_NODES = 100000
        N_EDGES = 25000
        K = 5
        F_IN, F_HID, F_OUT = (64, 128, 64)

        def _gcn_norm(edge_weight, row, col):
            deg = jax.ops.segment_sum(edge_weight, col, num_segments=N_NODES)
            safe_deg = jnp.where(deg > 0, deg, 1.0)
            dis = jnp.where(deg > 0, jax.lax.rsqrt(safe_deg), 0.0)
            return dis[row] * edge_weight * dis[col]

        def _tag_conv(x, row, col, norm, W, b):
            out = x @ W[0]
            h = x
            for k in range(1, K + 1):
                msg = h[row] * norm[:, None]
                h = jax.ops.segment_sum(msg, col, num_segments=N_NODES)
                out = out + h @ W[k]
            return out + b
        row, col = (edge_index[0], edge_index[1])
        norm = _gcn_norm(edge_weight, row, col)
        h = jax.nn.leaky_relu(_tag_conv(x, row, col, norm, W0, b0), negative_slope=0.01)
        h = jax.nn.leaky_relu(_tag_conv(h, row, col, norm, W1, b1), negative_slope=0.01)
        return h

    def _L1_gnn_ref(x, edge_index, W_sl, b_sl, W_sr, Wg_l, bg_l, Wg_r, bg_r, att, b_gat, gamma, beta):
        import jax, jax.numpy as jnp
        import numpy as np
        N, E, D_IN, D, H = (50000, 12500, 64, 64, 4)
        n = x.shape[0]
        heads, d = att.shape
        src, dst = (edge_index[0], edge_index[1])
        agg = jax.ops.segment_sum(x[src], dst, num_segments=n)
        cnt = jax.ops.segment_sum(jnp.ones(src.shape, x.dtype), dst, num_segments=n)
        agg = agg / jnp.maximum(cnt, 1.0)[:, None]
        h = agg @ W_sl + b_sl + x @ W_sr
        ar = jnp.arange(n, dtype=src.dtype)
        s2 = jnp.concatenate([src, ar])
        d2 = jnp.concatenate([dst, ar])
        xl = (h @ Wg_l + bg_l).reshape(n, heads, d)
        xr = (h @ Wg_r + bg_r).reshape(n, heads, d)
        z = jax.nn.leaky_relu(xl[s2] + xr[d2], 0.2)
        logit = jnp.einsum('ehd,hd->eh', z, att)
        m = jax.ops.segment_max(logit, d2, num_segments=n)
        a = jnp.exp(logit - m[d2])
        denom = jax.ops.segment_sum(a, d2, num_segments=n)
        alpha = a / denom[d2]
        out = jax.ops.segment_sum(alpha[:, :, None] * xl[s2], d2, num_segments=n)
        out = out.mean(axis=1) + b_gat
        mu = out.mean(-1, keepdims=True)
        var = out.var(-1, keepdims=True)
        out = (out - mu) * jax.lax.rsqrt(var + 1e-05) * gamma + beta
        return jax.nn.elu(out)

    def _L2_gnn_ref(x, edge_index, edge_attr, W, root, bias):
        import jax, jax.numpy as jnp
        import numpy as np
        N_NODES = 50000
        N_EDGES = 12500
        C_IN = 64
        C_HID = 64
        src = edge_index[0]
        dst = edge_index[1]
        n = x.shape[0]
        h = x @ W
        msg_sum = jax.ops.segment_sum(h[src], dst, num_segments=n)
        deg = jax.ops.segment_sum(jnp.ones_like(dst, dtype=h.dtype), dst, num_segments=n)
        agg = msg_sum / jnp.clip(deg, 1.0)[:, None]
        out = agg + x @ root + bias
        return jax.nn.relu(out)

    def _L3_gnn_ref(embedding, graph, W, att_src, att_dst, bias, dense_w, dense_b):
        import jax, jax.numpy as jnp
        import numpy as np
        N_NODES = 50000
        DIM = 64
        HEADS = 4
        N_EDGES = 12500
        NEG_SLOPE = 0.2
        N, D = embedding.shape
        H, C = att_src.shape
        x = (embedding @ W).reshape(N, H, C)
        ar = jnp.arange(N, dtype=graph.dtype)
        src = jnp.concatenate([graph[0], ar])
        dst = jnp.concatenate([graph[1], ar])
        a_src = jnp.einsum('nhc,hc->nh', x, att_src)
        a_dst = jnp.einsum('nhc,hc->nh', x, att_dst)
        alpha = jax.nn.leaky_relu(a_src[src] + a_dst[dst], NEG_SLOPE)
        amax = jax.ops.segment_max(alpha, dst, num_segments=N)
        amax = jnp.where(jnp.isfinite(amax), amax, 0.0)
        ex = jnp.exp(alpha - amax[dst])
        denom = jax.ops.segment_sum(ex, dst, num_segments=N)
        coef = ex / (denom[dst] + 1e-16)
        msg = x[src] * coef[:, :, None]
        agg = jax.ops.segment_sum(msg, dst, num_segments=N)
        gat_out = agg.reshape(N, H * C) + bias
        return gat_out @ dense_w + dense_b
    edge_index = jnp.stack([src, dst])
    x = _layernorm(x + _L0_gnn_ref(x, edge_index, edge_weight, L0_gnn_W0, L0_gnn_b0, L0_gnn_W1, L0_gnn_b1), axis=-1)
    x = _layernorm(x + _L1_gnn_ref(x, edge_index, L1_gnn_W_sl, L1_gnn_b_sl, L1_gnn_W_sr, L1_gnn_Wg_l, L1_gnn_bg_l, L1_gnn_Wg_r, L1_gnn_bg_r, L1_gnn_att, L1_gnn_b_gat, L1_gnn_gamma, L1_gnn_beta), axis=-1)
    x = _layernorm(x + _L2_gnn_ref(x, edge_index, edge_weight1, L2_gnn_W, L2_gnn_root, L2_gnn_bias), axis=-1)
    x = _layernorm(x + _L3_gnn_ref(x, edge_index, L3_gnn_W, L3_gnn_att_src, L3_gnn_att_dst, L3_gnn_bias, L3_gnn_dense_w, L3_gnn_dense_b), axis=-1)
    return x

_drawn_inputs = setup_inputs


def setup_inputs(seed=0):
    import zlib

    import numpy as np

    out = dict(_drawn_inputs(seed))
    spreads = {'L0_gnn_b0': (0.0, 0.29),
     'L0_gnn_b1': (0.0, 0.1),
     'L1_gnn_b_sl': (0.0, 0.1),
     'L1_gnn_bg_l': (0.0, 0.1),
     'L1_gnn_bg_r': (0.0, 2.0),
     'L1_gnn_b_gat': (0.0, 0.1),
     'L1_gnn_gamma': (1.0, 0.2),
     'L1_gnn_beta': (0.0, 0.1),
     'L2_gnn_bias': (0.0, 0.1),
     'L3_gnn_bias': (0.0, 0.1),
     'L3_gnn_dense_b': (0.0, 0.1)}
    factors = {'L1_gnn_Wg_r': 8.0, 'L1_gnn_att': 8.0}
    for name, (base, spread) in spreads.items():
        noise = np.random.default_rng([zlib.crc32(name.encode()), seed]).standard_normal(out[name].shape)
        drawn = base * np.exp(spread * noise) if base else spread * noise
        out[name] = jnp.asarray(drawn.astype(out[name].dtype))
    for name, factor in factors.items():
        out[name] = (out[name] * factor).astype(out[name].dtype)
    return out
```

```python
import concourse.bass as bass
from concourse import mybir
from concourse.alu_op_type import AluOpType as ALU
from contextlib import ExitStack

F32 = mybir.dt.float32
I32 = mybir.dt.int32
ACT = mybir.ActivationFunctionType
AX = mybir.AxisListType

N = 100000
E = 50000
D = 64
HID = 128
HOPS = 5
HEADS = 4
P = 128
TB = 4
LANES = 4
ROUNDS = -(-E // (P * TB * LANES))
TILES = ROUNDS * LANES * TB
EP = TILES * P
AB = EP // (P * TB)
SC = P * TB
NB = 8
CB = -(-N // (P * NB)) * P * NB
ABSENT = 1 << 20
NO_NODE = (1 << 17) - 1
EPS = 1e-5
LOW = -1.0e30
ENGINES = ("sync", "gpsimd", "scalar", "vector", "tensor")


class Steps:
    totals = {}

    def __init__(self, nc, sems, lanes, rounds, ahead=0):
        self.nc, self.sems, self.lanes, self.rounds, self.ahead = nc, sems, lanes, rounds, ahead
        self.list, self.place, self.per, self.base = [], {}, {}, {}

    def step(self, lane, name, engine, fn, after, dmas=0, early=False):
        key = (lane, name if dmas else engine)
        amount = 16 * dmas if dmas else 1
        if key not in self.base:
            if key not in self.sems:
                self.sems[key] = [self.nc.alloc_semaphore(f"done_{key[1]}_{lane}"), 0]
            self.base[key], self.per[key] = self.sems[key][1], 0
        self.per[key] += amount
        self.place[(lane, name)] = (key, self.per[key])
        self.list.append((lane, name, engine, fn, after, dmas, early, key))

    def emit(self, eng, which, i, s, shift):
        lane, name, engine, fn, after, dmas, early, key = s
        if engine != which:
            return
        waited = False
        r = i + shift
        for a in after:
            l, n, back = a if isinstance(a, tuple) else (lane, a, 0)
            k, upto = self.place[(l, n)]
            value = (r - back) * self.per[k] + (self.base[k] + upto)
            if isinstance(value, int) and value <= 0:
                continue
            eng.wait_ge(self.sems[k][0], value)
            if which in ("gpsimd", "sync"):
                eng.sem_inc(self.sems["waits_" + which][0], 1)
            waited = True
        made = fn(eng, r)
        if dmas:
            assert len(made) == dmas, (name, len(made), dmas)
            for m in made:
                m.then_inc(self.sems[key][0], 16)
        else:
            made.then_inc(self.sems[key][0], 1)

    def credit(self, eng, which):
        for lane, name, engine, fn, after, dmas, early, key in self.list:
            if engine == which and key in self.credits:
                n = self.credits[key]
                del self.credits[key]
                if not dmas:
                    eng.sem_inc(self.sems[key][0], n)
                else:
                    scratch, source = self.sems["scratch"]
                    at = self.sems["scratch_used"]
                    self.sems["scratch_used"] += 1
                    eng.dma_start(scratch[:, 8 * at:8 * at + 8], source).then_inc(self.sems[key][0], n)

    def sequence(self):
        if not self.ahead:
            return [], [(s, 0) for s in self.list], [(s, 0) for s in self.list]
        early = [[s for s in self.list if s[0] == l and s[6]] for l in range(self.lanes)]
        main = [[s for s in self.list if s[0] == l and not s[6]] for l in range(self.lanes)]
        pre = [(s, 0) for l in range(self.ahead) for s in early[l]]
        body, last = [], []
        for l in range(self.lanes):
            m = (l + self.ahead) % self.lanes
            nxt = 1 if l + self.ahead >= self.lanes else 0
            body += [(s, nxt) for s in early[m]] + [(s, 0) for s in main[l]]
            last += [(s, 0) for s in early[m] if not nxt] + [(s, 0) for s in main[l]]
        return pre, body, last

    def run(self):
        pre, body, last = self.sequence()
        self.credits = {}
        for k in self.base:
            if self.rounds > 1 and self.base[k] < self.per[k]:
                self.credits[k] = self.per[k]
                self.base[k] += self.per[k]
        block = self.nc.Block()
        with block:
            for which in ENGINES:
                def program(eng, which=which):
                    mine = any(s[2] == which for s in self.list)
                    if mine:
                        self.credit(eng, which)
                        for s, d in pre:
                            self.emit(eng, which, 0, s, d)
                        if self.rounds > 1:
                            with eng.Fori(0, self.rounds - 1, 1) as i:
                                for s, d in body:
                                    self.emit(eng, which, i, s, d)
                        for s, d in last:
                            self.emit(eng, which, self.rounds - 1, s, d)
                    if which == "sync":
                        for k in self.base:
                            if isinstance(k[1], str) and k[1].startswith("store"):
                                eng.wait_ge(self.sems[k][0], self.base[k] + self.per[k] * self.rounds)
                program_of(block, which)(program)
        for k in self.base:
            self.sems[k][1] = self.base[k] + self.per[k] * self.rounds


def program_of(block, which):
    return {"sync": block.sync, "gpsimd": block.gpsimd, "scalar": block.scalar,
            "vector": block.vector, "tensor": block.tensor}[which]


def ds(i, n):
    return bass.ds(i, n)


class Line:

    def __init__(self, steps, lane, first=()):
        self.steps, self.lane, self.n, self.after = steps, lane, 0, list(first)
        self.dma = 0
        self.stores = 0

    def _add(self, engine, fn, dmas=0, kind=""):
        self.n += 1
        name = f"{kind}{self.dma}" if dmas else f"s{self.n}"
        self.dma += bool(dmas)
        self.steps.step(self.lane, name, engine, fn, self.after, dmas)
        return name

    def on(self, engine, fn):
        self.after = [self._add(engine, fn)]

    def load(self, fn, dmas):
        self.after = [self._add("sync", fn, dmas, "load")]

    def store(self, fn, dmas=1):
        return self._add("sync", fn, dmas, "store")


def bass_gnn_resnorm(nc, x, src, dst, edge_weight, edge_weight1, W0, b0, W1, b1, W_sl, b_sl, W_sr, Wg_l, bg_l,
                     Wg_r, bg_r, att, b_gat, gamma, beta, L2W, L2root, L2bias, L3W, att_src, att_dst,
                     L3bias, dense_w, dense_b, out):
    stack = ExitStack()
    sems = {"waits_" + e: [nc.alloc_semaphore("waits_" + e), 0] for e in ("gpsimd", "sync")}

    def dram(name, shape, dt=F32):
        return nc.dram_tensor(name, shape, dt, kind="Internal").ap()

    named = {}

    def sb(ctx, name, shape, dt=F32):
        named[name] = named.get(name, 0) + 1
        return ctx.enter_context(nc.sbuf_tensor(f"{name}_{named[name]}", shape, dt))

    dst_p = dram("dst_padded", (EP + 2,), I32)
    src_p = dram("src_padded", (EP,), I32)
    w_p = dram("w_padded", (EP,))
    place = dram("place_of_node", (CB, 2), I32)
    x0 = dram("x0", (CB, D))
    xc = dram("xc", (EP, D))
    hop = [xc] + [dram(f"hop{k}", (EP, D)) for k in range(1, HOPS + 1)]
    ytab = [dram(f"y{k}", (EP, D)) for k in range(HOPS + 1)]
    utab = [dram(f"u{k}", (EP, D)) for k in range(HOPS)] + [ytab[HOPS]]
    x1, hh, x2, x3 = (dram(n, (CB + EP, D)) for n in ("x1", "h_sage", "x2", "x3"))
    x4 = dram("x4", (CB + EP, D))
    agg = dram("agg", (EP, D))
    hs_t = dram("source_features", (EP, D))
    agg4 = dram("agg_heads", (EP, HEADS * D))

    PS = [stack.enter_context(nc.psum_tensor(f"bank{b}", [P, 512], F32)) for b in range(8)]
    ident = sb(stack, "ident", [P, P])
    ones = sb(stack, "ones_row", [1, P])
    eps_col = sb(stack, "eps_col", [P, 1])
    last_row = sb(stack, "last_row", [P, 1])
    dstc = sb(stack, "dst_of_edge", [P, TILES + 1])
    comb = sb(stack, "row_of_source", [P, TILES], I32)
    posx = sb(stack, "compact_row_of_source", [P, TILES], I32)
    lastx = sb(stack, "row_of_last_edge", [P, TILES], I32)
    scat = sb(stack, "node_to_write", [P, TILES], I32)
    dsti = sb(stack, "dst_index", [P, TILES], I32)
    srci = sb(stack, "src_index", [P, TILES], I32)
    norm = sb(stack, "norm_of_edge", [P, TILES])
    rcnt = sb(stack, "one_over_count", [P, TILES])
    LG = sb(stack, "logits", [P, TILES, 2 * HEADS])
    AE = sb(stack, "exp_edge_self", [P, TILES, 2 * HEADS])
    idx_s, dst_s, w_s, rows, M, C, G, S, Z = ([] for _ in range(9))
    for l in range(LANES):
        idx_s.append(sb(stack, f"idx_slot{l}", [P, 2, TB], I32))
        dst_s.append(sb(stack, f"dst_slot{l}", [P, TB + 1]))
        w_s.append(sb(stack, f"weight_slot{l}", [P, TB]))
        rows.append(sb(stack, f"dst_rows{l}", [P, TB, P], I32))
        M.append(sb(stack, f"same_dst{l}", [P, TB, P]))
        C.append(sb(stack, f"goes_on{l}", [P, TB, P]))
        G.append(sb(stack, f"gathered{l}", [P, TB, 2, D]))
        S.append(sb(stack, f"sums{l}", [P, TB, HEADS * D + HEADS]))
        Z.append(sb(stack, f"work{l}", [P, TB * D]))

    sems["scratch"] = (sb(stack, "credit_scratch", [16, 8 * 64]), x[0:16, 0:8])
    sems["scratch_used"] = 0

    def phase(lanes=1, rounds=1, ahead=0):
        return Steps(nc, sems, lanes, rounds, ahead)

    wts = {}
    with nc.allow_non_contiguous_dma(reason="small weights"):
        with ExitStack() as ctx:
            raw = {}

            def w_sb(name, shape):
                wts[name] = sb(stack, name, shape)
                return wts[name]

            st = phase()
            ln = Line(st, 0)
            for n in ("bd_sl", "bd_sr", "bd_gmean", "bd_l2w", "bd_l2root", "bd_l3", "center", "mean"):
                w_sb(n, [P, P])
            w_sb("w00", [P, 2, P])
            w_sb("w10", [P, 2, P])
            w_sb("w0cat", [P, 3, P])
            w_sb("w1cat", [P, HOPS + 1, D])
            w_sb("gl_stack", [P, 2, 2, P])
            w_sb("g3_stack", [P, 2, 2, P])
            w_sb("glr", [P, 2, HEADS * D])
            w_sb("g3cols", [P, 2 * HEADS])
            w_sb("att_b", [P, 2 * HEADS * D])
            w_sb("glr_bias", [1, 2 * HEADS * D])
            for n in ("b0", "b1", "bsl", "bg", "gamma", "beta", "bl2", "bl3"):
                w_sb("v_" + n, [P, 1])
            t_w3 = sb(ctx, "t_w3", [D, HEADS * D])
            t_w3T = sb(ctx, "t_w3T", [D, HEADS, D])
            t_dw = sb(ctx, "t_dw", [D, HEADS, D])
            t_as = sb(ctx, "t_as", [D, HEADS])
            t_ad = sb(ctx, "t_ad", [D, HEADS])
            t_gl = sb(ctx, "t_gl", [P, HEADS * D])
            t_b3 = sb(ctx, "t_b3", [D, HEADS])
            t_bg = sb(ctx, "t_bg", [P, HEADS])
            t_bb = sb(ctx, "t_bb", [P, 3])
            t_br = sb(ctx, "t_br", [1, 2, HEADS * D])
            big = sb(ctx, "big", [P, CB // P, 2], I32)
            padv = sb(ctx, "padv", [1, 512], I32)
            zero = sb(ctx, "zero", [P, 256])

            def clear(eng, r):
                for t in (*wts.values(), t_gl, t_b3):
                    eng.memset(t[:], 0.0)
                for l in range(LANES):
                    for t in (G[l], S[l], w_s[l], Z[l], M[l], C[l]):
                        eng.memset(t[:], 0.0)
                    eng.memset(idx_s[l][:], 0)
                eng.memset(AE[:], 0.0)
                eng.memset(LG[:], 0.0)
                eng.memset(padv[:, 0:510], NO_NODE)
                eng.memset(padv[0:1, 510:511], -1)
                eng.memset(big[:, :, 0], ABSENT)
                eng.memset(big[:, :, 1], 0)
                eng.memset(zero[:], 0.0)
                eng.memset(ones[:], 1.0)
                eng.memset(eps_col[:], EPS)
                return eng.memset(dstc[:, 0:1], -1.0)

            def clear2(eng, r):
                eng.memset(wts["center"][0:D, 0:D], -1.0 / D)
                eng.memset(wts["center"][D:P, D:P], -1.0 / D)
                eng.memset(wts["mean"][0:D, 0:D], 1.0 / D)
                return eng.memset(wts["mean"][D:P, D:P], 1.0 / D)

            ln.on("vector", clear)
            ln.on("vector", clear2)

            def loads(eng, r):
                d = []

                def put(o, i_):
                    d.append(eng.dma_start(o, i_))
                for q, (lo, hi) in enumerate(((0, D), (D, P))):
                    put(wts["bd_sl"][lo:hi, lo:hi], W_sl)
                    put(wts["bd_sr"][lo:hi, lo:hi], W_sr)
                    put(wts["bd_l2w"][lo:hi, lo:hi], L2W)
                    put(wts["bd_l2root"][lo:hi, lo:hi], L2root)
                    put(wts["w00"][lo:hi, q, :], W0[0, :, :])
                    put(wts["w10"][:, q, lo:hi], W1[0, :, :])
                    for n, v in (("b1", b1), ("bsl", b_sl), ("gamma", gamma), ("beta", beta), ("bl2", L2bias)):
                        put(wts["v_" + n][lo:hi, :], v.rearrange("(p a) -> p a", a=1))
                    put(t_bg[lo:hi, :], bg_l.rearrange("(h p) -> p h", h=HEADS))
                    put(t_bb[lo:hi, 0:1], b_gat.rearrange("(p a) -> p a", a=1))
                    put(t_bb[lo:hi, 1:2], dense_b.rearrange("(p a) -> p a", a=1))
                    put(t_gl[lo:hi, :], Wg_l)
                put(wts["v_b0"][:, :], b0.rearrange("(p a) -> p a", a=1))
                put(wts["w0cat"][:, :, :], W0.rearrange("k f m -> (k f) m").rearrange("(c p) m -> p c m", p=P))
                put(wts["w1cat"][:, :, :], W1.rearrange("k f m -> f k m"))
                for c in range(2):
                    for q in range(2):
                        for j in range(2):
                            h = 2 * c + j
                            put(wts["gl_stack"][j * D:(j + 1) * D, c, q, q * D:(q + 1) * D],
                                Wg_l[:, h * D:(h + 1) * D])
                put(wts["glr"][0:D, 0, :], Wg_l)
                put(wts["glr"][D:P, 0, :], Wg_r)
                put(wts["glr"][D:P, 1, :], Wg_r)
                for s in range(2):
                    put(wts["att_b"][:, s * HEADS * D:(s + 1) * HEADS * D],
                        att.rearrange("h d -> (h d)").partition_broadcast(P))
                put(t_br[0:1, 0, :], bg_l.rearrange("(a n) -> a n", a=1))
                put(t_br[0:1, 1, :], bg_r.rearrange("(a n) -> a n", a=1))
                put(t_w3[:, :], L3W)
                put(t_dw[:, :, :], dense_w.rearrange("(h p) n -> p h n", h=HEADS))
                put(t_as[:, :], att_src.rearrange("h d -> d h"))
                put(t_ad[:, :], att_dst.rearrange("h d -> d h"))
                put(t_b3[:, :], L3bias.rearrange("(h p) -> p h", h=HEADS))
                row = lambda a: a.rearrange("(a n) -> a n", a=1)
                put(row(dst_p[1:E + 1]), row(dst))
                put(row(src_p[0:E]), row(src))
                put(row(w_p[0:E]), row(edge_weight))
                put(row(dst_p[0:1]), padv[0:1, 510:511])
                put(row(dst_p[EP + 1:EP + 2]), padv[0:1, 510:511])
                at = E
                while at < EP:
                    n = min(EP - at, 500)
                    put(row(dst_p[at + 1:at + 1 + n]), padv[0:1, 0:n])
                    at += n
                pad = EP - E
                assert pad % P == 0 or True
                q = 48
                put(src_p[E:EP].rearrange("(p n) -> p n", p=q), zero[0:q, 0:pad // q].bitcast(I32))
                put(w_p[E:EP].rearrange("(p n) -> p n", p=q), zero[0:q, 0:pad // q])
                put(place.rearrange("(p n) w -> p n w", p=P), big[:, :, :])
                put(x0[0:N, :].rearrange("(a n) d -> a (n d)", a=32), x.rearrange("(a n) d -> a (n d)", a=32))
                put(x0[N:CB, :].rearrange("(p n) d -> p (n d)", p=CB - N >> 1), zero[0:0 + P, 0:1][0:1, 0:1]) if False else None
                for k in range((CB - N) // 88):
                    put(x0[N + 88 * k:N + 88 * (k + 1), :], zero[0:88, 0:D])
                return d

            count = [0]

            class Fake:
                def dma_start(self, o, i_):
                    count[0] += 1
                    return 0
            loads(Fake(), 0)
            ln.load(loads, count[0])

            def iotas(eng, r):
                return eng.affine_select(out=ident[:], in_=ident[:], compare_op=ALU.not_equal, fill=1.0, base=0,
                                         pattern=[[-1, P]], channel_multiplier=1)
            ln.on("vector", lambda e, r: e.memset(ident[:], 0.0))
            ln.on("gpsimd", iotas)
            ln.on("vector", lambda e, r: e.tensor_copy(last_row[:], ident[:, P - 1:P]))

            def tr3(e, r):
                for h in range(HEADS):
                    m = e.transpose(PS[0][0:D, h * D:(h + 1) * D], t_w3[:, h * D:(h + 1) * D], ident[0:D, 0:D])
                return m
            ln.on("tensor", tr3)
            ln.on("vector", lambda e, r: e.tensor_copy(t_w3T[:].rearrange("p h d -> p (h d)"), PS[0][0:D, 0:HEADS * D]))

            def prods(e, r):
                for h in range(HEADS):
                    w = t_w3T[:, h, :]
                    e.matmul(PS[1][0:D, h:h + 1], w, t_as[:, h:h + 1], start=True, stop=True)
                    e.matmul(PS[1][0:D, HEADS + h:HEADS + h + 1], w, t_ad[:, h:h + 1], start=True, stop=True)
                    e.matmul(PS[2][0:D, h * D:(h + 1) * D], w, t_dw[:, h, :], start=True, stop=True)
                for h in range(HEADS):
                    m = e.matmul(PS[3][0:D, 0:1], t_dw[:, h, :], t_b3[:, h:h + 1], start=h == 0, stop=h == HEADS - 1)
                return m
            ln.on("tensor", prods)

            scr = sb(ctx, "scr", [D, 2 * HEADS + 1 + HEADS * D])

            def cp1(e, r):
                e.tensor_copy(scr[:, 0:2 * HEADS], PS[1][0:D, 0:2 * HEADS])
                e.tensor_copy(scr[:, 2 * HEADS + 1:], PS[2][0:D, 0:HEADS * D])
                return e.tensor_copy(scr[:, 2 * HEADS:2 * HEADS + 1], PS[3][0:D, 0:1])
            ln.on("vector", cp1)
            s_as, s_ad, s_c = scr[:, 0:HEADS], scr[:, HEADS:2 * HEADS], scr[:, 2 * HEADS:2 * HEADS + 1]
            s_wd = scr[:, 2 * HEADS + 1:].rearrange("p (h d) -> p h d", h=HEADS)
            s_sum = sb(ctx, "s_sum", [D, HEADS])
            s_m3 = sb(ctx, "s_m3", [D, D])
            ln.on("vector", lambda e, r: e.tensor_tensor(s_sum[:], s_as, s_ad, ALU.add))
            ln.on("vector", lambda e, r: e.tensor_reduce(s_m3[:], s_wd.rearrange("p h d -> p d h"), AX.X, ALU.add))
            ln.on("vector", lambda e, r: e.tensor_tensor(s_c, s_c, t_bb[0:D, 1:2], ALU.add))

            def spread(e, r):
                d = [e.dma_start(wts["g3cols"][0:D, 0:HEADS], s_as),
                     e.dma_start(wts["g3cols"][D:P, 0:HEADS], s_ad),
                     e.dma_start(wts["g3cols"][D:P, HEADS:2 * HEADS], s_sum[:])]
                for q in range(2):
                    d.append(e.dma_start(wts["bd_l3"][q * D:(q + 1) * D, q * D:(q + 1) * D], s_m3[:]))
                    d.append(e.dma_start(wts["v_bl3"][q * D:(q + 1) * D, :], s_c))
                    for c in range(2):
                        for j in range(2):
                            d.append(e.dma_start(wts["g3_stack"][j * D:(j + 1) * D, c, q, q * D:(q + 1) * D],
                                                 s_wd[:, 2 * c + j, :]))
                return d
            ln.load(spread, 3 + 2 * (2 + 4))
            t_m = sb(ctx, "t_m", [P, D])
            t_v = sb(ctx, "t_v", [P, 1])
            ln.on("vector", lambda e, r: e.tensor_reduce(t_m[:], t_gl[:].rearrange("p (h d) -> p d h", h=HEADS), AX.X, ALU.add))
            ln.on("vector", lambda e, r: e.tensor_reduce(t_v[:], t_bg[:], AX.X, ALU.add))

            def fin(e, r):
                q = 1.0 / HEADS
                for a in range(2):
                    sl = slice(a * D, (a + 1) * D)
                    e.tensor_scalar(wts["bd_gmean"][sl, sl], t_m[sl, :], q, None, ALU.mult)
                e.tensor_scalar(wts["v_bg"][:], t_v[:], q, t_bb[:, 0:1], ALU.mult, ALU.add)
                g = wts["gl_stack"][:].rearrange("p c q m -> p (c q m)")
                e.tensor_scalar(g, g, q, None, ALU.mult)
                e.tensor_tensor(wts["glr"][D:P, 1, :], wts["glr"][D:P, 1, :], t_gl[D:P, :], ALU.add)
                e.tensor_tensor(wts["center"][:], wts["center"][:], ident[:], ALU.add)
                s = HEADS * D
                e.tensor_tensor(wts["glr_bias"][0:1, 0:s], t_br[0:1, 0, :], t_br[0:1, 1, :], ALU.add)
                return e.tensor_tensor(wts["glr_bias"][0:1, s:2 * s], t_br[0:1, 0, :], t_br[0:1, 1, :], ALU.add)
            ln.on("vector", fin)
            st.run()

    def seg_scan(ln, ctx, tag, vals, outs, go, kind, reverse=False):
        V = len(vals)
        ends = sb(ctx, f"ends{tag}", [AB, 2, P])
        ends_r = sb(ctx, f"endsr{tag}", [P, 2, AB])
        carry = sb(ctx, f"carry{tag}", [P, AB + 1])
        ini = sb(ctx, f"ini{tag}", [AB, P])
        o0, o1, none = (ALU.mult, ALU.add, 0.0) if kind == "sum" else (ALU.add, ALU.max, LOW)
        rev = (lambda a: a[:, ::-1]) if reverse else (lambda a: a)
        end = 0 if reverse else SC - 1

        def scan(init):
            def f(e, r):
                for v in range(V):
                    m = e.tensor_tensor_scan(rev(outs[v]), rev(go), rev(vals[v]), init(v), o0, o1)
                return m
            return f
        ln.on("vector", lambda e, r: e.memset(ends[:], 0.0))
        ln.on("vector", scan(lambda v: none))

        def collect(e, r):
            for v in range(V):
                e.tensor_copy(ends[:, 0, v:v + 1], outs[v][:, end:end + 1])
            return e.tensor_reduce(ends[:, 1, 0:1], go, AX.X, ALU.min)
        ln.on("vector", collect)
        ln.on("vector", lambda e, r: e.tensor_copy(ends[:, 1, 1:V + 1], ends[:, 1, 0:1].to_broadcast([AB, V])))

        def tr(e, r):
            e.transpose(PS[6][:, 0:AB], ends[:, 0, :], ident[0:AB, 0:AB])
            return e.transpose(PS[6][:, P:P + AB], ends[:, 1, :], ident[0:AB, 0:AB])
        ln.on("tensor", tr)

        def back(e, r):
            e.tensor_copy(ends_r[:, 0, :], PS[6][:, 0:AB])
            e.memset(carry[:], none)
            return e.tensor_copy(ends_r[:, 1, :], PS[6][:, P:P + AB])
        ln.on("vector", back)
        o = carry[:, 0:AB] if reverse else carry[:, 1:AB + 1]
        ln.on("vector", lambda e, r: e.tensor_tensor_scan(rev(o), rev(ends_r[:, 1, :]), rev(ends_r[:, 0, :]), none, o0, o1))
        into = carry[:, 1:AB + 1] if reverse else carry[:, 0:AB]
        ln.on("tensor", lambda e, r: e.transpose(PS[7][0:AB, 0:P], into, ident[:, :]))
        ln.on("vector", lambda e, r: e.tensor_copy(ini[:], PS[7][0:AB, 0:P]))
        ln.on("vector", scan(lambda v: ini[:, v:v + 1]))

    def from_scan(ln, k, src_ap, dst_ap):
        def tr(e, r):
            for g in range(TB):
                m = e.transpose(PS[k][:, g * AB:(g + 1) * AB], src_ap[:, g * P:(g + 1) * P], ident[0:AB, 0:AB])
            return m
        ln.on("tensor", tr)
        ln.on("vector", lambda e, r: e.tensor_copy(dst_ap.rearrange("p (a g) -> p g a", g=TB),
                                                   PS[k][:, 0:TB * AB].rearrange("p (g a) -> p g a", g=TB)))

    def to_scan(ln, k, src_ap, dst_ap):
        v = src_ap.rearrange("p (a g) -> p g a", g=TB)

        def tr(e, r):
            for g in range(TB):
                m = e.transpose(PS[k][0:AB, g * P:(g + 1) * P], v[:, g, :], ident[:, :])
            return m
        ln.on("tensor", tr)
        ln.on("vector", lambda e, r: e.tensor_copy(dst_ap, PS[k][0:AB, :]))

    cont = sb(stack, "same_as_before", [AB, SC])
    nsame = sb(stack, "same_as_next", [AB, SC])
    last = sb(stack, "is_last", [AB, SC])
    wd = sb(stack, "w_times_dis", [P, TILES])
    own = sb(stack, "own_place", [P, TILES, 2], I32)
    found = sb(stack, "source_place", [P, TILES, 2], I32)

    with ExitStack() as ctx:
        st = phase()
        ln = Line(st, 0)
        t = {n: sb(ctx, "p1_" + n, [AB, SC], I32) for n in ("d", "dp", "dn", "s")}
        f = {n: sb(ctx, "p1f_" + n, [AB, SC]) for n in
             ("w", "one", "deg", "cnt", "d", "s", "m", "r", "rk", "fr", "fd", "ld", "lr", "sc")}

        def loads(e, r):
            v = lambda a: a.rearrange("(a n) -> a n", a=AB)
            return [e.dma_start(t["d"][:], v(dst_p[1:EP + 1])), e.dma_start(t["dp"][:], v(dst_p[0:EP])),
                    e.dma_start(t["dn"][:], v(dst_p[2:EP + 2])), e.dma_start(t["s"][:], v(src_p[:])),
                    e.dma_start(f["w"][:], v(w_p[:]))]
        ln.load(loads, 5)

        def flags(e, r):
            e.tensor_tensor(cont[:], t["d"][:], t["dp"][:], ALU.is_equal)
            e.tensor_tensor(nsame[:], t["d"][:], t["dn"][:], ALU.is_equal)
            e.tensor_copy(f["d"][:], t["d"][:])
            e.tensor_copy(f["s"][:], t["s"][:])
            return e.memset(f["one"][:], 1.0)
        ln.on("vector", flags)
        ln.on("vector", lambda e, r: e.tensor_scalar(last[:], nsame[:], -1.0, 1.0, ALU.mult, ALU.add))
        ri = sb(ctx, "ri", [AB, SC], I32)
        ln.on("gpsimd", lambda e, r: e.iota(ri[:].rearrange("a (g p) -> a g p", g=TB), pattern=[[1, TB], [TB, P]],
                                            base=0, channel_multiplier=SC))
        ln.on("gpsimd", lambda e, r: e.iota(own[:, :, 0].rearrange("p (a g) -> p a g", g=TB),
                                            pattern=[[SC, AB], [1, TB]], base=0, channel_multiplier=TB))
        seg_scan(ln, ctx, "a", [f["w"][:], f["one"][:]], [f["deg"][:], f["cnt"][:]], cont[:], "sum")
        ln.on("vector", lambda e, r: e.tensor_scalar(f["m"][:], f["deg"][:], 0.0, None, ALU.is_gt))
        ln.on("vector", lambda e, r: e.tensor_scalar(f["r"][:], f["m"][:], -1.0, 1.0, ALU.mult, ALU.add))
        ln.on("vector", lambda e, r: e.tensor_tensor(f["r"][:], f["r"][:], f["deg"][:], ALU.add))
        ln.on("scalar", lambda e, r: e.activation(f["r"][:], f["r"][:], ACT.Sqrt))
        ln.on("vector", lambda e, r: e.reciprocal(f["r"][:], f["r"][:]))
        ln.on("vector", lambda e, r: e.tensor_tensor(f["r"][:], f["r"][:], f["m"][:], ALU.mult))

        def prep(e, r):
            e.tensor_copy(f["rk"][:], ri[:])
            e.tensor_tensor(f["ld"][:], f["r"][:], last[:], ALU.mult)
            e.tensor_scalar(f["cnt"][:], f["cnt"][:], 1.0, None, ALU.max)
            return e.tensor_scalar(f["sc"][:], f["d"][:], float(-ABSENT), None, ALU.add)
        ln.on("vector", prep)

        def prep2(e, r):
            e.reciprocal(f["cnt"][:], f["cnt"][:])
            e.tensor_tensor(f["sc"][:], f["sc"][:], last[:], ALU.mult)
            return e.tensor_tensor(f["lr"][:], f["rk"][:], last[:], ALU.mult)
        ln.on("vector", prep2)
        seg_scan(ln, ctx, "b", [f["ld"][:], f["lr"][:]], [f["fd"][:], f["fr"][:]], nsame[:], "sum", reverse=True)

        def prep3(e, r):
            e.tensor_scalar(f["sc"][:], f["sc"][:], float(ABSENT), None, ALU.add)
            e.tensor_scalar(f["fr"][:], f["fr"][:], float(CB), None, ALU.add)
            return e.tensor_tensor(f["m"][:], f["w"][:], f["fd"][:], ALU.mult)
        ln.on("vector", prep3)
        disw = own[:, :, 1].bitcast(F32)
        for k, (a, b) in enumerate(((f["d"], dstc[:, 1:]), (f["d"], dsti[:]), (f["s"], srci[:]), (f["m"], wd[:]),
                                    (f["cnt"], rcnt[:]), (f["sc"], scat[:]), (f["fr"], lastx[:]), (f["r"], disw))):
            from_scan(ln, k % 6, a[:], b)
        st.run()

    def fetch(l, cols, weight=None):
        def f(e, r):
            t0 = r * (LANES * TB) + l * TB
            for n, c in enumerate(cols):
                m = e.tensor_copy(idx_s[l][:, n, :], c[:, ds(t0, TB)])
            e.tensor_copy(dst_s[l][:, :], dstc[:, ds(t0, TB + 1)])
            if weight is not None:
                e.tensor_copy(w_s[l][:, :], weight[:, ds(t0, TB)])
            return m
        return f

    def fetch_all(l, cols, weight=None):
        def f(e, r):
            t0 = r * (LANES * TB) + l * TB
            m = e.tensor_copy(dst_s[l][:, :], dstc[:, ds(t0, TB + 1)])
            for n, c in enumerate(cols):
                m = e.tensor_copy(idx_s[l][:, n, :], c[:, ds(t0, TB)])
            if weight is not None:
                m = e.tensor_copy(w_s[l][:, :], weight[:, ds(t0, TB)])
            return m
        return f

    def load_rows(l):
        return lambda e, r: [e.dma_start(rows[l][:].rearrange("p t n -> p (t n)"),
                                         dst_p[ds((r * LANES + l) * (TB * P) + 1, TB * P)].partition_broadcast(P))]

    def gather(l, pairs):
        def f(e, r):
            d = []
            for k in range(TB):
                for tab, where, n, top in pairs:
                    d.append(e.indirect_dma_start(
                        out=where(l, k), out_offset=None, in_=tab,
                        in_offset=bass.IndirectOffsetOnAxis(ap=idx_s[l][:, n, k:k + 1], axis=0),
                        bounds_check=top, oob_is_err=False))
            return d
        return f

    def masks(l, weighted):
        def f(e, r):
            for k in range(TB):
                if weighted:
                    e.tensor_scalar(M[l][:, k, :], rows[l][:, k, :], dst_s[l][:, k + 1:k + 2], w_s[l][:, k:k + 1],
                                    ALU.is_equal, ALU.mult)
                else:
                    e.tensor_scalar(M[l][:, k, :], rows[l][:, k, :], dst_s[l][:, k + 1:k + 2], None, ALU.is_equal)
                m = e.tensor_scalar(C[l][96:P, k, :], rows[l][96:P, k, :], dst_s[l][96:P, k:k + 1],
                                    last_row[96:P, :], ALU.is_equal, ALU.mult)
            return m
        return f

    def block_rows(tab, l, r, w=D, base=0):
        return tab[ds((r * LANES + l) * (TB * P) + base, TB * P), :].rearrange("(p k) d -> p k d", k=TB)

    def sums(st, l, rhs, width, first):
        for k in range(TB):
            def main(e, r, k=k):
                return e.matmul(PS[k][:, 0:width], M[l][:, k, :], rhs(k), start=True, stop=False)

            def carry(e, r, k=k):
                pl = l if k else (l - 1) % LANES
                pk = (k - 1) % TB
                return e.matmul(PS[k][:, 0:width], C[l][96:P, k, :], S[pl][96:P, pk, 0:width], start=False, stop=True)
            prev_lane, back = (l - 1) % LANES, (1 if l == 0 else 0)
            st.step(l, f"main{k}", "tensor", main, (first if k == 0 else []) + [(prev_lane, f"out{k}", back)])
            before = f"out{k - 1}" if k else (prev_lane, f"out{TB - 1}", back)
            st.step(l, f"carry{k}", "tensor", carry, [before])
            st.step(l, f"out{k}", "scalar",
                    lambda e, r, k=k: e.copy(S[l][:, k, 0:width], PS[k][:, 0:width]),
                    [f"carry{k}"] + ([(l, "store", 1)] if k == 0 else []))

    def edge_sum(tab, top, index, weight, scale, target, add=None):
        st = phase(LANES, ROUNDS, ahead=2)
        for l in range(LANES):
            st.step(l, "fetch", "vector", fetch_all(l, [index] , weight) if scale is None else
                    fetch_all(l, [index], scale), [(l, "store", 1)], early=True)
            st.step(l, "rows", "sync", load_rows(l), [(l, "store", 1)], dmas=1, early=True)
            if add is not None:
                st.step(l, "extra", "sync", lambda e, r, l=l: [e.dma_start(
                    Z[l][:].rearrange("p (k d) -> p k d", k=TB), block_rows(add, l, r))],
                    [(l, "store", 1)], dmas=1, early=True)
            st.step(l, "gather", "gpsimd", gather(l, [(tab, lambda l, k: G[l][:, k, 0, :], 0, top)]), ["fetch"],
                    dmas=TB, early=True)
            st.step(l, "mask", "vector", masks(l, weight is not None), ["fetch", "rows"], early=True)
            sums(st, l, lambda k, l=l: G[l][:, k, 0, :], D, ["mask", "gather"])
            if add is not None:
                st.step(l, "post", "vector", lambda e, r, l=l: e.tensor_tensor(
                    Z[l][:].rearrange("p (k d) -> p k d", k=TB), Z[l][:].rearrange("p (k d) -> p k d", k=TB),
                    S[l][:, :, 0:D], ALU.add), [f"out{TB - 1}", "extra"])
            elif scale is not None:
                st.step(l, "post", "vector", lambda e, r, l=l: e.tensor_tensor(
                    Z[l][:].rearrange("p (k d) -> p k d", k=TB), S[l][:, :, 0:D],
                    w_s[l][:].rearrange("p (k a) -> p k a", a=1).to_broadcast([P, TB, D]), ALU.mult),
                    [f"out{TB - 1}"])
            direct = add is None and scale is None
            st.step(l, "store", "sync", lambda e, r, l=l: [e.dma_start(
                block_rows(target, l, r), S[l][:, :, 0:D] if direct else
                Z[l][:].rearrange("p (k d) -> p k d", k=TB))],
                [f"out{TB - 1}"] if direct else ["post"], dmas=1)
        st.run()

    def place_nodes():
        st = phase(LANES, ROUNDS, ahead=2)
        for l in range(LANES):
            def fe(e, r, l=l):
                t0 = r * (LANES * TB) + l * TB
                e.tensor_copy(G[l][:, :, 0, 0:2].bitcast(I32), own[:, ds(t0, TB), :])
                return e.tensor_copy(idx_s[l][:, 0, :], scat[:, ds(t0, TB)])
            st.step(l, "fetch", "vector", fe, [(l, "store_p", 1)], early=True)

            def sc(e, r, l=l):
                return [e.indirect_dma_start(
                    out=place, out_offset=bass.IndirectOffsetOnAxis(ap=idx_s[l][:, 0, k:k + 1], axis=0),
                    in_=G[l][:, k, 0, 0:2].bitcast(I32), in_offset=None, bounds_check=N - 1, oob_is_err=False)
                    for k in range(TB)]
            st.step(l, "store_p", "gpsimd", sc, ["fetch"], dmas=TB)
        st.run()

    def find_sources():
        st = phase(LANES, ROUNDS, ahead=2)
        for l in range(LANES):
            st.step(l, "fetch", "vector", fetch_all(l, [srci, dsti]), [(l, "store", 1), (l, "keep", 1)], early=True)
            st.step(l, "gather2", "gpsimd", gather(l, [
                (place, lambda l, k: G[l][:, k, 1, 0:2].bitcast(I32), 0, N - 1),
                (x, lambda l, k: G[l][:, k, 0, :], 1, N - 1)]), ["fetch"], dmas=2 * TB, early=True)

            def keep(e, r, l=l):
                return e.tensor_copy(found[:, ds(r * (LANES * TB) + l * TB, TB), :], G[l][:, :, 1, 0:2].bitcast(I32))
            st.step(l, "keep", "vector", keep, ["gather2"])
            st.step(l, "store", "sync", lambda e, r, l=l: [e.dma_start(block_rows(xc, l, r), G[l][:, :, 0, :])],
                    ["gather2"], dmas=1)
        st.run()

    def finish_indices():
        with ExitStack() as ctx:
            st = phase()
            ln = Line(st, 0)
            pf, sf, v = (sb(ctx, n, [P, TILES]) for n in ("pf", "sf", "v"))

            def a(e, r):
                e.tensor_copy(pf[:], found[:, :, 0])
                e.tensor_copy(sf[:], srci[:])
                e.tensor_copy(posx[:], found[:, :, 0])
                return e.tensor_tensor(norm[:], wd[:], found[:, :, 1].bitcast(F32), ALU.mult)
            ln.on("vector", a)
            ln.on("vector", lambda e, r: e.tensor_scalar(v[:], pf[:], float(ABSENT), None, ALU.is_lt))
            ln.on("vector", lambda e, r: e.scalar_tensor_tensor(pf[:], pf[:], float(CB), sf[:], ALU.add, ALU.subtract))
            ln.on("vector", lambda e, r: e.tensor_tensor(pf[:], pf[:], v[:], ALU.mult))
            ln.on("vector", lambda e, r: e.tensor_tensor(comb[:], pf[:], sf[:], ALU.add))
            st.run()

    def logits(tab, v2):
        st = phase(LANES, ROUNDS, ahead=2)
        WZ = 2 * HEADS * D
        for l in range(LANES):
            st.step(l, "fetch", "vector", fetch_all(l, [comb, lastx]), [(l, "store", 1), (l, "tr3", 1)], early=True)
            st.step(l, "gather2", "gpsimd", gather(l, [
                (tab, lambda l, k: G[l][:, k, 0, :], 0, CB + EP - 1),
                (tab, lambda l, k: G[l][:, k, 1, :], 1, CB + EP - 1)]), ["fetch"], dmas=2 * TB, early=True)
            st.step(l, "store", "sync", lambda e, r, l=l: [e.dma_start(block_rows(hs_t, l, r), G[l][:, :, 0, :])],
                    ["gather2"], dmas=1)
            pv, bk = (l - 1) % LANES, (1 if l == 0 else 0)
            for k in range(TB):
                def tr(e, r, k=k, l=l):
                    return e.transpose(PS[k][:, 0:P], G[l][:, k, :, :].rearrange("p a d -> p (a d)"), ident[:])
                st.step(l, f"tr{k}", "tensor", tr, (["gather2"] if k == 0 else []) + [(pv, f"cp{k}", bk)])
                st.step(l, f"cp{k}", "scalar", lambda e, r, k=k, l=l: e.copy(M[l][:, k, :], PS[k][:, 0:P]),
                        [f"tr{k}", (l, f"z{k}", 1)])

                def zmm(e, r, k=k, l=l):
                    if not v2:
                        return e.matmul(PS[4 + k][:, 0:2 * HEADS], M[l][:, k, :], wts["g3cols"][:], start=True, stop=True)
                    e.matmul(PS[4 + k][:, 0:WZ], M[l][:, k, :], wts["glr"][:].rearrange("p a n -> p (a n)"),
                             start=True, stop=False)
                    return e.matmul(PS[4 + k][:, 0:WZ], ones[0:1, :], wts["glr_bias"][0:1, :], start=False, stop=True)
                st.step(l, f"z{k}", "tensor", zmm, [f"cp{k}", (pv, f"zc{k}", bk)])
                zb = zbuf[k % 2]
                if v2:
                    st.step(l, f"zc{k}", "scalar", lambda e, r, k=k, l=l, zb=zb: e.copy(zb[0][:], PS[4 + k][:, 0:WZ]),
                            [f"z{k}", (l, f"rd{k - 2}", 0) if k >= 2 else (pv, f"rd{k + 2}", bk)])
                    st.step(l, f"lr{k}", "vector", lambda e, r, zb=zb: e.scalar_tensor_tensor(
                        zb[1][:], zb[0][:], 0.2, zb[0][:], ALU.mult, ALU.max), [f"zc{k}"])
                    st.step(l, f"at{k}", "vector", lambda e, r, zb=zb: e.tensor_tensor(
                        zb[1][:], zb[1][:], wts["att_b"][:], ALU.mult), [f"lr{k}"])

                    def rd(e, r, k=k, l=l, zb=zb):
                        t = r * (LANES * TB) + (l * TB + k)
                        return e.tensor_reduce(LG[:, ds(t, 1), :].rearrange("p a h -> p (a h)"),
                                               zb[1][:].rearrange("p (h d) -> p h d", d=D), AX.X, ALU.add)
                    st.step(l, f"rd{k}", "vector", rd, [f"at{k}"])
                else:
                    st.step(l, f"zc{k}", "scalar", lambda e, r, k=k, l=l, zb=zb: e.copy(
                        zb[0][:, 0:2 * HEADS], PS[4 + k][:, 0:2 * HEADS]),
                        [f"z{k}", (l, f"rd{k - 2}", 0) if k >= 2 else (pv, f"rd{k + 2}", bk)])

                    def rd(e, r, k=k, l=l, zb=zb):
                        t = r * (LANES * TB) + (l * TB + k)
                        z = zb[0][:, 0:2 * HEADS]
                        return e.scalar_tensor_tensor(LG[:, ds(t, 1), :].rearrange("p a h -> p (a h)"), z, 0.2, z,
                                                      ALU.mult, ALU.max)
                    st.step(l, f"rd{k}", "vector", rd, [f"zc{k}"])
        st.run()

    def softmax_terms():
        with ExitStack() as ctx:
            st = phase()
            ln = Line(st, 0)
            pen = sb(ctx, "pen", [AB, SC])
            a = [sb(ctx, f"smx_a{h}", [AB, SC]) for h in range(HEADS)]
            b = [sb(ctx, f"smx_b{h}", [AB, SC]) for h in range(HEADS)]
            mx = sb(ctx, "smx_m", [P, TILES, HEADS])
            ln.on("vector", lambda e, r: e.tensor_scalar(pen[:], cont[:], -1.0, -LOW, ALU.add, ALU.mult))
            for h in range(HEADS):
                to_scan(ln, h, LG[:, :, h], a[h][:])
            seg_scan(ln, ctx, "m", [x_[:] for x_ in a], [x_[:] for x_ in b], pen[:], "max")

            def only_last(e, r):
                for h in range(HEADS):
                    m = e.tensor_tensor(b[h][:], b[h][:], last[:], ALU.mult)
                return m
            ln.on("vector", only_last)
            seg_scan(ln, ctx, "n", [x_[:] for x_ in b], [x_[:] for x_ in a], nsame[:], "sum", reverse=True)
            for h in range(HEADS):
                from_scan(ln, h, a[h][:], mx[:, :, h])
            ln.on("vector", lambda e, r: e.tensor_tensor(mx[:], mx[:], LG[:, :, HEADS:], ALU.max))

            def sub(e, r):
                e.tensor_tensor(AE[:, :, 0:HEADS], LG[:, :, 0:HEADS], mx[:], ALU.subtract)
                return e.tensor_tensor(AE[:, :, HEADS:], LG[:, :, HEADS:], mx[:], ALU.subtract)
            ln.on("vector", sub)
            ln.on("scalar", lambda e, r: e.activation(AE[:], AE[:], ACT.Exp))
            st.run()

    def attend(tab, tiny):
        with ExitStack() as ctx:
            R = [sb(ctx, f"weighted{k}", [P, TB, HEADS * D + HEADS]) for k in range(2)]
            ae = [sb(ctx, f"ae{l}", [P, TB, 2 * HEADS]) for l in range(LANES)]
            O = [sb(ctx, f"heads{l}", [P, TB, HEADS * D]) for l in range(LANES)]
            st = phase(LANES, ROUNDS, ahead=2)
            W = HEADS * D
            for l in range(LANES):
                def fe(e, r, l=l):
                    t0 = r * (LANES * TB) + l * TB
                    e.tensor_copy(ae[l][:], AE[:, ds(t0, TB), :])
                    return e.tensor_copy(dst_s[l][:, :], dstc[:, ds(t0, TB + 1)])
                st.step(l, "fetch", "vector", fe, [(l, "store", 1)], early=True)
                st.step(l, "rows", "sync", load_rows(l), [(l, "store", 1)], dmas=1, early=True)
                st.step(l, "feats", "sync", lambda e, r, l=l: [
                    e.dma_start(G[l][:, :, 0, :], block_rows(hs_t, l, r)),
                    e.dma_start(G[l][:, :, 1, :], block_rows(tab, l, r, base=CB))], [(l, "store", 1)], dmas=2, early=True)
                st.step(l, "mask", "vector", masks(l, False), ["fetch", "rows"], early=True)
                pl = (l - 2) % LANES
                rb = 1 if l < 2 else 0

                def weigh(e, r, l=l):
                    for k in range(TB):
                        e.tensor_tensor(
                            R[l % 2][:, k, 0:W].rearrange("p (h d) -> p h d", h=HEADS),
                            G[l][:, k, 0:1, :].to_broadcast([P, HEADS, D]),
                            ae[l][:, k, 0:HEADS].rearrange("p (h a) -> p h a", a=1).to_broadcast([P, HEADS, D]), ALU.mult)
                    return e.tensor_copy(R[l % 2][:, :, W:], ae[l][:, :, 0:HEADS])
                st.step(l, "weigh", "vector", weigh, ["fetch", "feats", (pl, f"main{TB - 1}", rb)])
                sums(st, l, lambda k, l=l: R[l % 2][:, k, :], W + HEADS, ["mask", "weigh"])
                den = w4[l]
                st.step(l, "den", "vector", lambda e, r, l=l, den=den: e.tensor_tensor(
                    den[:], S[l][:, :, W:], ae[l][:, :, HEADS:], ALU.add), [f"out{TB - 1}"])
                st.step(l, "den2", "vector", lambda e, r, den=den: e.tensor_scalar(
                    den[:], den[:], tiny, None, ALU.add), ["den"])
                st.step(l, "inv", "vector", lambda e, r, den=den: e.reciprocal(den[:], den[:]), ["den2"])

                def own_term(e, r, l=l):
                    for k in range(TB):
                        m = e.tensor_tensor(
                            O[l][:, k, :].rearrange("p (h d) -> p h d", h=HEADS),
                            G[l][:, k, 1:2, :].to_broadcast([P, HEADS, D]),
                            ae[l][:, k, HEADS:].rearrange("p (h a) -> p h a", a=1).to_broadcast([P, HEADS, D]), ALU.mult)
                    return m
                st.step(l, "own", "vector", own_term, [f"out{TB - 1}"])
                st.step(l, "whole", "vector", lambda e, r, l=l: e.tensor_tensor(O[l][:], O[l][:], S[l][:, :, 0:W], ALU.add),
                        ["own"])

                def share(e, r, l=l, den=den):
                    for k in range(TB):
                        o = O[l][:, k, :].rearrange("p (h d) -> p h d", h=HEADS)
                        m = e.tensor_tensor(o, o, den[:, k, :].rearrange("p (h a) -> p h a", a=1)
                                            .to_broadcast([P, HEADS, D]), ALU.mult)
                    return m
                st.step(l, "share", "vector", share, ["whole", "inv"])
                st.step(l, "store", "sync", lambda e, r, l=l: [e.dma_start(block_rows(agg4, l, r), O[l][:])],
                        ["share"], dmas=1)
            st.run()

    zbuf = [[sb(stack, f"z{k}{j}", [P, 2 * HEADS * D]) for j in range(2)] for k in range(2)]
    w4 = [sb(stack, f"den{l}", [P, TB, HEADS]) for l in range(LANES)]

    FC = 4 * P

    def rows_phase(base, rounds, build):
        with ExitStack() as ctx:
            st = phase(2, rounds)
            lines = []
            for l in range(2):
                st_l = Steps(nc, sems, 2, rounds)
                ln = Line(st_l, l)
                build(ln, l, ctx)
                stores = [s[1] for s in st_l.list if s[1].startswith("store")]
                lines.append((st_l.list, stores))
            for a in range(len(lines[0][0])):
                for l in range(2):
                    lane, name, engine, fn, after, dmas, early, key = lines[l][0][a]
                    if a == 0:
                        after = [(l, s, 1) for s in lines[l][1]]
                    st.step(lane, name, engine, fn, after, dmas)
            st.run()

    def make(ln, l, ctx):
        bank = PS[4 * l:4 * l + 4]
        made = {}

        def buf(name, cols=FC):
            if name not in made:
                made[name] = sb(ctx, f"{name}_{l}", [P, cols])
            return made[name][:, :]

        def rows_at(tab, r, base):
            return tab[ds((r * 2 + l) * (P * NB) + base, P * NB), :].rearrange("(p k) d -> p (k d)", k=NB)

        def load(pairs):
            ln.load(lambda e, r: [e.dma_start(b, rows_at(t, r, base)) for b, t, base in pairs], len(pairs))

        def turn(into, rowsb, step=P, at=0):
            def f(e, r):
                for q in range(4):
                    m = e.transpose(bank[0][:, q * P:(q + 1) * P], rowsb[:, q * step + at:q * step + at + P], ident[:])
                return m
            ln.on("tensor", f)
            ln.on("scalar", lambda e, r: e.copy(into, bank[0][:, :]))

        def unturn(into, cols, tab, base):
            def f(e, r):
                for q in range(4):
                    m = e.transpose(bank[0][:, q * P:(q + 1) * P], cols[:, q * P:(q + 1) * P], ident[:])
                return m
            ln.on("tensor", f)
            ln.on("scalar", lambda e, r: e.copy(into, bank[0][:, :]))
            ln.store(lambda e, r: [e.dma_start(rows_at(tab, r, base), into)])

        def mm(b, pairs):
            def f(e, r):
                for n, (w, v) in enumerate(pairs):
                    m = e.matmul(bank[b][:, :], w, v, start=n == 0, stop=n == len(pairs) - 1)
                return m
            ln.on("tensor", f)

        def bias(into, b, v):
            ln.on("scalar", lambda e, r: e.activation(into, bank[b][:, :], ACT.Identity, bias=wts[v][:, 0:1]))

        def stt(o, a, s, b, o0, o1):
            ln.on("vector", lambda e, r: e.scalar_tensor_tensor(o, a, s, b, o0, o1))

        def tt(o, a, b, op):
            ln.on("vector", lambda e, r: e.tensor_tensor(o, a, b, op))

        def norm_to(o, y, affine=False):
            t = buf("tmp")
            mm(1, [(wts["center"][:], y)])
            ln.on("scalar", lambda e, r: e.activation(t, bank[1][:, :], ACT.Square))
            mm(2, [(wts["mean"][:], t)])
            ln.on("scalar", lambda e, r: e.activation(t, bank[2][:, :], ACT.Ln, bias=eps_col[:, 0:1]))
            ln.on("scalar", lambda e, r: e.activation(t, t, ACT.Exp, scale=-0.5))
            tt(o, bank[1][:, :], t, ALU.mult)
            if affine:
                ln.on("vector", lambda e, r: e.tensor_scalar(o, o, wts["v_gamma"][:, 0:1], wts["v_beta"][:, 0:1],
                                                             ALU.mult, ALU.add))

        def sage(o, xT, aT=None):
            mm(1, [(wts["bd_sr"][:], xT)] + ([(wts["bd_sl"][:], aT)] if aT is not None else []))
            bias(o, 1, "v_bsl")

        def gat1(o, xT, pairs):
            a, b = buf("a"), buf("b")
            mm(1, pairs)
            bias(a, 1, "v_bg")
            norm_to(a, a, affine=True)
            ln.on("vector", lambda e, r: e.tensor_scalar(b, a, 0.0, None, ALU.min))
            ln.on("scalar", lambda e, r: e.activation(b, b, ACT.Exp))
            stt(a, a, 0.0, b, ALU.max, ALU.add)
            stt(a, a, -1.0, xT, ALU.add, ALU.add)
            norm_to(o, a)

        def layer2(o, xT, aT=None):
            a = buf("a")
            mm(1, [(wts["bd_l2root"][:], xT)] + ([(wts["bd_l2w"][:], aT)] if aT is not None else []))
            ln.on("scalar", lambda e, r: e.activation(a, bank[1][:, :], ACT.Relu, bias=wts["v_bl2"][:, 0:1]))
            tt(a, a, xT, ALU.add)
            norm_to(o, a)

        def layer3(o, xT, pairs):
            a = buf("a")
            mm(1, pairs)
            bias(a, 1, "v_bl3")
            tt(a, a, xT, ALU.add)
            norm_to(o, a)

        def heads(stackw):
            g = buf("g", NB * HEADS * D)
            pairs = []
            W = HEADS * D
            for q in range(2):
                for c in range(2):
                    t = buf(f"gt{q}{c}")
                    turn(t, g, step=2 * W, at=q * W + c * P)
                    pairs.append((wts[stackw][:, c, q, :], t))
            return pairs
        return dict(buf=buf, load=load, turn=turn, unturn=unturn, mm=mm, bias=bias, stt=stt, tt=tt, norm=norm_to,
                    sage=sage, gat1=gat1, layer2=layer2, layer3=layer3, heads=heads, bank=bank, rows_at=rows_at)

    def dense():
        def build(ln, l, ctx):
            o = make(ln, l, ctx)
            buf = o["buf"]
            xT, yT, a, b, t = buf("xT"), buf("yT"), buf("a"), buf("b"), buf("tmp")
            raw = buf("raw")
            o["load"]([(raw, x0, 0)])
            o["turn"](xT, raw)
            for q in range(2):
                o["mm"](1 + q, [(wts["w00"][:, q, :], xT)])
                h = (a, b)[q]
                o["bias"](h, 1 + q, "v_b0")
                o["stt"](h, h, 0.01, h, ALU.mult, ALU.max)
            o["mm"](1, [(wts["w10"][:, 0, :], a), (wts["w10"][:, 1, :], b)])
            o["bias"](a, 1, "v_b1")
            o["stt"](a, a, 0.01, a, ALU.mult, ALU.max)
            o["tt"](a, a, xT, ALU.add)
            o["norm"](yT, a)
            o["unturn"](buf("o1"), yT, x1, 0)
            o["sage"](t, yT)
            o["tt"](b, t, t, ALU.max)
            o["unturn"](buf("oh"), b, hh, 0)
            o["gat1"](xT, yT, [(wts["bd_gmean"][:], b)])
            o["unturn"](buf("o2"), xT, x2, 0)
            o["layer2"](yT, xT)
            o["unturn"](buf("o3"), yT, x3, 0)
            o["layer3"](xT, yT, [(wts["bd_l3"][:], yT)])
            o["unturn"](buf("o4"), xT, x4, 0)
        rows_phase(0, CB // (P * NB * 2), build)

    CR = EP // (P * NB * 2)

    def conv1():
        def build(ln, l, ctx):
            o = make(ln, l, ctx)
            buf, bank = o["buf"], o["bank"]
            K6 = HOPS + 1
            cat = buf("cat", NB * K6 * D)
            catv = cat.rearrange("p (k m d) -> p k m d", k=NB, m=K6)
            y = buf("y", NB * K6 * D)
            yv = y.rearrange("p (k m d) -> p k m d", k=NB, m=K6)
            ln.load(lambda e, r: [e.dma_start(catv[:, :, m, :], tab[ds((r * 2 + l) * (P * NB), P * NB), :]
                                              .rearrange("(p k) d -> p k d", k=NB)) for m, tab in enumerate(hop)], K6)
            for half in range(2):
                ts = []
                for c in range(3):
                    t = buf(f"t{c}")
                    o["turn"](t, cat[:, half * 4 * K6 * D:], step=K6 * D, at=c * P)
                    ts.append((wts["w0cat"][:, c, :], t))
                o["mm"](1, ts)
                h = buf("a")
                o["bias"](h, 1, "v_b0")
                o["stt"](h, h, 0.01, h, ALU.mult, ALU.max)
                for pair in range(2):
                    def ymm(e, r, pair=pair):
                        for j in range(2):
                            c = pair * 2 + j
                            m = e.matmul(bank[2 + j][:, 0:K6 * D], h[:, c * P:(c + 1) * P],
                                         wts["w1cat"][:].rearrange("p k d -> p (k d)"), start=True, stop=True)
                        return m
                    ln.on("tensor", ymm)

                    def ycp(e, r, pair=pair, half=half):
                        for j in range(2):
                            k = half * 4 + pair * 2 + j
                            m = e.copy(y[:, k * K6 * D:(k + 1) * K6 * D], bank[2 + j][:, 0:K6 * D])
                        return m
                    ln.on("scalar", ycp)
            ln.store(lambda e, r: [e.dma_start(tab[ds((r * 2 + l) * (P * NB), P * NB), :]
                                               .rearrange("(p k) d -> p k d", k=NB), yv[:, :, m, :])
                                   for m, tab in enumerate(ytab)], K6)
        rows_phase(0, CR, build)

    def compact(kind):
        def build(ln, l, ctx):
            o = make(ln, l, ctx)
            buf = o["buf"]
            xT, aT, a, b = buf("xT"), buf("aT"), buf("a"), buf("b")
            r1, r2 = buf("raw1"), buf("raw2")
            if kind == "x1":
                o["load"]([(r1, xc, 0), (r2, utab[0], 0)])
                o["turn"](xT, r1)
                o["turn"](aT, r2)
                ln.on("vector", lambda e, r: e.tensor_scalar(aT, aT, wts["v_b1"][:, 0:1], None, ALU.add))
                o["stt"](aT, aT, 0.01, aT, ALU.mult, ALU.max)
                o["tt"](aT, aT, xT, ALU.add)
                o["norm"](b, aT)
                o["unturn"](buf("o"), b, x1, CB)
            elif kind == "h":
                o["load"]([(r1, x1, CB), (r2, agg, 0)])
                o["turn"](xT, r1)
                o["turn"](aT, r2)
                o["sage"](b, xT, aT)
                o["unturn"](buf("o"), b, hh, CB)
            elif kind == "x3":
                o["load"]([(r1, x2, CB), (r2, agg, 0)])
                o["turn"](xT, r1)
                o["turn"](aT, r2)
                o["layer2"](b, xT, aT)
                o["unturn"](buf("o"), b, x3, CB)
            else:
                g = buf("g", NB * HEADS * D)
                tab, to, w = (x1, x2, "gl_stack") if kind == "x2" else (x3, x4, "g3_stack")
                o["load"]([(r1, tab, CB), (g, agg4, 0)])
                o["turn"](xT, r1)
                pairs = o["heads"](w)
                o["gat1" if kind == "x2" else "layer3"](aT, xT, pairs)
                o["unturn"](buf("o"), aT, to, CB)
        rows_phase(CB, CR, build)

    def write_out():
        st = phase()
        ln = Line(st, 0)
        ln.load(lambda e, r: [e.dma_start(out.rearrange("(a n) d -> a (n d)", a=32),
                                          x4[0:N, :].rearrange("(a n) d -> a (n d)", a=32))], 1)
        ln.on("vector", lambda e, r: e.memset(Z[0][:], 0.0))
        st.run()
        st = phase(LANES, ROUNDS, ahead=2)
        for l in range(LANES):
            st.step(l, "fetch", "vector", fetch_all(l, [scat]), [(l, "store_p", 1)], early=True)
            st.step(l, "feats", "sync", lambda e, r, l=l: [e.dma_start(G[l][:, :, 0, :], block_rows(x4, l, r, base=CB))],
                    [(l, "store_p", 1)], dmas=1, early=True)

            def sc(e, r, l=l):
                return [e.indirect_dma_start(
                    out=out, out_offset=bass.IndirectOffsetOnAxis(ap=idx_s[l][:, 0, k:k + 1], axis=0),
                    in_=G[l][:, k, 0, :], in_offset=None, bounds_check=N - 1, oob_is_err=False) for k in range(TB)]
            st.step(l, "store_p", "gpsimd", sc, ["fetch", "feats"], dmas=TB)
        st.run()

    place_nodes()
    find_sources()
    finish_indices()
    for k in range(HOPS):
        edge_sum(hop[k], EP - 1, posx, norm, None, hop[k + 1])
    conv1()
    for k in range(HOPS - 1, -1, -1):
        edge_sum(utab[k + 1], EP - 1, posx, norm, None, utab[k], add=ytab[k])
    dense()
    compact("x1")
    edge_sum(x1, CB + EP - 1, comb, None, rcnt, agg)
    compact("h")
    logits(hh, True)
    softmax_terms()
    attend(hh, 0.0)
    compact("x2")
    edge_sum(x2, CB + EP - 1, comb, None, rcnt, agg)
    compact("x3")
    logits(x3, False)
    softmax_terms()
    attend(x3, 1e-16)
    compact("x4")
    write_out()
    stack.close()


_INS = ["x", "src", "dst", "edge_weight", "edge_weight1", "L0_gnn_W0", "L0_gnn_b0", "L0_gnn_W1", "L0_gnn_b1",
        "L1_gnn_W_sl", "L1_gnn_b_sl", "L1_gnn_W_sr", "L1_gnn_Wg_l", "L1_gnn_bg_l", "L1_gnn_Wg_r", "L1_gnn_bg_r",
        "L1_gnn_att", "L1_gnn_b_gat", "L1_gnn_gamma", "L1_gnn_beta", "L2_gnn_W", "L2_gnn_root", "L2_gnn_bias",
        "L3_gnn_W", "L3_gnn_att_src", "L3_gnn_att_dst", "L3_gnn_bias", "L3_gnn_dense_w", "L3_gnn_dense_b"]


def kernel(**inputs):
    import numpy as _np
    import concourse.bacc as _bacc
    from concourse import mybir as _mybir
    from concourse.bass_utils import run_bass_kernel_spmd as _run

    nc = _bacc.Bacc("TRN2", target_bir_lowering=False, num_devices=1)
    arrays, args = {}, []
    for name in _INS:
        a = _np.ascontiguousarray(inputs[name])
        arrays[f"in_{name}_dram"] = a
        args.append(nc.dram_tensor(f"in_{name}_dram", a.shape, _mybir.dt.from_np(a.dtype), kind="ExternalInput").ap())
    args.append(nc.dram_tensor("out_0_dram", (N, D), _mybir.dt.float32, kind="ExternalOutput").ap())
    bass_gnn_resnorm(nc, *args)
    r = _run(nc, [arrays], core_ids=[0])
    return r.results[0]["out_0_dram"]
```

```python
import concourse.bass as bass
from concourse import mybir
from concourse.alu_op_type import AluOpType as ALU
from contextlib import ExitStack

F32 = mybir.dt.float32
I32 = mybir.dt.int32
BF16 = mybir.dt.bfloat16
ACT = mybir.ActivationFunctionType
AX = mybir.AxisListType

N = 100000
E = 50000
D = 64
HID = 128
HOPS = 5
HEADS = 4
P = 128
TB = 4
LANES = 4
ROUNDS = -(-E // (P * TB * LANES))
TILES = ROUNDS * LANES * TB
EP = TILES * P
AB = EP // (P * TB)
SC = P * TB
NB = 8
CB = LANES * ROUNDS * P * NB
assert CB >= N
ABSENT = 1 << 20
NO_NODE = (1 << 17) - 1
EPS = 1e-5
LOW = -1.0e30
ENGINES = ("sync", "gpsimd", "scalar", "vector", "tensor")


class Steps:
    totals = {}

    def __init__(self, nc, sems, lanes, rounds, ahead=0):
        self.nc, self.sems, self.lanes, self.rounds, self.ahead = nc, sems, lanes, rounds, ahead
        self.list, self.late, self.place, self.per, self.base = [], [], {}, {}, {}

    def step(self, lane, name, engine, fn, after, dmas=0, early=False, late=False):
        key = (lane, name if dmas else engine)
        amount = 16 * dmas if dmas else 1
        if key not in self.base:
            if key not in self.sems:
                self.sems[key] = [self.nc.alloc_semaphore(f"done_{key[1]}_{lane}"), 0]
            self.base[key], self.per[key] = self.sems[key][1], 0
        self.per[key] += amount
        self.place[(lane, name)] = (key, self.per[key])
        entry = (lane, name, engine, fn, after, dmas, early, key)
        (self.late if late else self.list).append(entry)

    def emit(self, eng, which, i, s, shift):
        lane, name, engine, fn, after, dmas, early, key = s
        if engine != which:
            return
        waited = False
        r = i + shift
        for a in after:
            l, n, back = a if isinstance(a, tuple) else (lane, a, 0)
            k, upto = self.place[(l, n)]
            value = (r - back) * self.per[k] + (self.base[k] + upto)
            if isinstance(value, int) and value <= 0:
                continue
            eng.wait_ge(self.sems[k][0], value)
            if which in ("gpsimd", "sync"):
                eng.sem_inc(self.sems["waits_" + which][0], 1)
            waited = True
        made = fn(eng, r)
        if dmas:
            assert len(made) == dmas, (name, len(made), dmas)
            for m in made:
                m.then_inc(self.sems[key][0], 16)
        else:
            made.then_inc(self.sems[key][0], 1)

    def credit(self, eng, which):
        for lane, name, engine, fn, after, dmas, early, key in self.list + self.late:
            if engine == which and key in self.credits:
                n = self.credits[key]
                del self.credits[key]
                if not dmas:
                    eng.sem_inc(self.sems[key][0], n)
                else:
                    scratch, source = self.sems["scratch"]
                    at = self.sems["scratch_used"]
                    self.sems["scratch_used"] += 1
                    eng.dma_start(scratch[:, 8 * at:8 * at + 8], source).then_inc(self.sems[key][0], n)

    def sequence(self):
        if not self.ahead:
            whole = [(s, 0) for s in self.list]
            return [], whole, whole
        early = [[s for s in self.list if s[0] == l and s[6]] for l in range(self.lanes)]
        main = [[s for s in self.list if s[0] == l and not s[6]] for l in range(self.lanes)]
        pre = [(s, 0) for l in range(self.ahead) for s in early[l]]
        body, last = [], []
        for l in range(self.lanes):
            m = (l + self.ahead) % self.lanes
            nxt = 1 if l + self.ahead >= self.lanes else 0
            body += [(s, nxt) for s in early[m]] + [(s, 0) for s in main[l]]
            last += [(s, 0) for s in early[m] if not nxt] + [(s, 0) for s in main[l]]
        return pre, body, last

    @staticmethod
    def mixed(a, b):
        if not b:
            return a
        both = [((n + 0.5) / len(a), 0, n, x) for n, x in enumerate(a)]
        both += [((n + 0.5) / len(b), 1, n, x) for n, x in enumerate(b)]
        return [x for *_, x in sorted(both, key=lambda t: t[:3])]

    def program(self, eng, which):
        pre, body, last = self.sequence()
        late = [(s, 0) for s in self.late]
        on = lambda steps, n: [(s, d + n) for s, d in steps]
        R = self.rounds

        def put(i, steps):
            for s, d in steps:
                self.emit(eng, which, i, s, d)
        put(0, pre)
        if not late:
            if R > 1:
                with eng.Fori(0, R - 1, 1) as i:
                    put(i, body)
            put(R - 1, last)
            return
        put(0, body)
        with eng.Fori(0, R - 2, 1) as i:
            put(i, self.mixed(on(body, 1), late))
        put(R - 2, self.mixed(on(last, 1), late))
        put(R - 1, late)

    def run(self):
        self.credits = {}
        for k in self.base:
            if self.rounds > 1 and self.base[k] < self.per[k]:
                self.credits[k] = self.per[k]
                self.base[k] += self.per[k]
        block = self.nc.Block()
        with block:
            for which in ENGINES:
                def program(eng, which=which):
                    if any(s[2] == which for s in self.list + self.late):
                        self.credit(eng, which)
                        self.program(eng, which)
                    if which == "sync":
                        for k in self.base:
                            if isinstance(k[1], str) and k[1].startswith("store"):
                                eng.wait_ge(self.sems[k][0], self.base[k] + self.per[k] * self.rounds)
                program_of(block, which)(program)
        for k in self.base:
            self.sems[k][1] = self.base[k] + self.per[k] * self.rounds


def program_of(block, which):
    return {"sync": block.sync, "gpsimd": block.gpsimd, "scalar": block.scalar,
            "vector": block.vector, "tensor": block.tensor}[which]


def ds(i, n):
    return bass.ds(i, n)


class Line:

    def __init__(self, steps, lane, first=()):
        self.steps, self.lane, self.n, self.after = steps, lane, 0, list(first)
        self.dma = 0
        self.stores = 0

    def _add(self, engine, fn, dmas=0, kind=""):
        self.n += 1
        name = f"{kind}{self.dma}" if dmas else f"s{self.n}"
        self.dma += bool(dmas)
        self.steps.step(self.lane, name, engine, fn, self.after, dmas)
        return name

    def on(self, engine, fn):
        self.after = [self._add(engine, fn)]

    def load(self, fn, dmas):
        self.after = [self._add("sync", fn, dmas, "load")]

    def store(self, fn, dmas=1):
        return self._add("sync", fn, dmas, "store")


def bass_gnn_resnorm(nc, x, src, dst, edge_weight, edge_weight1, W0, b0, W1, b1, W_sl, b_sl, W_sr, Wg_l, bg_l,
                     Wg_r, bg_r, att, b_gat, gamma, beta, L2W, L2root, L2bias, L3W, att_src, att_dst,
                     L3bias, dense_w, dense_b, out):
    stack = ExitStack()
    sems = {"waits_" + e: [nc.alloc_semaphore("waits_" + e), 0] for e in ("gpsimd", "sync")}

    def dram(name, shape, dt=F32):
        return nc.dram_tensor(name, shape, dt, kind="Internal").ap()

    named = {}

    def sb(ctx, name, shape, dt=F32):
        named[name] = named.get(name, 0) + 1
        return ctx.enter_context(nc.sbuf_tensor(f"{name}_{named[name]}", shape, dt))

    dst_p = dram("dst_padded", (EP + 2,), I32)
    src_p = dram("src_padded", (EP,), I32)
    w_p = dram("w_padded", (EP,))
    place = dram("place_of_node", (CB, 2), I32)
    x0 = dram("x0", (CB, D))
    xc = dram("xc", (EP, D))
    hop = [xc] + [dram(f"hop{k}", (EP, D)) for k in range(1, HOPS + 1)]
    ytab = [dram(f"y{k}", (EP, D)) for k in range(HOPS + 1)]
    utab = [dram(f"u{k}", (EP, D)) for k in range(HOPS)] + [ytab[HOPS]]
    x1, hh, x2, x3 = (dram(n, (CB + EP, D)) for n in ("x1", "h_sage", "x2", "x3"))
    x4 = dram("x4", (CB + EP, D))
    agg = dram("agg", (EP, D))
    hs_t = dram("source_features", (EP, D))
    agg4 = dram("agg_heads", (EP, HEADS * D))

    PS = [stack.enter_context(nc.psum_tensor(f"bank{b}", [P, 512], F32)) for b in range(8)]
    ident = sb(stack, "ident", [P, P])
    bias_ones = sb(stack, "bias_ones", [1, P], BF16)
    bias_parts = [sb(stack, f"bias_part{n}", [1, 2 * HEADS * D], BF16) for n in range(3)]
    eps_col = sb(stack, "eps_col", [P, 1])
    last_row = sb(stack, "last_row", [P, 1])
    dstc = sb(stack, "dst_of_edge", [P, TILES + 1])
    comb = sb(stack, "row_of_source", [P, TILES], I32)
    posx = sb(stack, "compact_row_of_source", [P, TILES], I32)
    lastx = sb(stack, "row_of_last_edge", [P, TILES], I32)
    scat = sb(stack, "node_to_write", [P, TILES], I32)
    dsti = sb(stack, "dst_index", [P, TILES], I32)
    srci = sb(stack, "src_index", [P, TILES], I32)
    norm = sb(stack, "norm_of_edge", [P, TILES])
    rcnt = sb(stack, "one_over_count", [P, TILES])
    LG = sb(stack, "logits", [P, TILES, 2 * HEADS])
    AE = LG
    idx_s, dst_s, w_s, rows, M, C, G, S, Z = ([] for _ in range(9))
    for l in range(LANES):
        idx_s.append(sb(stack, f"idx_slot{l}", [P, 2, TB], I32))
        dst_s.append(sb(stack, f"dst_slot{l}", [P, TB + 1]))
        w_s.append(sb(stack, f"weight_slot{l}", [P, TB]))
        rows.append(sb(stack, f"dst_rows{l}", [P, TB, P], I32))
        M.append(sb(stack, f"same_dst{l}", [P, TB, P]))
        C.append(sb(stack, f"goes_on{l}", [P, TB, P]))
        G.append(sb(stack, f"gathered{l}", [P, TB, 2, D]))
        S.append(sb(stack, f"sums{l}", [P, TB, HEADS * D + HEADS]))
        Z.append(sb(stack, f"work{l}", [P, TB * D]))

    sems["scratch"] = (sb(stack, "credit_scratch", [16, 8 * 64]), x[0:16, 0:8])
    sems["scratch_used"] = 0

    def phase(lanes=1, rounds=1, ahead=0):
        return Steps(nc, sems, lanes, rounds, ahead)

    wts = {}
    with nc.allow_non_contiguous_dma(reason="small weights"):
        with ExitStack() as ctx:
            raw = {}

            def w_sb(name, shape):
                wts[name] = sb(stack, name, shape)
                return wts[name]

            st = phase()
            ln = Line(st, 0)
            for n in ("bd_sl", "bd_sr", "bd_gmean", "bd_l2w", "bd_l2root", "bd_l3", "center", "mean"):
                w_sb(n, [P, P])
            w_sb("w00", [P, 2, P])
            w_sb("w10", [P, 2, P])
            w_sb("w0cat", [P, 3, P])
            w_sb("w1cat", [P, HOPS + 1, D])
            w_sb("gl_stack", [P, 2, 2, P])
            w_sb("g3_stack", [P, 2, 2, P])
            w_sb("glr", [P, 2, HEADS * D])
            w_sb("g3cols", [P, 2 * HEADS])
            w_sb("att_b", [P, 2 * HEADS * D])
            w_sb("glr_bias", [1, 2 * HEADS * D])
            for n in ("b0", "b1", "bsl", "bg", "gamma", "beta", "bl2", "bl3"):
                w_sb("v_" + n, [P, 1])
            t_w3 = sb(ctx, "t_w3", [D, HEADS * D])
            t_w3T = sb(ctx, "t_w3T", [D, HEADS, D])
            t_dw = sb(ctx, "t_dw", [D, HEADS, D])
            t_as = sb(ctx, "t_as", [D, HEADS])
            t_ad = sb(ctx, "t_ad", [D, HEADS])
            t_gl = sb(ctx, "t_gl", [P, HEADS * D])
            t_b3 = sb(ctx, "t_b3", [D, HEADS])
            t_bg = sb(ctx, "t_bg", [P, HEADS])
            t_bb = sb(ctx, "t_bb", [P, 3])
            t_br = sb(ctx, "t_br", [1, 2, HEADS * D])
            big = sb(ctx, "big", [P, CB // P, 2], I32)
            padv = sb(ctx, "padv", [1, 512], I32)
            zero = sb(ctx, "zero", [P, 256])

            def clear(eng, r):
                for t in (*wts.values(), t_gl, t_b3):
                    eng.memset(t[:], 0.0)
                for l in range(LANES):
                    for t in (G[l], S[l], w_s[l], Z[l], M[l], C[l]):
                        eng.memset(t[:], 0.0)
                    eng.memset(idx_s[l][:], 0)
                eng.memset(LG[:], 0.0)
                eng.memset(padv[:, 0:510], NO_NODE)
                eng.memset(padv[0:1, 510:511], -1)
                eng.memset(big[:, :, 0], ABSENT)
                eng.memset(big[:, :, 1], 0)
                eng.memset(zero[:], 0.0)
                eng.memset(bias_ones[:], 1.0)
                eng.memset(eps_col[:], EPS)
                return eng.memset(dstc[:, 0:1], -1.0)

            def clear2(eng, r):
                eng.memset(wts["center"][0:D, 0:D], -1.0 / D)
                eng.memset(wts["center"][D:P, D:P], -1.0 / D)
                eng.memset(wts["mean"][0:D, 0:D], 1.0 / D)
                return eng.memset(wts["mean"][D:P, D:P], 1.0 / D)

            ln.on("vector", clear)
            ln.on("vector", clear2)

            def loads(eng, r):
                d = []

                def put(o, i_):
                    d.append(eng.dma_start(o, i_))
                for q, (lo, hi) in enumerate(((0, D), (D, P))):
                    put(wts["bd_sl"][lo:hi, lo:hi], W_sl)
                    put(wts["bd_sr"][lo:hi, lo:hi], W_sr)
                    put(wts["bd_l2w"][lo:hi, lo:hi], L2W)
                    put(wts["bd_l2root"][lo:hi, lo:hi], L2root)
                    put(wts["w00"][lo:hi, q, :], W0[0, :, :])
                    put(wts["w10"][:, q, lo:hi], W1[0, :, :])
                    for n, v in (("b1", b1), ("bsl", b_sl), ("gamma", gamma), ("beta", beta), ("bl2", L2bias)):
                        put(wts["v_" + n][lo:hi, :], v.rearrange("(p a) -> p a", a=1))
                    put(t_bg[lo:hi, :], bg_l.rearrange("(h p) -> p h", h=HEADS))
                    put(t_bb[lo:hi, 0:1], b_gat.rearrange("(p a) -> p a", a=1))
                    put(t_bb[lo:hi, 1:2], dense_b.rearrange("(p a) -> p a", a=1))
                    put(t_gl[lo:hi, :], Wg_l)
                put(wts["v_b0"][:, :], b0.rearrange("(p a) -> p a", a=1))
                put(wts["w0cat"][:, :, :], W0.rearrange("k f m -> (k f) m").rearrange("(c p) m -> p c m", p=P))
                put(wts["w1cat"][:, :, :], W1.rearrange("k f m -> f k m"))
                for c in range(2):
                    for q in range(2):
                        for j in range(2):
                            h = 2 * c + j
                            put(wts["gl_stack"][j * D:(j + 1) * D, c, q, q * D:(q + 1) * D],
                                Wg_l[:, h * D:(h + 1) * D])
                put(wts["glr"][0:D, 0, :], Wg_l)
                put(wts["glr"][D:P, 0, :], Wg_r)
                put(wts["glr"][D:P, 1, :], Wg_r)
                for s in range(2):
                    put(wts["att_b"][:, s * HEADS * D:(s + 1) * HEADS * D],
                        att.rearrange("h d -> (h d)").partition_broadcast(P))
                put(t_br[0:1, 0, :], bg_l.rearrange("(a n) -> a n", a=1))
                put(t_br[0:1, 1, :], bg_r.rearrange("(a n) -> a n", a=1))
                put(t_w3[:, :], L3W)
                put(t_dw[:, :, :], dense_w.rearrange("(h p) n -> p h n", h=HEADS))
                put(t_as[:, :], att_src.rearrange("h d -> d h"))
                put(t_ad[:, :], att_dst.rearrange("h d -> d h"))
                put(t_b3[:, :], L3bias.rearrange("(h p) -> p h", h=HEADS))
                row = lambda a: a.rearrange("(a n) -> a n", a=1)
                put(row(dst_p[1:E + 1]), row(dst))
                put(row(src_p[0:E]), row(src))
                put(row(w_p[0:E]), row(edge_weight))
                put(row(dst_p[0:1]), padv[0:1, 510:511])
                put(row(dst_p[EP + 1:EP + 2]), padv[0:1, 510:511])
                at = E
                while at < EP:
                    n = min(EP - at, 500)
                    put(row(dst_p[at + 1:at + 1 + n]), padv[0:1, 0:n])
                    at += n
                pad = EP - E
                assert (CB - N) % 96 == 0
                q = 48
                put(src_p[E:EP].rearrange("(p n) -> p n", p=q), zero[0:q, 0:pad // q].bitcast(I32))
                put(w_p[E:EP].rearrange("(p n) -> p n", p=q), zero[0:q, 0:pad // q])
                put(place.rearrange("(p n) w -> p n w", p=P), big[:, :, :])
                put(x0[0:N, :].rearrange("(a n) d -> a (n d)", a=32), x.rearrange("(a n) d -> a (n d)", a=32))
                for k in range((CB - N) // 96):
                    put(x0[N + 96 * k:N + 96 * (k + 1), :], zero[0:96, 0:D])
                return d

            count = [0]

            class Fake:
                def dma_start(self, o, i_):
                    count[0] += 1
                    return 0
            loads(Fake(), 0)
            ln.load(loads, count[0])

            def iotas(eng, r):
                return eng.affine_select(out=ident[:], in_=ident[:], compare_op=ALU.not_equal, fill=1.0, base=0,
                                         pattern=[[-1, P]], channel_multiplier=1)
            ln.on("vector", lambda e, r: e.memset(ident[:], 0.0))
            ln.on("gpsimd", iotas)
            ln.on("vector", lambda e, r: e.tensor_copy(last_row[:], ident[:, P - 1:P]))

            def tr3(e, r):
                for h in range(HEADS):
                    m = e.transpose(PS[0][0:D, h * D:(h + 1) * D], t_w3[:, h * D:(h + 1) * D], ident[0:D, 0:D])
                return m
            ln.on("tensor", tr3)
            ln.on("vector", lambda e, r: e.tensor_copy(t_w3T[:].rearrange("p h d -> p (h d)"), PS[0][0:D, 0:HEADS * D]))

            def prods(e, r):
                for h in range(HEADS):
                    w = t_w3T[:, h, :]
                    e.matmul(PS[1][0:D, h:h + 1], w, t_as[:, h:h + 1], start=True, stop=True)
                    e.matmul(PS[1][0:D, HEADS + h:HEADS + h + 1], w, t_ad[:, h:h + 1], start=True, stop=True)
                    e.matmul(PS[2][0:D, h * D:(h + 1) * D], w, t_dw[:, h, :], start=True, stop=True)
                for h in range(HEADS):
                    m = e.matmul(PS[3][0:D, 0:1], t_dw[:, h, :], t_b3[:, h:h + 1], start=h == 0, stop=h == HEADS - 1)
                return m
            ln.on("tensor", prods)

            scr = sb(ctx, "scr", [D, 2 * HEADS + 1 + HEADS * D])

            def cp1(e, r):
                e.tensor_copy(scr[:, 0:2 * HEADS], PS[1][0:D, 0:2 * HEADS])
                e.tensor_copy(scr[:, 2 * HEADS + 1:], PS[2][0:D, 0:HEADS * D])
                return e.tensor_copy(scr[:, 2 * HEADS:2 * HEADS + 1], PS[3][0:D, 0:1])
            ln.on("vector", cp1)
            s_as, s_ad, s_c = scr[:, 0:HEADS], scr[:, HEADS:2 * HEADS], scr[:, 2 * HEADS:2 * HEADS + 1]
            s_wd = scr[:, 2 * HEADS + 1:].rearrange("p (h d) -> p h d", h=HEADS)
            s_sum = sb(ctx, "s_sum", [D, HEADS])
            s_m3 = sb(ctx, "s_m3", [D, D])
            ln.on("vector", lambda e, r: e.tensor_tensor(s_sum[:], s_as, s_ad, ALU.add))
            ln.on("vector", lambda e, r: e.tensor_reduce(s_m3[:], s_wd.rearrange("p h d -> p d h"), AX.X, ALU.add))
            ln.on("vector", lambda e, r: e.tensor_tensor(s_c, s_c, t_bb[0:D, 1:2], ALU.add))

            def spread(e, r):
                d = [e.dma_start(wts["g3cols"][0:D, 0:HEADS], s_as),
                     e.dma_start(wts["g3cols"][D:P, 0:HEADS], s_ad),
                     e.dma_start(wts["g3cols"][D:P, HEADS:2 * HEADS], s_sum[:])]
                for q in range(2):
                    d.append(e.dma_start(wts["bd_l3"][q * D:(q + 1) * D, q * D:(q + 1) * D], s_m3[:]))
                    d.append(e.dma_start(wts["v_bl3"][q * D:(q + 1) * D, :], s_c))
                    for c in range(2):
                        for j in range(2):
                            d.append(e.dma_start(wts["g3_stack"][j * D:(j + 1) * D, c, q, q * D:(q + 1) * D],
                                                 s_wd[:, 2 * c + j, :]))
                return d
            ln.load(spread, 3 + 2 * (2 + 4))
            t_m = sb(ctx, "t_m", [P, D])
            t_v = sb(ctx, "t_v", [P, 1])
            ln.on("vector", lambda e, r: e.tensor_reduce(t_m[:], t_gl[:].rearrange("p (h d) -> p d h", h=HEADS), AX.X, ALU.add))
            ln.on("vector", lambda e, r: e.tensor_reduce(t_v[:], t_bg[:], AX.X, ALU.add))

            def fin(e, r):
                q = 1.0 / HEADS
                for a in range(2):
                    sl = slice(a * D, (a + 1) * D)
                    e.tensor_scalar(wts["bd_gmean"][sl, sl], t_m[sl, :], q, None, ALU.mult)
                e.tensor_scalar(wts["v_bg"][:], t_v[:], q, t_bb[:, 0:1], ALU.mult, ALU.add)
                g = wts["gl_stack"][:].rearrange("p c q m -> p (c q m)")
                e.tensor_scalar(g, g, q, None, ALU.mult)
                e.tensor_tensor(wts["glr"][D:P, 1, :], wts["glr"][D:P, 1, :], t_gl[D:P, :], ALU.add)
                e.tensor_tensor(wts["center"][:], wts["center"][:], ident[:], ALU.add)
                s = HEADS * D
                e.tensor_tensor(wts["glr_bias"][0:1, 0:s], t_br[0:1, 0, :], t_br[0:1, 1, :], ALU.add)
                return e.tensor_tensor(wts["glr_bias"][0:1, s:2 * s], t_br[0:1, 0, :], t_br[0:1, 1, :], ALU.add)
            ln.on("vector", fin)
            rest, cut = wts["glr_bias"], sb(ctx, "cut", [1, 2 * HEADS * D])
            for n in range(3):
                ln.on("vector", lambda e, r, n=n: e.tensor_copy(bias_parts[n][:], rest[:]))
                ln.on("vector", lambda e, r, n=n: e.tensor_copy(cut[:], bias_parts[n][:]))
                ln.on("vector", lambda e, r: e.tensor_tensor(rest[:], rest[:], cut[:], ALU.subtract))
            ln.on("vector", lambda e, r: e.tensor_tensor(wts["bd_l3"][:], wts["bd_l3"][:], ident[:], ALU.add))
            squares = [wts["bd_gmean"][:], wts["bd_l3"][:]] + [
                wts[n][:, c, q, :] for n in ("gl_stack", "g3_stack") for c in range(2) for q in range(2)]
            turned = sb(ctx, "turned", [P, P])
            for w in squares:
                ln.on("tensor", lambda e, r, w=w: e.transpose(PS[0][:, 0:P], w, ident[:]))
                ln.on("vector", lambda e, r: e.tensor_copy(turned[:], PS[0][:, 0:P]))
                ln.on("tensor", lambda e, r: e.matmul(PS[1][:, 0:P], turned[:], wts["center"][:], start=True, stop=True))
                ln.on("vector", lambda e, r, w=w: e.tensor_copy(w, PS[1][:, 0:P]))
            for n in ("v_bg", "v_bl3"):
                ln.on("tensor", lambda e, r, n=n: e.matmul(PS[1][:, 0:1], wts["center"][:], wts[n][:], start=True, stop=True))
                ln.on("vector", lambda e, r, n=n: e.tensor_copy(wts[n][:], PS[1][:, 0:1]))
            st.run()

    def seg_scan(ln, ctx, tag, vals, outs, go, kind, reverse=False):
        V = len(vals)
        ends = sb(ctx, f"ends{tag}", [AB, 2, P])
        ends_r = sb(ctx, f"endsr{tag}", [P, 2, AB])
        carry = sb(ctx, f"carry{tag}", [P, AB + 1])
        ini = sb(ctx, f"ini{tag}", [AB, P])
        o0, o1, none = (ALU.mult, ALU.add, 0.0) if kind == "sum" else (ALU.add, ALU.max, LOW)
        rev = (lambda a: a[:, ::-1]) if reverse else (lambda a: a)
        end = 0 if reverse else SC - 1

        def scan(init):
            def f(e, r):
                for v in range(V):
                    m = e.tensor_tensor_scan(rev(outs[v]), rev(go), rev(vals[v]), init(v), o0, o1)
                return m
            return f
        ln.on("vector", lambda e, r: e.memset(ends[:], 0.0))
        ln.on("vector", scan(lambda v: none))

        def collect(e, r):
            for v in range(V):
                e.tensor_copy(ends[:, 0, v:v + 1], outs[v][:, end:end + 1])
            return e.tensor_reduce(ends[:, 1, 0:1], go, AX.X, ALU.min)
        ln.on("vector", collect)
        ln.on("vector", lambda e, r: e.tensor_copy(ends[:, 1, 1:V + 1], ends[:, 1, 0:1].to_broadcast([AB, V])))

        def tr(e, r):
            e.transpose(PS[6][:, 0:AB], ends[:, 0, :], ident[0:AB, 0:AB])
            return e.transpose(PS[6][:, P:P + AB], ends[:, 1, :], ident[0:AB, 0:AB])
        ln.on("tensor", tr)

        def back(e, r):
            e.tensor_copy(ends_r[:, 0, :], PS[6][:, 0:AB])
            e.memset(carry[:], none)
            return e.tensor_copy(ends_r[:, 1, :], PS[6][:, P:P + AB])
        ln.on("vector", back)
        o = carry[:, 0:AB] if reverse else carry[:, 1:AB + 1]
        ln.on("vector", lambda e, r: e.tensor_tensor_scan(rev(o), rev(ends_r[:, 1, :]), rev(ends_r[:, 0, :]), none, o0, o1))
        into = carry[:, 1:AB + 1] if reverse else carry[:, 0:AB]
        ln.on("tensor", lambda e, r: e.transpose(PS[7][0:AB, 0:P], into, ident[:, :]))
        ln.on("vector", lambda e, r: e.tensor_copy(ini[:], PS[7][0:AB, 0:P]))
        ln.on("vector", scan(lambda v: ini[:, v:v + 1]))

    def from_scan(ln, k, src_ap, dst_ap):
        def tr(e, r):
            for g in range(TB):
                m = e.transpose(PS[k][:, g * AB:(g + 1) * AB], src_ap[:, g * P:(g + 1) * P], ident[0:AB, 0:AB])
            return m
        ln.on("tensor", tr)
        ln.on("vector", lambda e, r: e.tensor_copy(dst_ap.rearrange("p (a g) -> p g a", g=TB),
                                                   PS[k][:, 0:TB * AB].rearrange("p (g a) -> p g a", g=TB)))

    def to_scan(ln, k, src_ap, dst_ap):
        v = src_ap.rearrange("p (a g) -> p g a", g=TB)

        def tr(e, r):
            for g in range(TB):
                m = e.transpose(PS[k][0:AB, g * P:(g + 1) * P], v[:, g, :], ident[:, :])
            return m
        ln.on("tensor", tr)
        ln.on("vector", lambda e, r: e.tensor_copy(dst_ap, PS[k][0:AB, :]))

    cont = sb(stack, "same_as_before", [AB, SC])
    nsame = sb(stack, "same_as_next", [AB, SC])
    last = sb(stack, "is_last", [AB, SC])
    wd = sb(stack, "w_times_dis", [P, TILES])
    own = sb(stack, "own_place", [P, TILES, 2], I32)
    found = sb(stack, "source_place", [P, TILES, 2], I32)

    with ExitStack() as ctx:
        st = phase()
        ln = Line(st, 0)
        t = {n: sb(ctx, "p1_" + n, [AB, SC], I32) for n in ("d", "dp", "dn", "s")}
        f = {n: sb(ctx, "p1f_" + n, [AB, SC]) for n in
             ("w", "one", "deg", "cnt", "d", "s", "m", "r", "rk", "fr", "fd", "ld", "lr", "sc")}

        def loads(e, r):
            v = lambda a: a.rearrange("(a n) -> a n", a=AB)
            return [e.dma_start(t["d"][:], v(dst_p[1:EP + 1])), e.dma_start(t["dp"][:], v(dst_p[0:EP])),
                    e.dma_start(t["dn"][:], v(dst_p[2:EP + 2])), e.dma_start(t["s"][:], v(src_p[:])),
                    e.dma_start(f["w"][:], v(w_p[:]))]
        ln.load(loads, 5)

        def flags(e, r):
            e.tensor_tensor(cont[:], t["d"][:], t["dp"][:], ALU.is_equal)
            e.tensor_tensor(nsame[:], t["d"][:], t["dn"][:], ALU.is_equal)
            e.tensor_copy(f["d"][:], t["d"][:])
            e.tensor_copy(f["s"][:], t["s"][:])
            return e.memset(f["one"][:], 1.0)
        ln.on("vector", flags)
        ln.on("vector", lambda e, r: e.tensor_scalar(last[:], nsame[:], -1.0, 1.0, ALU.mult, ALU.add))
        ri = sb(ctx, "ri", [AB, SC], I32)
        ln.on("gpsimd", lambda e, r: e.iota(ri[:].rearrange("a (g p) -> a g p", g=TB), pattern=[[1, TB], [TB, P]],
                                            base=0, channel_multiplier=SC))
        ln.on("gpsimd", lambda e, r: e.iota(own[:, :, 0].rearrange("p (a g) -> p a g", g=TB),
                                            pattern=[[SC, AB], [1, TB]], base=0, channel_multiplier=TB))
        seg_scan(ln, ctx, "a", [f["w"][:], f["one"][:]], [f["deg"][:], f["cnt"][:]], cont[:], "sum")
        ln.on("vector", lambda e, r: e.tensor_scalar(f["m"][:], f["deg"][:], 0.0, None, ALU.is_gt))
        ln.on("vector", lambda e, r: e.tensor_scalar(f["r"][:], f["m"][:], -1.0, 1.0, ALU.mult, ALU.add))
        ln.on("vector", lambda e, r: e.tensor_tensor(f["r"][:], f["r"][:], f["deg"][:], ALU.add))
        ln.on("scalar", lambda e, r: e.activation(f["r"][:], f["r"][:], ACT.Sqrt))
        ln.on("vector", lambda e, r: e.reciprocal(f["r"][:], f["r"][:]))
        ln.on("vector", lambda e, r: e.tensor_tensor(f["r"][:], f["r"][:], f["m"][:], ALU.mult))

        def prep(e, r):
            e.tensor_copy(f["rk"][:], ri[:])
            e.tensor_tensor(f["ld"][:], f["r"][:], last[:], ALU.mult)
            e.tensor_scalar(f["cnt"][:], f["cnt"][:], 1.0, None, ALU.max)
            return e.tensor_scalar(f["sc"][:], f["d"][:], float(-ABSENT), None, ALU.add)
        ln.on("vector", prep)

        def prep2(e, r):
            e.reciprocal(f["cnt"][:], f["cnt"][:])
            e.tensor_tensor(f["sc"][:], f["sc"][:], last[:], ALU.mult)
            return e.tensor_tensor(f["lr"][:], f["rk"][:], last[:], ALU.mult)
        ln.on("vector", prep2)
        seg_scan(ln, ctx, "b", [f["ld"][:], f["lr"][:]], [f["fd"][:], f["fr"][:]], nsame[:], "sum", reverse=True)

        def prep3(e, r):
            e.tensor_scalar(f["sc"][:], f["sc"][:], float(ABSENT), None, ALU.add)
            e.tensor_scalar(f["fr"][:], f["fr"][:], float(CB), None, ALU.add)
            return e.tensor_tensor(f["m"][:], f["w"][:], f["fd"][:], ALU.mult)
        ln.on("vector", prep3)
        disw = own[:, :, 1].bitcast(F32)
        for k, (a, b) in enumerate(((f["d"], dstc[:, 1:]), (f["d"], dsti[:]), (f["s"], srci[:]), (f["m"], wd[:]),
                                    (f["cnt"], rcnt[:]), (f["sc"], scat[:]), (f["fr"], lastx[:]), (f["r"], disw))):
            from_scan(ln, k % 6, a[:], b)
        st.run()

    def fetch(l, cols, weight=None):
        def f(e, r):
            t0 = r * (LANES * TB) + l * TB
            for n, c in enumerate(cols):
                m = e.tensor_copy(idx_s[l][:, n, :], c[:, ds(t0, TB)])
            e.tensor_copy(dst_s[l][:, :], dstc[:, ds(t0, TB + 1)])
            if weight is not None:
                e.tensor_copy(w_s[l][:, :], weight[:, ds(t0, TB)])
            return m
        return f

    def fetch_all(l, cols, weight=None):
        def f(e, r):
            t0 = r * (LANES * TB) + l * TB
            m = e.tensor_copy(dst_s[l][:, :], dstc[:, ds(t0, TB + 1)])
            for n, c in enumerate(cols):
                m = e.tensor_copy(idx_s[l][:, n, :], c[:, ds(t0, TB)])
            if weight is not None:
                m = e.tensor_copy(w_s[l][:, :], weight[:, ds(t0, TB)])
            return m
        return f

    def load_rows(l):
        return lambda e, r: [e.dma_start(rows[l][:].rearrange("p t n -> p (t n)"),
                                         dst_p[ds((r * LANES + l) * (TB * P) + 1, TB * P)].partition_broadcast(P))]

    def gather(l, pairs):
        def f(e, r):
            d = []
            for k in range(TB):
                for tab, where, n, top in pairs:
                    d.append(e.indirect_dma_start(
                        out=where(l, k), out_offset=None, in_=tab,
                        in_offset=bass.IndirectOffsetOnAxis(ap=idx_s[l][:, n, k:k + 1], axis=0),
                        bounds_check=top, oob_is_err=False))
            return d
        return f

    def masks(l, weighted):
        def f(e, r):
            for k in range(TB):
                if weighted:
                    e.tensor_scalar(M[l][:, k, :], rows[l][:, k, :], dst_s[l][:, k + 1:k + 2], w_s[l][:, k:k + 1],
                                    ALU.is_equal, ALU.mult)
                else:
                    e.tensor_scalar(M[l][:, k, :], rows[l][:, k, :], dst_s[l][:, k + 1:k + 2], None, ALU.is_equal)
                m = e.tensor_scalar(C[l][96:P, k, :], rows[l][96:P, k, :], dst_s[l][96:P, k:k + 1],
                                    last_row[96:P, :], ALU.is_equal, ALU.mult)
            return m
        return f

    def block_rows(tab, l, r, w=D, base=0):
        return tab[ds((r * LANES + l) * (TB * P) + base, TB * P), :].rearrange("(p k) d -> p k d", k=TB)

    def sums(st, l, rhs, width, first):
        for k in range(TB):
            def main(e, r, k=k):
                return e.matmul(PS[k][:, 0:width], M[l][:, k, :], rhs(k), start=True, stop=False)

            def carry(e, r, k=k):
                pl = l if k else (l - 1) % LANES
                pk = (k - 1) % TB
                return e.matmul(PS[k][:, 0:width], C[l][96:P, k, :], S[pl][96:P, pk, 0:width], start=False, stop=True)
            prev_lane, back = (l - 1) % LANES, (1 if l == 0 else 0)
            st.step(l, f"main{k}", "tensor", main, (first if k == 0 else []) + [(prev_lane, f"out{k}", back)])
            before = f"out{k - 1}" if k else (prev_lane, f"out{TB - 1}", back)
            st.step(l, f"carry{k}", "tensor", carry, [before])
            st.step(l, f"out{k}", "scalar",
                    lambda e, r, k=k: e.copy(S[l][:, k, 0:width], PS[k][:, 0:width]),
                    [f"carry{k}"] + ([(l, "store", 1)] if k == 0 else []))

    def edge_sum(tab, top, index, weight, scale, target, add=None, beside=()):
        st = phase(LANES, ROUNDS, ahead=2)
        for l in range(LANES):
            st.step(l, "fetch", "vector", fetch_all(l, [index], weight if scale is None else scale),
                    [(l, "mask", 1), (l, f"main{TB - 1}", 1)] + ([(l, "post", 1)] if scale is not None else []),
                    early=True)
            st.step(l, "rows", "sync", load_rows(l), [(l, "mask", 1)], dmas=1, early=True)
            if add is not None:
                st.step(l, "extra", "sync", lambda e, r, l=l: [e.dma_start(
                    Z[l][:].rearrange("p (k d) -> p k d", k=TB), block_rows(add, l, r))],
                    [(l, "store", 1)], dmas=1, early=True)
            st.step(l, "gather", "gpsimd", gather(l, [(tab, lambda l, k: G[l][:, k, 0, :], 0, top)]), ["fetch"],
                    dmas=TB, early=True)
            st.step(l, "mask", "vector", masks(l, weight is not None), ["fetch", "rows", (l, f"carry{TB - 1}", 1)],
                    early=True)
            sums(st, l, lambda k, l=l: G[l][:, k, 0, :], D, ["mask", "gather"])
            if add is not None:
                st.step(l, "post", "vector", lambda e, r, l=l: e.tensor_tensor(
                    Z[l][:].rearrange("p (k d) -> p k d", k=TB), Z[l][:].rearrange("p (k d) -> p k d", k=TB),
                    S[l][:, :, 0:D], ALU.add), [f"out{TB - 1}", "extra"])
            elif scale is not None:
                st.step(l, "post", "vector", lambda e, r, l=l: e.tensor_tensor(
                    Z[l][:].rearrange("p (k d) -> p k d", k=TB), S[l][:, :, 0:D],
                    w_s[l][:].rearrange("p (k a) -> p k a", a=1).to_broadcast([P, TB, D]), ALU.mult),
                    [f"out{TB - 1}", (l, "store", 1)])
            direct = add is None and scale is None
            st.step(l, "store", "sync", lambda e, r, l=l: [e.dma_start(
                block_rows(target, l, r), S[l][:, :, 0:D] if direct else
                Z[l][:].rearrange("p (k d) -> p k d", k=TB))],
                [f"out{TB - 1}"] if direct else ["post"], dmas=1)
        finish(st, beside)

    def finish(st, beside):
        with ExitStack() as ctx:
            for rows_work in beside:
                rows_work(st, ctx)
            st.run()

    def place_nodes(beside=()):
        st = phase(LANES, ROUNDS, ahead=2)
        for l in range(LANES):
            def fe(e, r, l=l):
                t0 = r * (LANES * TB) + l * TB
                e.tensor_copy(G[l][:, :, 0, 0:2].bitcast(I32), own[:, ds(t0, TB), :])
                return e.tensor_copy(idx_s[l][:, 0, :], scat[:, ds(t0, TB)])
            st.step(l, "fetch", "vector", fe, [(l, "store_p", 1)], early=True)

            def sc(e, r, l=l):
                return [e.indirect_dma_start(
                    out=place, out_offset=bass.IndirectOffsetOnAxis(ap=idx_s[l][:, 0, k:k + 1], axis=0),
                    in_=G[l][:, k, 0, 0:2].bitcast(I32), in_offset=None, bounds_check=N - 1, oob_is_err=False)
                    for k in range(TB)]
            st.step(l, "store_p", "gpsimd", sc, ["fetch"], dmas=TB)
        finish(st, beside)

    def find_sources(beside=()):
        st = phase(LANES, ROUNDS, ahead=2)
        for l in range(LANES):
            st.step(l, "fetch", "vector", fetch_all(l, [srci, dsti]), [(l, "store", 1), (l, "keep", 1)], early=True)
            st.step(l, "gather2", "gpsimd", gather(l, [
                (place, lambda l, k: G[l][:, k, 1, 0:2].bitcast(I32), 0, N - 1),
                (x, lambda l, k: G[l][:, k, 0, :], 1, N - 1)]), ["fetch"], dmas=2 * TB, early=True)

            def keep(e, r, l=l):
                return e.tensor_copy(found[:, ds(r * (LANES * TB) + l * TB, TB), :], G[l][:, :, 1, 0:2].bitcast(I32))
            st.step(l, "keep", "vector", keep, ["gather2"])
            st.step(l, "store", "sync", lambda e, r, l=l: [e.dma_start(block_rows(xc, l, r), G[l][:, :, 0, :])],
                    ["gather2"], dmas=1)
        finish(st, beside)

    def finish_indices():
        with ExitStack() as ctx:
            st = phase()
            ln = Line(st, 0)
            pf, sf, v = (sb(ctx, n, [P, TILES]) for n in ("pf", "sf", "v"))

            def a(e, r):
                e.tensor_copy(pf[:], found[:, :, 0])
                e.tensor_copy(sf[:], srci[:])
                e.tensor_copy(posx[:], found[:, :, 0])
                return e.tensor_tensor(norm[:], wd[:], found[:, :, 1].bitcast(F32), ALU.mult)
            ln.on("vector", a)
            ln.on("vector", lambda e, r: e.tensor_scalar(v[:], pf[:], float(ABSENT), None, ALU.is_lt))
            ln.on("vector", lambda e, r: e.scalar_tensor_tensor(pf[:], pf[:], float(CB), sf[:], ALU.add, ALU.subtract))
            ln.on("vector", lambda e, r: e.tensor_tensor(pf[:], pf[:], v[:], ALU.mult))
            ln.on("vector", lambda e, r: e.tensor_tensor(comb[:], pf[:], sf[:], ALU.add))
            st.run()

    def logits(tab, v2):
        st = phase(LANES, ROUNDS, ahead=2)
        WZ = 2 * HEADS * D
        ctx = ExitStack()
        zbuf = [[sb(ctx, f"z{k}{j}", [P, WZ]) for j in range(2)] for k in range(2)]
        for l in range(LANES):
            st.step(l, "fetch", "vector", fetch_all(l, [comb, lastx]), [(l, "store", 1), (l, "tr3", 1)], early=True)
            st.step(l, "gather2", "gpsimd", gather(l, [
                (tab, lambda l, k: G[l][:, k, 0, :], 0, CB + EP - 1),
                (tab, lambda l, k: G[l][:, k, 1, :], 1, CB + EP - 1)]), ["fetch"], dmas=2 * TB, early=True)
            st.step(l, "store", "sync", lambda e, r, l=l: [e.dma_start(block_rows(hs_t, l, r), G[l][:, :, 0, :])],
                    ["gather2"], dmas=1)
            pv, bk = (l - 1) % LANES, (1 if l == 0 else 0)
            def front(k, l=l, pv=pv, bk=bk):
                def tr(e, r, k=k, l=l):
                    return e.transpose(PS[k][:, 0:P], G[l][:, k, :, :].rearrange("p a d -> p (a d)"), ident[:])
                st.step(l, f"tr{k}", "tensor", tr, (["gather2"] if k == 0 else []) + [(pv, f"cp{k}", bk)])
                st.step(l, f"cp{k}", "scalar", lambda e, r, k=k, l=l: e.copy(M[l][:, k, :], PS[k][:, 0:P]),
                        [f"tr{k}", (l, f"z{k}", 1)])

            def back_(k, l=l, pv=pv, bk=bk):
                def zmm(e, r, k=k, l=l):
                    if not v2:
                        return e.matmul(PS[4 + k][:, 0:2 * HEADS], M[l][:, k, :], wts["g3cols"][:], start=True, stop=True)
                    e.matmul(PS[4 + k][:, 0:WZ], bias_ones[0:1, :], bias_parts[0][0:1, :], start=True, stop=False)
                    e.matmul(PS[4 + k][:, 0:WZ], bias_ones[0:1, :], bias_parts[1][0:1, :], start=False, stop=False)
                    e.matmul(PS[4 + k][:, 0:WZ], bias_ones[0:1, :], bias_parts[2][0:1, :], start=False, stop=False)
                    return e.matmul(PS[4 + k][:, 0:WZ], M[l][:, k, :],
                                    wts["glr"][:].rearrange("p a n -> p (a n)"), start=False, stop=True)
                st.step(l, f"z{k}", "tensor", zmm, [f"cp{k}", (pv, f"zc{k}", bk)])
                zb = zbuf[k % 2]
                if v2:
                    st.step(l, f"zc{k}", "scalar", lambda e, r, k=k, l=l, zb=zb: e.copy(zb[0][:], PS[4 + k][:, 0:WZ]),
                            [f"z{k}", (l, f"rd{k - 2}", 0) if k >= 2 else (pv, f"rd{k + 2}", bk)])
                    st.step(l, f"lr{k}", "vector", lambda e, r, zb=zb: e.scalar_tensor_tensor(
                        zb[1][:], zb[0][:], 0.2, zb[0][:], ALU.mult, ALU.max), [f"zc{k}"])
                    st.step(l, f"at{k}", "vector", lambda e, r, zb=zb: e.tensor_tensor(
                        zb[1][:], zb[1][:], wts["att_b"][:], ALU.mult), [f"lr{k}"])

                    def rd(e, r, k=k, l=l, zb=zb):
                        t = r * (LANES * TB) + (l * TB + k)
                        return e.tensor_reduce(LG[:, ds(t, 1), :].rearrange("p a h -> p (a h)"),
                                               zb[1][:].rearrange("p (h d) -> p h d", d=D), AX.X, ALU.add)
                    st.step(l, f"rd{k}", "vector", rd, [f"at{k}"])
                else:
                    st.step(l, f"zc{k}", "scalar", lambda e, r, k=k, l=l, zb=zb: e.copy(
                        zb[0][:, 0:2 * HEADS], PS[4 + k][:, 0:2 * HEADS]),
                        [f"z{k}", (l, f"rd{k - 2}", 0) if k >= 2 else (pv, f"rd{k + 2}", bk)])

                    def rd(e, r, k=k, l=l, zb=zb):
                        t = r * (LANES * TB) + (l * TB + k)
                        z = zb[0][:, 0:2 * HEADS]
                        return e.scalar_tensor_tensor(LG[:, ds(t, 1), :].rearrange("p a h -> p (a h)"), z, 0.2, z,
                                                      ALU.mult, ALU.max)
                    st.step(l, f"rd{k}", "vector", rd, [f"zc{k}"])
            front(0)
            for k in range(TB):
                if k + 1 < TB:
                    front(k + 1)
                back_(k)
        st.run()
        ctx.close()

    def softmax_terms():
        with ExitStack() as ctx:
            st = phase()
            ln = Line(st, 0)
            pen = sb(ctx, "pen", [AB, SC])
            a = [sb(ctx, f"smx_a{h}", [AB, SC]) for h in range(HEADS)]
            b = [sb(ctx, f"smx_b{h}", [AB, SC]) for h in range(HEADS)]
            mx = sb(ctx, "smx_m", [P, TILES, HEADS])
            ln.on("vector", lambda e, r: e.tensor_scalar(pen[:], cont[:], -1.0, -LOW, ALU.add, ALU.mult))
            for h in range(HEADS):
                to_scan(ln, h, LG[:, :, h], a[h][:])
            seg_scan(ln, ctx, "m", [x_[:] for x_ in a], [x_[:] for x_ in b], pen[:], "max")

            def only_last(e, r):
                for h in range(HEADS):
                    m = e.tensor_tensor(b[h][:], b[h][:], last[:], ALU.mult)
                return m
            ln.on("vector", only_last)
            seg_scan(ln, ctx, "n", [x_[:] for x_ in b], [x_[:] for x_ in a], nsame[:], "sum", reverse=True)
            for h in range(HEADS):
                from_scan(ln, h, a[h][:], mx[:, :, h])
            ln.on("vector", lambda e, r: e.tensor_tensor(mx[:], mx[:], LG[:, :, HEADS:], ALU.max))

            def sub(e, r):
                e.tensor_tensor(AE[:, :, 0:HEADS], LG[:, :, 0:HEADS], mx[:], ALU.subtract)
                return e.tensor_tensor(AE[:, :, HEADS:], LG[:, :, HEADS:], mx[:], ALU.subtract)
            ln.on("vector", sub)
            ln.on("scalar", lambda e, r: e.activation(AE[:], AE[:], ACT.Exp))
            st.run()

    def attend(tab, tiny, beside=()):
        with ExitStack() as ctx:
            R = [sb(ctx, f"weighted{k}", [P, TB, HEADS * D + HEADS]) for k in range(LANES)]
            ae = [sb(ctx, f"ae{l}", [P, TB, 2 * HEADS]) for l in range(LANES)]
            O = [sb(ctx, f"heads{l}", [P, TB, HEADS * D]) for l in range(LANES)]
            st = phase(LANES, ROUNDS, ahead=2)
            W = HEADS * D
            for l in range(LANES):
                def fe(e, r, l=l):
                    t0 = r * (LANES * TB) + l * TB
                    e.tensor_copy(ae[l][:], AE[:, ds(t0, TB), :])
                    return e.tensor_copy(dst_s[l][:, :], dstc[:, ds(t0, TB + 1)])
                st.step(l, "fetch", "vector", fe, [(l, "store", 1)], early=True)
                st.step(l, "rows", "sync", load_rows(l), [(l, "store", 1)], dmas=1, early=True)
                st.step(l, "feats", "sync", lambda e, r, l=l: [
                    e.dma_start(G[l][:, :, 0, :], block_rows(hs_t, l, r)),
                    e.dma_start(G[l][:, :, 1, :], block_rows(tab, l, r, base=CB))], [(l, "store", 1)], dmas=2, early=True)
                st.step(l, "mask", "vector", masks(l, False), ["fetch", "rows"], early=True)

                def weigh(e, r, l=l):
                    for k in range(TB):
                        e.tensor_tensor(
                            R[l][:, k, 0:W].rearrange("p (h d) -> p h d", h=HEADS),
                            G[l][:, k, 0:1, :].to_broadcast([P, HEADS, D]),
                            ae[l][:, k, 0:HEADS].rearrange("p (h a) -> p h a", a=1).to_broadcast([P, HEADS, D]), ALU.mult)
                    return e.tensor_copy(R[l][:, :, W:], ae[l][:, :, 0:HEADS])
                st.step(l, "weigh", "vector", weigh, ["fetch", "feats"], early=True)
                sums(st, l, lambda k, l=l: R[l][:, k, :], W + HEADS, ["mask", "weigh"])
                den = w4[l]
                st.step(l, "den", "vector", lambda e, r, l=l, den=den: e.tensor_tensor(
                    den[:], S[l][:, :, W:], ae[l][:, :, HEADS:], ALU.add), [f"out{TB - 1}"])
                st.step(l, "den2", "vector", lambda e, r, den=den: e.tensor_scalar(
                    den[:], den[:], tiny, None, ALU.add), ["den"])
                st.step(l, "inv", "vector", lambda e, r, den=den: e.reciprocal(den[:], den[:]), ["den2"])

                def own_term(e, r, l=l):
                    for k in range(TB):
                        m = e.tensor_tensor(
                            O[l][:, k, :].rearrange("p (h d) -> p h d", h=HEADS),
                            G[l][:, k, 1:2, :].to_broadcast([P, HEADS, D]),
                            ae[l][:, k, HEADS:].rearrange("p (h a) -> p h a", a=1).to_broadcast([P, HEADS, D]), ALU.mult)
                    return m
                st.step(l, "own", "vector", own_term, [f"out{TB - 1}"])
                st.step(l, "whole", "vector", lambda e, r, l=l: e.tensor_tensor(O[l][:], O[l][:], S[l][:, :, 0:W], ALU.add),
                        ["own"])

                def share(e, r, l=l, den=den):
                    for k in range(TB):
                        o = O[l][:, k, :].rearrange("p (h d) -> p h d", h=HEADS)
                        m = e.tensor_tensor(o, o, den[:, k, :].rearrange("p (h a) -> p h a", a=1)
                                            .to_broadcast([P, HEADS, D]), ALU.mult)
                    return m
                st.step(l, "share", "vector", share, ["whole", "inv"])
                st.step(l, "store", "sync", lambda e, r, l=l: [e.dma_start(block_rows(agg4, l, r), O[l][:])],
                        ["share"], dmas=1)
            finish(st, beside)

    w4 = [sb(stack, f"den{l}", [P, TB, HEADS]) for l in range(LANES)]

    FC = 4 * P

    def rows_phase(rounds, build):
        with ExitStack() as ctx:
            st = phase(2, rounds)
            add_rows(st, ctx, build, (0, 1), [PS[0:4], PS[4:8]], rounds, False)
            st.run()

    def add_rows(st, ctx, build, lanes, banks, rounds, late, feeds=None):
        lines = []
        for n, l in enumerate(lanes):
            own_steps = Steps(nc, sems, len(lanes), rounds)
            build(Line(own_steps, l), n, ctx, banks[n])
            lines.append((own_steps.list, [s[1] for s in own_steps.list if s[1].startswith("store")]))
        for a in range(len(lines[0][0])):
            for n in range(len(lanes)):
                lane, name, engine, fn, after, dmas, _, _ = lines[n][0][a]
                if a == 0:
                    after = [(lane, s, 1) for s in lines[n][1]] + (feeds(n) if feeds else [])
                st.step(lane, name, engine, fn, after, dmas, late=late)

    def make(ln, l, ctx, bank, block=None):
        if len(bank) == 2:
            bank = [bank[0], bank[1], bank[0]]
        block = block or (lambda r: r * 2 + l)
        made = {}

        def buf(name, cols=FC):
            if name not in made:
                made[name] = sb(ctx, f"{name}_{l}", [P, cols])
            return made[name][:, :]

        def rows_at(tab, r, base):
            return tab[ds(block(r) * (P * NB) + base, P * NB), :].rearrange("(p k) d -> p (k d)", k=NB)

        def load(pairs):
            ln.load(lambda e, r: [e.dma_start(b, rows_at(t, r, base)) for b, t, base in pairs], len(pairs))

        def turn(into, rowsb, step=P, at=0):
            def f(e, r):
                for q in range(4):
                    m = e.transpose(bank[0][:, q * P:(q + 1) * P], rowsb[:, q * step + at:q * step + at + P], ident[:])
                return m
            ln.on("tensor", f)
            ln.on("scalar", lambda e, r: e.copy(into, bank[0][:, :]))

        outs = []

        def unturn(cols, tab, base):
            n = len(outs)
            into = buf(f"out{n % 3}")

            def f(e, r):
                for q in range(4):
                    m = e.transpose(bank[0][:, q * P:(q + 1) * P], cols[:, q * P:(q + 1) * P], ident[:])
                return m
            ln.on("tensor", f)
            if n >= 3:
                ln.after = ln.after + [outs[n - 3]]
            ln.on("vector", lambda e, r: e.tensor_copy(into, bank[0][:, :]))
            outs.append(ln.store(lambda e, r: [e.dma_start(rows_at(tab, r, base), into)]))

        def mm(b, pairs):
            if not pairs:
                return
            def f(e, r):
                for n, (w, v) in enumerate(pairs):
                    m = e.matmul(bank[b][:, :], w, v, start=n == 0, stop=n == len(pairs) - 1)
                return m
            ln.on("tensor", f)

        def bias(into, b, v):
            ln.on("scalar", lambda e, r: e.activation(into, bank[b][:, :], ACT.Identity, bias=wts[v][:, 0:1]))

        def stt(o, a, s, b, o0, o1):
            ln.on("vector", lambda e, r: e.scalar_tensor_tensor(o, a, s, b, o0, o1))

        def tt(o, a, b, op):
            ln.on("vector", lambda e, r: e.tensor_tensor(o, a, b, op))

        def norm_to(o, y, affine=False, centred=False):
            t = buf("tmp")
            if centred:
                c = y
            else:
                mm(1, [(wts["center"][:], y)])
                c = bank[1][:, :]
            ln.on("scalar", lambda e, r: e.activation(t, c, ACT.Square))
            mm(2, [(wts["mean"][:], t)])
            ln.on("scalar", lambda e, r: e.activation(t, bank[2][:, :], ACT.Ln, bias=eps_col[:, 0:1]))
            ln.on("scalar", lambda e, r: e.activation(t, t, ACT.Exp, scale=-0.5))
            tt(o, c, t, ALU.mult)
            if affine:
                ln.on("vector", lambda e, r: e.tensor_scalar(o, o, wts["v_gamma"][:, 0:1], wts["v_beta"][:, 0:1],
                                                             ALU.mult, ALU.add))

        def sage(o, xT, aT=None):
            mm(1, [(wts["bd_sr"][:], xT)] + ([(wts["bd_sl"][:], aT)] if aT is not None else []))
            bias(o, 1, "v_bsl")

        def gat1(o, xT, pairs):
            a, b = buf("a"), buf("b")
            mm(1, pairs)
            bias(a, 1, "v_bg")
            norm_to(a, a, affine=True, centred=True)
            ln.on("vector", lambda e, r: e.tensor_scalar(b, a, 0.0, None, ALU.min))
            ln.on("scalar", lambda e, r: e.activation(b, b, ACT.Exp))
            stt(a, a, 0.0, b, ALU.max, ALU.add)
            stt(a, a, -1.0, xT, ALU.add, ALU.add)
            norm_to(o, a)

        def layer2(o, xT, aT=None):
            a = buf("a")
            mm(1, [(wts["bd_l2root"][:], xT)] + ([(wts["bd_l2w"][:], aT)] if aT is not None else []))
            ln.on("scalar", lambda e, r: e.activation(a, bank[1][:, :], ACT.Relu, bias=wts["v_bl2"][:, 0:1]))
            tt(a, a, xT, ALU.add)
            norm_to(o, a)

        def layer3(o, pairs):
            a = buf("a")
            mm(1, pairs)
            bias(a, 1, "v_bl3")
            norm_to(o, a, centred=True)

        def heads(stackw, more):
            g = buf("g", NB * HEADS * D)
            W = HEADS * D
            count = 4 + len(more)
            for n in range(4):
                q, c = n // 2, n % 2
                t = buf(f"gt{c}")
                turn(t, g, step=2 * W, at=q * W + c * P)
                ln.on("tensor", lambda e, r, n=n, q=q, c=c, t=t: e.matmul(
                    bank[1][:, :], wts[stackw][:, c, q, :], t, start=n == 0, stop=n == count - 1))
            for n, (w, v) in enumerate(more):
                ln.on("tensor", lambda e, r, n=n, w=w, v=v: e.matmul(
                    bank[1][:, :], w, v, start=False, stop=n == len(more) - 1))
            return []
        return dict(buf=buf, load=load, turn=turn, unturn=unturn, mm=mm, bias=bias, stt=stt, tt=tt, norm=norm_to,
                    sage=sage, gat1=gat1, layer2=layer2, layer3=layer3, heads=heads, bank=bank, rows_at=rows_at)

    def dense(st, ctx):
        def build(ln, l, ctx, bank):
            o = make(ln, l, ctx, bank, lambda r: r * 4 + l)
            buf = o["buf"]
            xT, yT, a, b = buf("xT"), buf("yT"), buf("a"), buf("b")
            o["load"]([(a, x0, 0)])
            o["turn"](xT, a)
            for q in range(2):
                o["mm"](1 + q, [(wts["w00"][:, q, :], xT)])
                h = (a, b)[q]
                o["bias"](h, 1 + q, "v_b0")
                o["stt"](h, h, 0.01, h, ALU.mult, ALU.max)
            o["mm"](1, [(wts["w10"][:, 0, :], a), (wts["w10"][:, 1, :], b)])
            o["bias"](a, 1, "v_b1")
            o["stt"](a, a, 0.01, a, ALU.mult, ALU.max)
            o["tt"](a, a, xT, ALU.add)
            o["norm"](yT, a)
            o["unturn"](yT, x1, 0)
            o["sage"](a, yT)
            o["unturn"](a, hh, 0)
            o["gat1"](xT, yT, [(wts["bd_gmean"][:], a)])
            o["unturn"](xT, x2, 0)
            o["layer2"](yT, xT)
            o["unturn"](yT, x3, 0)
            o["layer3"](xT, [(wts["bd_l3"][:], yT)])
            o["unturn"](xT, x4, 0)
        add_rows(st, ctx, build, (4, 5, 6, 7), [PS[2 * n:2 * n + 2] for n in range(4)], ROUNDS, True)

    CR = EP // (P * NB * 2)

    def conv1():
        def build(ln, l, ctx, bank):
            o = make(ln, l, ctx, bank)
            buf = o["buf"]
            K6 = HOPS + 1
            cat = buf("cat", NB * K6 * D)
            catv = cat.rearrange("p (k m d) -> p k m d", k=NB, m=K6)
            y = buf("y", NB * K6 * D)
            yv = y.rearrange("p (k m d) -> p k m d", k=NB, m=K6)
            ln.load(lambda e, r: [e.dma_start(catv[:, :, m, :], tab[ds((r * 2 + l) * (P * NB), P * NB), :]
                                              .rearrange("(p k) d -> p k d", k=NB)) for m, tab in enumerate(hop)], K6)
            for half in range(2):
                ts = []
                for c in range(3):
                    t = buf(f"t{c}")
                    o["turn"](t, cat[:, half * 4 * K6 * D:], step=K6 * D, at=c * P)
                    ts.append((wts["w0cat"][:, c, :], t))
                o["mm"](1, ts)
                h = buf("a")
                o["bias"](h, 1, "v_b0")
                o["stt"](h, h, 0.01, h, ALU.mult, ALU.max)
                for pair in range(2):
                    def ymm(e, r, pair=pair):
                        for j in range(2):
                            c = pair * 2 + j
                            m = e.matmul(bank[2 + j][:, 0:K6 * D], h[:, c * P:(c + 1) * P],
                                         wts["w1cat"][:].rearrange("p k d -> p (k d)"), start=True, stop=True)
                        return m
                    ln.on("tensor", ymm)

                    def ycp(e, r, pair=pair, half=half):
                        for j in range(2):
                            k = half * 4 + pair * 2 + j
                            m = e.copy(y[:, k * K6 * D:(k + 1) * K6 * D], bank[2 + j][:, 0:K6 * D])
                        return m
                    ln.on("scalar", ycp)
            ln.store(lambda e, r: [e.dma_start(tab[ds((r * 2 + l) * (P * NB), P * NB), :]
                                               .rearrange("(p k) d -> p k d", k=NB), yv[:, :, m, :])
                                   for m, tab in enumerate(ytab)], K6)
        rows_phase(CR, build)

    def compact(kind):
        def build(ln, l, ctx, bank):
            o = make(ln, l, ctx, bank)
            buf = o["buf"]
            xT, aT, a, b = buf("xT"), buf("aT"), buf("a"), buf("b")
            r1, r2 = buf("raw1"), buf("raw2")
            if kind == "x1":
                o["load"]([(r1, xc, 0), (r2, utab[0], 0)])
                o["turn"](xT, r1)
                o["turn"](aT, r2)
                ln.on("vector", lambda e, r: e.tensor_scalar(aT, aT, wts["v_b1"][:, 0:1], None, ALU.add))
                o["stt"](aT, aT, 0.01, aT, ALU.mult, ALU.max)
                o["tt"](aT, aT, xT, ALU.add)
                o["norm"](b, aT)
                o["unturn"](b, x1, CB)
            elif kind == "h":
                o["load"]([(r1, x1, CB), (r2, agg, 0)])
                o["turn"](xT, r1)
                o["turn"](aT, r2)
                o["sage"](b, xT, aT)
                o["unturn"](b, hh, CB)
            elif kind == "x3":
                o["load"]([(r1, x2, CB), (r2, agg, 0)])
                o["turn"](xT, r1)
                o["turn"](aT, r2)
                o["layer2"](b, xT, aT)
                o["unturn"](b, x3, CB)
            else:
                g = buf("g", NB * HEADS * D)
                tab, to, w = (x1, x2, "gl_stack") if kind == "x2" else (x3, x4, "g3_stack")
                o["load"]([(r1, tab, CB), (g, agg4, 0)])
                o["turn"](xT, r1)
                if kind == "x2":
                    o["gat1"](aT, xT, o["heads"](w, []))
                else:
                    o["layer3"](aT, o["heads"](w, [(wts["center"][:], xT)]))
                o["unturn"](aT, to, CB)
        return lambda st, ctx: add_rows(st, ctx, build, (4, 5), [PS[4:6], PS[6:8]], ROUNDS, True,
                                        lambda n: [(2 * n, "store", 0), (2 * n + 1, "store", 0)])

    def write_out():
        st = phase()
        ln = Line(st, 0)
        ln.load(lambda e, r: [e.dma_start(out.rearrange("(a n) d -> a (n d)", a=32),
                                          x4[0:N, :].rearrange("(a n) d -> a (n d)", a=32))], 1)
        ln.on("vector", lambda e, r: e.memset(Z[0][:], 0.0))
        st.run()
        st = phase(LANES, ROUNDS, ahead=2)
        for l in range(LANES):
            st.step(l, "fetch", "vector", fetch_all(l, [scat]), [(l, "store_p", 1)], early=True)
            st.step(l, "feats", "sync", lambda e, r, l=l: [e.dma_start(G[l][:, :, 0, :], block_rows(x4, l, r, base=CB))],
                    [(l, "store_p", 1)], dmas=1, early=True)

            def sc(e, r, l=l):
                return [e.indirect_dma_start(
                    out=out, out_offset=bass.IndirectOffsetOnAxis(ap=idx_s[l][:, 0, k:k + 1], axis=0),
                    in_=G[l][:, k, 0, :], in_offset=None, bounds_check=N - 1, oob_is_err=False) for k in range(TB)]
            st.step(l, "store_p", "gpsimd", sc, ["fetch", "feats"], dmas=TB)
        st.run()

    place_nodes()
    find_sources([dense])
    finish_indices()
    for k in range(HOPS):
        edge_sum(hop[k], EP - 1, posx, norm, None, hop[k + 1])
    conv1()
    for k in range(HOPS - 1, 0, -1):
        edge_sum(utab[k + 1], EP - 1, posx, norm, None, utab[k], add=ytab[k])
    edge_sum(utab[1], EP - 1, posx, norm, None, utab[0], add=ytab[0], beside=[compact("x1")])
    edge_sum(x1, CB + EP - 1, comb, None, rcnt, agg, beside=[compact("h")])
    logits(hh, True)
    softmax_terms()
    attend(hh, 0.0, beside=[compact("x2")])
    edge_sum(x2, CB + EP - 1, comb, None, rcnt, agg, beside=[compact("x3")])
    logits(x3, False)
    softmax_terms()
    attend(x3, 1e-16, beside=[compact("x4")])
    write_out()
    stack.close()


_INS = ["x", "src", "dst", "edge_weight", "edge_weight1", "L0_gnn_W0", "L0_gnn_b0", "L0_gnn_W1", "L0_gnn_b1",
        "L1_gnn_W_sl", "L1_gnn_b_sl", "L1_gnn_W_sr", "L1_gnn_Wg_l", "L1_gnn_bg_l", "L1_gnn_Wg_r", "L1_gnn_bg_r",
        "L1_gnn_att", "L1_gnn_b_gat", "L1_gnn_gamma", "L1_gnn_beta", "L2_gnn_W", "L2_gnn_root", "L2_gnn_bias",
        "L3_gnn_W", "L3_gnn_att_src", "L3_gnn_att_dst", "L3_gnn_bias", "L3_gnn_dense_w", "L3_gnn_dense_b"]


def kernel(**inputs):
    import numpy as _np
    import concourse.bacc as _bacc
    from concourse import mybir as _mybir
    from concourse.bass_utils import run_bass_kernel_spmd as _run

    nc = _bacc.Bacc("TRN2", target_bir_lowering=False, num_devices=1)
    arrays, args = {}, []
    for name in _INS:
        a = _np.ascontiguousarray(inputs[name])
        arrays[f"in_{name}_dram"] = a
        args.append(nc.dram_tensor(f"in_{name}_dram", a.shape, _mybir.dt.from_np(a.dtype), kind="ExternalInput").ap())
    args.append(nc.dram_tensor("out_0_dram", (N, D), _mybir.dt.float32, kind="ExternalOutput").ap())
    bass_gnn_resnorm(nc, *args)
    r = _run(nc, [arrays], core_ids=[0])
    return r.results[0]["out_0_dram"]
```

```python
import concourse.bass as bass
from concourse import mybir
from concourse.alu_op_type import AluOpType as ALU
from contextlib import ExitStack

F32 = mybir.dt.float32
I32 = mybir.dt.int32
BF16 = mybir.dt.bfloat16
ACT = mybir.ActivationFunctionType
AX = mybir.AxisListType

N = 100000
E = 50000
D = 64
HID = 128
HOPS = 5
HEADS = 4
P = 128
TB = 4
LANES = 4
ROUNDS = -(-E // (P * TB * LANES))
TILES = ROUNDS * LANES * TB
EP = TILES * P
AB = EP // (P * TB)
SC = P * TB
NB = 8
CB = LANES * ROUNDS * P * NB
assert CB >= N
ABSENT = 1 << 20
NO_NODE = (1 << 17) - 1
EPS = 1e-5
LOW = -1.0e30
ENGINES = ("sync", "gpsimd", "scalar", "vector", "tensor")


class Steps:

    def __init__(self, nc, sems, lanes, rounds, ahead=0):
        self.nc, self.sems, self.lanes, self.rounds, self.ahead = nc, sems, lanes, rounds, ahead
        self.list, self.late, self.place, self.per, self.base = [], [], {}, {}, {}

    def step(self, lane, name, engine, fn, after, dmas=0, early=False, late=False):
        key = (lane, name if dmas else engine)
        amount = 16 * dmas if dmas else 1
        if key not in self.base:
            if key not in self.sems:
                self.sems[key] = [self.nc.alloc_semaphore(f"done_{key[1]}_{lane}"), 0]
            self.base[key], self.per[key] = self.sems[key][1], 0
        self.per[key] += amount
        self.place[(lane, name)] = (key, self.per[key])
        entry = (lane, name, engine, fn, after, dmas, early, key)
        (self.late if late else self.list).append(entry)

    def emit(self, eng, which, i, s, shift):
        lane, name, engine, fn, after, dmas, early, key = s
        if engine != which:
            return
        waited = False
        r = i + shift
        for a in after:
            l, n, back = a if isinstance(a, tuple) else (lane, a, 0)
            k, upto = self.place[(l, n)]
            value = (r - back) * self.per[k] + (self.base[k] + upto)
            if isinstance(value, int) and value <= 0:
                continue
            eng.wait_ge(self.sems[k][0], value)
            if which in ("gpsimd", "sync"):
                eng.sem_inc(self.sems["waits_" + which][0], 1)
            waited = True
        made = fn(eng, r)
        if dmas:
            assert len(made) == dmas, (name, len(made), dmas)
            for m in made:
                m.then_inc(self.sems[key][0], 16)
        else:
            made.then_inc(self.sems[key][0], 1)

    def credit(self, eng, which):
        for lane, name, engine, fn, after, dmas, early, key in self.list + self.late:
            if engine == which and key in self.credits:
                n = self.credits[key]
                del self.credits[key]
                if not dmas:
                    eng.sem_inc(self.sems[key][0], n)
                else:
                    scratch, source = self.sems["scratch"]
                    at = self.sems["scratch_used"]
                    self.sems["scratch_used"] += 1
                    eng.dma_start(scratch[:, 8 * at:8 * at + 8], source).then_inc(self.sems[key][0], n)

    def sequence(self):
        if not self.ahead:
            body = [(s, 0) for s in self.list]
        else:
            body = []
            for l in range(self.lanes):
                for level in (self.ahead, 1):
                    m = (l + level) % self.lanes
                    delay = 0 if l + level >= self.lanes else 1
                    body += [(s, delay) for s in self.list if s[0] == m and s[6] == (
                        "next" if level == 1 else True)]
                body += [(s, 1) for s in self.list if s[0] == l and not s[6]]
        placed = [((n + 0.5) / len(body), 0, n, x) for n, x in enumerate(body)]
        behind = 2 if self.ahead else 0
        late = [(s, behind) for s in self.late]
        placed += [((n + 0.5) / len(late), 1, n, x) for n, x in enumerate(late)]
        return [x for *_, x in sorted(placed, key=lambda t: t[:3])]

    def program(self, eng, which):
        queue = self.sequence()
        if which == "scalar" and self.late:
            eng.preload_act_table_set("natural_log_exp_and_others")
        most = max(d for _, d in queue)
        for t in range(most):
            for s, d in queue:
                if t >= d:
                    self.emit(eng, which, t - d, s, 0)
        steady = self.rounds - most
        if steady > 1:
            with eng.Fori(0, steady, 1) as i:
                for s, d in queue:
                    self.emit(eng, which, i, s, most - d)
        else:
            for s, d in queue:
                self.emit(eng, which, 0, s, most - d)
        for t in range(self.rounds, self.rounds + most):
            for s, d in queue:
                if t - d < self.rounds:
                    self.emit(eng, which, t - d, s, 0)

    def run(self):
        self.credits = {}
        for k in self.base:
            if self.rounds > 1 and self.base[k] < self.per[k]:
                self.credits[k] = self.per[k]
                self.base[k] += self.per[k]
        block = self.nc.Block()
        with block:
            for which in ENGINES:
                def program(eng, which=which):
                    if any(s[2] == which for s in self.list + self.late):
                        self.credit(eng, which)
                        self.program(eng, which)
                    if which == "sync":
                        for k in self.base:
                            if isinstance(k[1], str) and k[1].startswith("store"):
                                eng.wait_ge(self.sems[k][0], self.base[k] + self.per[k] * self.rounds)
                program_of(block, which)(program)
        for k in self.base:
            self.sems[k][1] = self.base[k] + self.per[k] * self.rounds


def program_of(block, which):
    return {"sync": block.sync, "gpsimd": block.gpsimd, "scalar": block.scalar,
            "vector": block.vector, "tensor": block.tensor}[which]


def ds(i, n):
    return bass.ds(i, n)


class Line:

    def __init__(self, steps, lane, first=()):
        self.steps, self.lane, self.n, self.after = steps, lane, 0, list(first)
        self.dma = 0
        self.load_after = None

    def _add(self, engine, fn, dmas=0, kind="", name=None):
        self.n += 1
        name = f"{kind}{self.dma}" if dmas else name or f"s{self.n}"
        self.dma += bool(dmas)
        self.steps.step(self.lane, name, engine, fn, self.after, dmas)
        return name

    def on(self, engine, fn, name=None):
        self.after = [self._add(engine, fn, name=name)]

    def load(self, fn, dmas):
        self.after = [self._add("sync", fn, dmas, "load")]

    def store(self, fn, dmas=1, engine="sync"):
        return self._add(engine, fn, dmas, "store_soft" if engine == "gpsimd" else "store")


def bass_gnn_resnorm(nc, x, src, dst, edge_weight, edge_weight1, W0, b0, W1, b1, W_sl, b_sl, W_sr, Wg_l, bg_l,
                     Wg_r, bg_r, att, b_gat, gamma, beta, L2W, L2root, L2bias, L3W, att_src, att_dst,
                     L3bias, dense_w, dense_b, out):
    stack = ExitStack()
    sems = {"waits_" + e: [nc.alloc_semaphore("waits_" + e), 0] for e in ("gpsimd", "sync")}

    def dram(name, shape, dt=F32):
        return nc.dram_tensor(name, shape, dt, kind="Internal").ap()

    named = {}

    def sb(ctx, name, shape, dt=F32):
        named[name] = named.get(name, 0) + 1
        return ctx.enter_context(nc.sbuf_tensor(f"{name}_{named[name]}", shape, dt))

    dst_p = dram("dst_padded", (EP + 2,), I32)
    src_p = dram("src_padded", (EP,), I32)
    w_p = dram("w_padded", (EP,))
    place = dram("place_of_node", (CB, 2), I32)
    x0 = dram("x0", (CB, D))
    xc = dram("xc", (EP, D))
    hop = [xc] + [dram(f"hop{k}", (EP, D)) for k in range(1, HOPS + 1)]
    h1t = dram("h1_transposed", (HID, EP))
    utab = [dram(f"u{k}", (EP, D)) for k in range(HOPS + 1)]
    x1, hh, x2, x3 = (dram(n, (CB + EP, D)) for n in ("x1", "h_sage", "x2", "x3"))
    x4 = dram("x4", (CB + EP, D))
    agg = dram("agg", (EP, D))
    hs_t = dram("source_features", (EP, D))
    agg4 = dram("agg_heads", (EP, HEADS * D))

    PS = [stack.enter_context(nc.psum_tensor(f"bank{b}", [P, 512], F32)) for b in range(8)]
    ident = sb(stack, "ident", [P, P])
    eps_col = sb(stack, "eps_col", [P, 1])
    last_row = sb(stack, "last_row", [P, 1])
    dstc = sb(stack, "dst_of_edge", [P, TILES + 1])
    comb = sb(stack, "row_of_source", [P, TILES], I32)
    posx = sb(stack, "compact_row_of_source", [P, TILES], I32)
    lastx = sb(stack, "row_of_last_edge", [P, TILES], I32)
    scat = sb(stack, "node_to_write", [P, TILES], I32)
    dsti = sb(stack, "dst_index", [P, TILES], I32)
    srci = sb(stack, "src_index", [P, TILES], I32)
    norm = sb(stack, "norm_of_edge", [P, TILES])
    rcnt = sb(stack, "one_over_count", [P, TILES])
    LG = sb(stack, "logits", [P, TILES, 2 * HEADS])
    AE = LG
    idx_s, dst_s, w_s, rows, M, C, G, S, Z = ([] for _ in range(9))
    for l in range(LANES):
        idx_s.append(sb(stack, f"idx_slot{l}", [P, 2, TB], I32))
        dst_s.append(sb(stack, f"dst_slot{l}", [P, TB + 1]))
        w_s.append(sb(stack, f"weight_slot{l}", [P, TB]))
        rows.append(sb(stack, f"dst_rows{l}", [P, TB, P], I32))
        M.append(sb(stack, f"same_dst{l}", [P, TB, P]))
        C.append(sb(stack, f"goes_on{l}", [P, TB, P]))
        G.append(sb(stack, f"gathered{l}", [P, TB, 2, D]))
        S.append(sb(stack, f"sums{l}", [P, TB, HEADS * D + HEADS]))
        Z.append(sb(stack, f"work{l}", [P, TB * D]))

    sems["scratch"] = (sb(stack, "credit_scratch", [16, 8 * 64]), x[0:16, 0:8])
    sems["scratch_used"] = 0

    def phase(lanes=1, rounds=1, ahead=0):
        return Steps(nc, sems, lanes, rounds, ahead)

    wts = {}
    with nc.allow_non_contiguous_dma(reason="small weights"):
        with ExitStack() as ctx:
            raw = {}

            def w_sb(name, shape):
                wts[name] = sb(stack, name, shape)
                return wts[name]

            st = phase()
            ln = Line(st, 0)
            for n in ("bd_sl", "bd_sr", "bd_gmean", "bd_l2w", "bd_l2root", "bd_l3", "center", "mean"):
                w_sb(n, [P, P])
            w_sb("w00", [P, 2, P])
            w_sb("w10", [P, 2, P])
            w_sb("w0cat", [P, 3, P])
            w_sb("w1cat", [P, HOPS + 1, D])
            w_sb("gl_stack", [P, 2, 2, P])
            w_sb("g3_stack", [P, 2, 2, P])
            w_sb("glr", [P, 2, HEADS * D])
            w_sb("g3cols", [P, 2 * HEADS])
            w_sb("att_b", [P, 2 * HEADS * D])
            w_sb("bias_lr", [P, HEADS * D])
            for n in ("b0", "b1", "bsl", "bg", "gamma", "beta", "bl2", "bl3"):
                w_sb("v_" + n, [P, 1])
            t_w3 = sb(ctx, "t_w3", [D, HEADS * D])
            t_w3T = sb(ctx, "t_w3T", [D, HEADS, D])
            t_dw = sb(ctx, "t_dw", [D, HEADS, D])
            t_as = sb(ctx, "t_as", [D, HEADS])
            t_ad = sb(ctx, "t_ad", [D, HEADS])
            t_gl = sb(ctx, "t_gl", [P, HEADS * D])
            t_b3 = sb(ctx, "t_b3", [D, HEADS])
            t_bg = sb(ctx, "t_bg", [P, HEADS])
            t_bb = sb(ctx, "t_bb", [P, 3])
            t_br = sb(ctx, "t_br", [P, 2, HEADS * D])
            big = sb(ctx, "big", [P, CB // P, 2], I32)
            padv = sb(ctx, "padv", [1, 512], I32)
            zero = sb(ctx, "zero", [P, 256])

            def clear(eng, r):
                for t in (*wts.values(), t_gl, t_b3):
                    eng.memset(t[:], 0.0)
                for l in range(LANES):
                    for t in (G[l], S[l], w_s[l], Z[l], M[l], C[l]):
                        eng.memset(t[:], 0.0)
                    eng.memset(idx_s[l][:], 0)
                eng.memset(LG[:], 0.0)
                eng.memset(padv[:, 0:510], NO_NODE)
                eng.memset(padv[0:1, 510:511], -1)
                eng.memset(big[:, :, 0], ABSENT)
                eng.memset(big[:, :, 1], 0)
                eng.memset(zero[:], 0.0)
                eng.memset(eps_col[:], EPS)
                return eng.memset(dstc[:, 0:1], -1.0)

            def clear2(eng, r):
                eng.memset(wts["center"][0:D, 0:D], -1.0 / D)
                eng.memset(wts["center"][D:P, D:P], -1.0 / D)
                eng.memset(wts["mean"][0:D, 0:D], 1.0 / D)
                return eng.memset(wts["mean"][D:P, D:P], 1.0 / D)

            ln.on("vector", clear)
            ln.on("vector", clear2)

            def loads(eng, r):
                d = []

                def put(o, i_):
                    d.append(eng.dma_start(o, i_))
                for q, (lo, hi) in enumerate(((0, D), (D, P))):
                    put(wts["bd_sl"][lo:hi, lo:hi], W_sl)
                    put(wts["bd_sr"][lo:hi, lo:hi], W_sr)
                    put(wts["bd_l2w"][lo:hi, lo:hi], L2W)
                    put(wts["bd_l2root"][lo:hi, lo:hi], L2root)
                    put(wts["w00"][lo:hi, q, :], W0[0, :, :])
                    put(wts["w10"][:, q, lo:hi], W1[0, :, :])
                    for n, v in (("b1", b1), ("bsl", b_sl), ("gamma", gamma), ("beta", beta), ("bl2", L2bias)):
                        put(wts["v_" + n][lo:hi, :], v.rearrange("(p a) -> p a", a=1))
                    put(t_bg[lo:hi, :], bg_l.rearrange("(h p) -> p h", h=HEADS))
                    put(t_bb[lo:hi, 0:1], b_gat.rearrange("(p a) -> p a", a=1))
                    put(t_bb[lo:hi, 1:2], dense_b.rearrange("(p a) -> p a", a=1))
                    put(t_gl[lo:hi, :], Wg_l)
                put(wts["v_b0"][:, :], b0.rearrange("(p a) -> p a", a=1))
                put(wts["w0cat"][:, :, :], W0.rearrange("k f m -> (k f) m").rearrange("(c p) m -> p c m", p=P))
                put(wts["w1cat"][:, :, :], W1.rearrange("k f m -> f k m"))
                for c in range(2):
                    for q in range(2):
                        for j in range(2):
                            h = 2 * c + j
                            put(wts["gl_stack"][j * D:(j + 1) * D, c, q, q * D:(q + 1) * D],
                                Wg_l[:, h * D:(h + 1) * D])
                put(wts["glr"][0:D, 0, :], Wg_l)
                put(wts["glr"][D:P, 0, :], Wg_r)
                put(wts["glr"][D:P, 1, :], Wg_r)
                for s in range(2):
                    put(wts["att_b"][:, s * HEADS * D:(s + 1) * HEADS * D],
                        att.rearrange("h d -> (h d)").partition_broadcast(P))
                put(t_br[:, 0, :], bg_l.partition_broadcast(P))
                put(t_br[:, 1, :], bg_r.partition_broadcast(P))
                put(t_w3[:, :], L3W)
                put(t_dw[:, :, :], dense_w.rearrange("(h p) n -> p h n", h=HEADS))
                put(t_as[:, :], att_src.rearrange("h d -> d h"))
                put(t_ad[:, :], att_dst.rearrange("h d -> d h"))
                put(t_b3[:, :], L3bias.rearrange("(h p) -> p h", h=HEADS))
                row = lambda a: a.rearrange("(a n) -> a n", a=1)
                put(row(dst_p[1:E + 1]), row(dst))
                put(row(src_p[0:E]), row(src))
                put(row(w_p[0:E]), row(edge_weight))
                put(row(dst_p[0:1]), padv[0:1, 510:511])
                put(row(dst_p[EP + 1:EP + 2]), padv[0:1, 510:511])
                at = E
                while at < EP:
                    n = min(EP - at, 500)
                    put(row(dst_p[at + 1:at + 1 + n]), padv[0:1, 0:n])
                    at += n
                pad = EP - E
                assert (CB - N) % 96 == 0
                q = 48
                put(src_p[E:EP].rearrange("(p n) -> p n", p=q), zero[0:q, 0:pad // q].bitcast(I32))
                put(w_p[E:EP].rearrange("(p n) -> p n", p=q), zero[0:q, 0:pad // q])
                put(place.rearrange("(p n) w -> p n w", p=P), big[:, :, :])
                put(x0[0:N, :].rearrange("(a n) d -> a (n d)", a=32), x.rearrange("(a n) d -> a (n d)", a=32))
                for k in range((CB - N) // 96):
                    put(x0[N + 96 * k:N + 96 * (k + 1), :], zero[0:96, 0:D])
                return d

            count = [0]

            class Counter:
                def dma_start(self, o, i_):
                    count[0] += 1
                    return 0
            loads(Counter(), 0)
            ln.load(loads, count[0])

            def diagonal(eng, r):
                return eng.affine_select(out=ident[:], in_=ident[:], compare_op=ALU.not_equal, fill=1.0, base=0,
                                         pattern=[[-1, P]], channel_multiplier=1)
            ln.on("vector", lambda e, r: e.memset(ident[:], 0.0))
            ln.on("gpsimd", diagonal)
            ln.on("vector", lambda e, r: e.tensor_copy(last_row[:], ident[:, P - 1:P]))

            def tr3(e, r):
                for h in range(HEADS):
                    m = e.transpose(PS[0][0:D, h * D:(h + 1) * D], t_w3[:, h * D:(h + 1) * D], ident[0:D, 0:D])
                return m
            ln.on("tensor", tr3)
            ln.on("vector", lambda e, r: e.tensor_copy(t_w3T[:].rearrange("p h d -> p (h d)"), PS[0][0:D, 0:HEADS * D]))

            def prods(e, r):
                for h in range(HEADS):
                    w = t_w3T[:, h, :]
                    e.matmul(PS[1][0:D, h:h + 1], w, t_as[:, h:h + 1], start=True, stop=True)
                    e.matmul(PS[1][0:D, HEADS + h:HEADS + h + 1], w, t_ad[:, h:h + 1], start=True, stop=True)
                    e.matmul(PS[2][0:D, h * D:(h + 1) * D], w, t_dw[:, h, :], start=True, stop=True)
                for h in range(HEADS):
                    m = e.matmul(PS[3][0:D, 0:1], t_dw[:, h, :], t_b3[:, h:h + 1], start=h == 0, stop=h == HEADS - 1)
                return m
            ln.on("tensor", prods)

            scr = sb(ctx, "scr", [D, 2 * HEADS + 1 + HEADS * D])

            def cp1(e, r):
                e.tensor_copy(scr[:, 0:2 * HEADS], PS[1][0:D, 0:2 * HEADS])
                e.tensor_copy(scr[:, 2 * HEADS + 1:], PS[2][0:D, 0:HEADS * D])
                return e.tensor_copy(scr[:, 2 * HEADS:2 * HEADS + 1], PS[3][0:D, 0:1])
            ln.on("vector", cp1)
            s_as, s_ad, s_c = scr[:, 0:HEADS], scr[:, HEADS:2 * HEADS], scr[:, 2 * HEADS:2 * HEADS + 1]
            s_wd = scr[:, 2 * HEADS + 1:].rearrange("p (h d) -> p h d", h=HEADS)
            s_sum = sb(ctx, "s_sum", [D, HEADS])
            s_m3 = sb(ctx, "s_m3", [D, D])
            ln.on("vector", lambda e, r: e.tensor_tensor(s_sum[:], s_as, s_ad, ALU.add))
            ln.on("vector", lambda e, r: e.tensor_reduce(s_m3[:], s_wd.rearrange("p h d -> p d h"), AX.X, ALU.add))
            ln.on("vector", lambda e, r: e.tensor_tensor(s_c, s_c, t_bb[0:D, 1:2], ALU.add))

            def spread(e, r):
                d = [e.dma_start(wts["g3cols"][0:D, 0:HEADS], s_as),
                     e.dma_start(wts["g3cols"][D:P, 0:HEADS], s_ad),
                     e.dma_start(wts["g3cols"][D:P, HEADS:2 * HEADS], s_sum[:])]
                for q in range(2):
                    d.append(e.dma_start(wts["bd_l3"][q * D:(q + 1) * D, q * D:(q + 1) * D], s_m3[:]))
                    d.append(e.dma_start(wts["v_bl3"][q * D:(q + 1) * D, :], s_c))
                    for c in range(2):
                        for j in range(2):
                            d.append(e.dma_start(wts["g3_stack"][j * D:(j + 1) * D, c, q, q * D:(q + 1) * D],
                                                 s_wd[:, 2 * c + j, :]))
                return d
            ln.load(spread, 3 + 2 * (2 + 4))
            t_m = sb(ctx, "t_m", [P, D])
            t_v = sb(ctx, "t_v", [P, 1])
            ln.on("vector", lambda e, r: e.tensor_reduce(t_m[:], t_gl[:].rearrange("p (h d) -> p d h", h=HEADS), AX.X, ALU.add))
            ln.on("vector", lambda e, r: e.tensor_reduce(t_v[:], t_bg[:], AX.X, ALU.add))

            def fin(e, r):
                q = 1.0 / HEADS
                for a in range(2):
                    sl = slice(a * D, (a + 1) * D)
                    e.tensor_scalar(wts["bd_gmean"][sl, sl], t_m[sl, :], q, None, ALU.mult)
                e.tensor_scalar(wts["v_bg"][:], t_v[:], q, t_bb[:, 0:1], ALU.mult, ALU.add)
                g = wts["gl_stack"][:].rearrange("p c q m -> p (c q m)")
                e.tensor_scalar(g, g, q, None, ALU.mult)
                e.tensor_tensor(wts["glr"][D:P, 1, :], wts["glr"][D:P, 1, :], t_gl[D:P, :], ALU.add)
                e.tensor_tensor(wts["center"][:], wts["center"][:], ident[:], ALU.add)
                return e.tensor_tensor(wts["bias_lr"][:], t_br[:, 0, :], t_br[:, 1, :], ALU.add)
            ln.on("vector", fin)
            ln.on("vector", lambda e, r: e.tensor_tensor(wts["bd_l3"][:], wts["bd_l3"][:], ident[:], ALU.add))
            squares = [wts["bd_gmean"][:], wts["bd_l3"][:]] + [
                wts[n][:, c, q, :] for n in ("gl_stack", "g3_stack") for c in range(2) for q in range(2)]
            turned = sb(ctx, "turned", [P, P])
            for w in squares:
                ln.on("tensor", lambda e, r, w=w: e.transpose(PS[0][:, 0:P], w, ident[:]))
                ln.on("vector", lambda e, r: e.tensor_copy(turned[:], PS[0][:, 0:P]))
                ln.on("tensor", lambda e, r: e.matmul(PS[1][:, 0:P], turned[:], wts["center"][:], start=True, stop=True))
                ln.on("vector", lambda e, r, w=w: e.tensor_copy(w, PS[1][:, 0:P]))
            for n in ("v_bg", "v_bl3"):
                ln.on("tensor", lambda e, r, n=n: e.matmul(PS[1][:, 0:1], wts["center"][:], wts[n][:], start=True, stop=True))
                ln.on("vector", lambda e, r, n=n: e.tensor_copy(wts[n][:], PS[1][:, 0:1]))
            st.run()

    def seg_scan(ln, ctx, tag, vals, outs, go, kind, reverse=False):
        V = len(vals)
        ends = sb(ctx, f"ends{tag}", [AB, 2, P])
        ends_r = sb(ctx, f"endsr{tag}", [P, 2, AB])
        carry = sb(ctx, f"carry{tag}", [P, AB + 1])
        ini = sb(ctx, f"ini{tag}", [AB, P])
        o0, o1, none = (ALU.mult, ALU.add, 0.0) if kind == "sum" else (ALU.add, ALU.max, LOW)
        rev = (lambda a: a[:, ::-1]) if reverse else (lambda a: a)
        end = 0 if reverse else SC - 1

        def scan(init):
            def f(e, r):
                for v in range(V):
                    m = e.tensor_tensor_scan(rev(outs[v]), rev(go), rev(vals[v]), init(v), o0, o1)
                return m
            return f
        ln.on("vector", lambda e, r: e.memset(ends[:], 0.0))
        ln.on("vector", scan(lambda v: none))

        def collect(e, r):
            for v in range(V):
                e.tensor_copy(ends[:, 0, v:v + 1], outs[v][:, end:end + 1])
            return e.tensor_reduce(ends[:, 1, 0:1], go, AX.X, ALU.min)
        ln.on("vector", collect)
        ln.on("vector", lambda e, r: e.tensor_copy(ends[:, 1, 1:V + 1], ends[:, 1, 0:1].to_broadcast([AB, V])))

        def tr(e, r):
            e.transpose(PS[6][:, 0:AB], ends[:, 0, :], ident[0:AB, 0:AB])
            return e.transpose(PS[6][:, P:P + AB], ends[:, 1, :], ident[0:AB, 0:AB])
        ln.on("tensor", tr)

        def back(e, r):
            e.tensor_copy(ends_r[:, 0, :], PS[6][:, 0:AB])
            e.memset(carry[:], none)
            return e.tensor_copy(ends_r[:, 1, :], PS[6][:, P:P + AB])
        ln.on("vector", back)
        o = carry[:, 0:AB] if reverse else carry[:, 1:AB + 1]
        ln.on("vector", lambda e, r: e.tensor_tensor_scan(rev(o), rev(ends_r[:, 1, :]), rev(ends_r[:, 0, :]), none, o0, o1))
        into = carry[:, 1:AB + 1] if reverse else carry[:, 0:AB]
        ln.on("tensor", lambda e, r: e.transpose(PS[7][0:AB, 0:P], into, ident[:, :]))
        ln.on("vector", lambda e, r: e.tensor_copy(ini[:], PS[7][0:AB, 0:P]))
        ln.on("vector", scan(lambda v: ini[:, v:v + 1]))

    def from_scan(ln, k, src_ap, dst_ap):
        def tr(e, r):
            for g in range(TB):
                m = e.transpose(PS[k][:, g * AB:(g + 1) * AB], src_ap[:, g * P:(g + 1) * P], ident[0:AB, 0:AB])
            return m
        ln.on("tensor", tr)
        ln.on("vector", lambda e, r: e.tensor_copy(dst_ap.rearrange("p (a g) -> p g a", g=TB),
                                                   PS[k][:, 0:TB * AB].rearrange("p (g a) -> p g a", g=TB)))

    def to_scan(ln, k, src_ap, dst_ap):
        v = src_ap.rearrange("p (a g) -> p g a", g=TB)

        def tr(e, r):
            for g in range(TB):
                m = e.transpose(PS[k][0:AB, g * P:(g + 1) * P], v[:, g, :], ident[:, :])
            return m
        ln.on("tensor", tr)
        ln.on("vector", lambda e, r: e.tensor_copy(dst_ap, PS[k][0:AB, :]))

    cont = sb(stack, "same_as_before", [AB, SC])
    nsame = sb(stack, "same_as_next", [AB, SC])
    last = sb(stack, "is_last", [AB, SC])
    wd = sb(stack, "w_times_dis", [P, TILES])
    own = sb(stack, "own_place", [P, TILES, 2], I32)
    found = sb(stack, "source_place", [P, TILES, 2], I32)

    with ExitStack() as ctx:
        st = phase()
        ln = Line(st, 0)
        t = {n: sb(ctx, "p1_" + n, [AB, SC], I32) for n in ("d", "dp", "dn", "s")}
        f = {n: sb(ctx, "p1f_" + n, [AB, SC]) for n in
             ("w", "one", "deg", "cnt", "d", "s", "m", "r", "rk", "fr", "fd", "ld", "lr", "sc")}

        def loads(e, r):
            v = lambda a: a.rearrange("(a n) -> a n", a=AB)
            return [e.dma_start(t["d"][:], v(dst_p[1:EP + 1])), e.dma_start(t["dp"][:], v(dst_p[0:EP])),
                    e.dma_start(t["dn"][:], v(dst_p[2:EP + 2])), e.dma_start(t["s"][:], v(src_p[:])),
                    e.dma_start(f["w"][:], v(w_p[:]))]
        ln.load(loads, 5)

        def flags(e, r):
            e.tensor_tensor(cont[:], t["d"][:], t["dp"][:], ALU.is_equal)
            e.tensor_tensor(nsame[:], t["d"][:], t["dn"][:], ALU.is_equal)
            e.tensor_copy(f["d"][:], t["d"][:])
            e.tensor_copy(f["s"][:], t["s"][:])
            return e.memset(f["one"][:], 1.0)
        ln.on("vector", flags)
        ln.on("vector", lambda e, r: e.tensor_scalar(last[:], nsame[:], -1.0, 1.0, ALU.mult, ALU.add))
        ri = sb(ctx, "ri", [AB, SC], I32)
        ln.on("gpsimd", lambda e, r: e.iota(ri[:].rearrange("a (g p) -> a g p", g=TB), pattern=[[1, TB], [TB, P]],
                                            base=0, channel_multiplier=SC))
        ln.on("gpsimd", lambda e, r: e.iota(own[:, :, 0].rearrange("p (a g) -> p a g", g=TB),
                                            pattern=[[SC, AB], [1, TB]], base=0, channel_multiplier=TB))
        seg_scan(ln, ctx, "a", [f["w"][:], f["one"][:]], [f["deg"][:], f["cnt"][:]], cont[:], "sum")
        ln.on("vector", lambda e, r: e.tensor_scalar(f["m"][:], f["deg"][:], 0.0, None, ALU.is_gt))
        ln.on("vector", lambda e, r: e.tensor_scalar(f["r"][:], f["m"][:], -1.0, 1.0, ALU.mult, ALU.add))
        ln.on("vector", lambda e, r: e.tensor_tensor(f["r"][:], f["r"][:], f["deg"][:], ALU.add))
        ln.on("scalar", lambda e, r: e.activation(f["r"][:], f["r"][:], ACT.Sqrt))
        ln.on("vector", lambda e, r: e.reciprocal(f["r"][:], f["r"][:]))
        ln.on("vector", lambda e, r: e.tensor_tensor(f["r"][:], f["r"][:], f["m"][:], ALU.mult))

        def prep(e, r):
            e.tensor_copy(f["rk"][:], ri[:])
            e.tensor_tensor(f["ld"][:], f["r"][:], last[:], ALU.mult)
            e.tensor_scalar(f["cnt"][:], f["cnt"][:], 1.0, None, ALU.max)
            return e.tensor_scalar(f["sc"][:], f["d"][:], float(-ABSENT), None, ALU.add)
        ln.on("vector", prep)

        def prep2(e, r):
            e.reciprocal(f["cnt"][:], f["cnt"][:])
            e.tensor_tensor(f["sc"][:], f["sc"][:], last[:], ALU.mult)
            return e.tensor_tensor(f["lr"][:], f["rk"][:], last[:], ALU.mult)
        ln.on("vector", prep2)
        seg_scan(ln, ctx, "b", [f["ld"][:], f["lr"][:]], [f["fd"][:], f["fr"][:]], nsame[:], "sum", reverse=True)

        def prep3(e, r):
            e.tensor_scalar(f["sc"][:], f["sc"][:], float(ABSENT), None, ALU.add)
            e.tensor_scalar(f["fr"][:], f["fr"][:], float(CB), None, ALU.add)
            return e.tensor_tensor(f["m"][:], f["w"][:], f["fd"][:], ALU.mult)
        ln.on("vector", prep3)
        disw = own[:, :, 1].bitcast(F32)
        for k, (a, b) in enumerate(((f["d"], dstc[:, 1:]), (f["d"], dsti[:]), (f["s"], srci[:]), (f["m"], wd[:]),
                                    (f["cnt"], rcnt[:]), (f["sc"], scat[:]), (f["fr"], lastx[:]), (f["r"], disw))):
            from_scan(ln, k % 6, a[:], b)
        st.run()

    def fetch_all(l, cols, weight=None):
        def f(e, r):
            t0 = r * (LANES * TB) + l * TB
            m = e.tensor_copy(dst_s[l][:, :], dstc[:, ds(t0, TB + 1)])
            for n, c in enumerate(cols):
                m = e.tensor_copy(idx_s[l][:, n, :], c[:, ds(t0, TB)])
            if weight is not None:
                m = e.tensor_copy(w_s[l][:, :], weight[:, ds(t0, TB)])
            return m
        return f

    def load_rows(l):
        return lambda e, r: [e.dma_start(rows[l][:].rearrange("p t n -> p (t n)"),
                                         dst_p[ds((r * LANES + l) * (TB * P) + 1, TB * P)].partition_broadcast(P))]

    def gather(l, pairs):
        def f(e, r):
            d = []
            for k in range(TB):
                for tab, where, n, top in pairs:
                    d.append(e.indirect_dma_start(
                        out=where(l, k), out_offset=None, in_=tab,
                        in_offset=bass.IndirectOffsetOnAxis(ap=idx_s[l][:, n, k:k + 1], axis=0),
                        bounds_check=top, oob_is_err=False))
            return d
        return f

    def masks(l, weighted):
        def f(e, r):
            for k in range(TB):
                if weighted:
                    e.tensor_scalar(M[l][:, k, :], rows[l][:, k, :], dst_s[l][:, k + 1:k + 2], w_s[l][:, k:k + 1],
                                    ALU.is_equal, ALU.mult)
                else:
                    e.tensor_scalar(M[l][:, k, :], rows[l][:, k, :], dst_s[l][:, k + 1:k + 2], None, ALU.is_equal)
                m = e.tensor_scalar(C[l][96:P, k, :], rows[l][96:P, k, :], dst_s[l][96:P, k:k + 1],
                                    last_row[96:P, :], ALU.is_equal, ALU.mult)
            return m
        return f

    def block_rows(tab, l, r, w=D, base=0):
        return tab[ds((r * LANES + l) * (TB * P) + base, TB * P), :].rearrange("(p k) d -> p k d", k=TB)

    def sums(st, l, rhs, width, first, other=None, copied=None, free="store"):
        copied = copied or width
        for k in range(TB):
            def main(e, r, k=k):
                if other is not None:
                    other(e, k)
                return e.matmul(PS[k][:, 0:width], M[l][:, k, :], rhs(k), start=True, stop=False)

            def carry(e, r, k=k):
                pl = l if k else (l - 1) % LANES
                pk = (k - 1) % TB
                return e.matmul(PS[k][:, 0:width], C[l][96:P, k, :], S[pl][96:P, pk, 0:width], start=False, stop=True)
            prev_lane, back = (l - 1) % LANES, (1 if l == 0 else 0)
            st.step(l, f"main{k}", "tensor", main, (first if k == 0 else []) + [(prev_lane, f"out{k}", back)])
            before = f"out{k - 1}" if k else (prev_lane, f"out{TB - 1}", back)
            st.step(l, f"carry{k}", "tensor", carry, [before])
            st.step(l, f"out{k}", "scalar",
                    lambda e, r, k=k: e.copy(S[l][:, k, 0:copied], PS[k][:, 0:copied]),
                    [f"carry{k}"] + ([(l, free, 1)] if k == 0 else []))

    def edge_sum(tab, top, index, weight, scale, target, add=None, beside=()):
        post = add is not None or scale is not None
        st = phase(LANES, ROUNDS, ahead=3)
        for l in range(LANES):
            st.step(l, "fetch", "vector", fetch_all(l, [index], weight if scale is None else scale),
                    [(l, "mask", 1), (l, f"main{TB - 1}", 1)] + ([(l, "post", 1)] if scale is not None else []),
                    early=True)
            st.step(l, "rows", "sync", load_rows(l), [(l, "mask", 1)], dmas=1, early=True)
            if add is not None:
                st.step(l, "hidden", "sync", lambda e, r, l=l: [e.dma_start(
                    hT[l][:], h1t[:, ds((r * LANES + l) * SC, SC)])], [(l, f"main{TB - 1}", 1)], dmas=1, early=True)
            st.step(l, "gather", "gpsimd", gather(l, [(tab, lambda l, k: G[l][:, k, 0, :], 0, top)]), ["fetch"],
                    dmas=TB, early=True)
            st.step(l, "mask", "vector", masks(l, weight is not None), ["fetch", "rows", (l, f"carry{TB - 1}", 1)],
                    early="next")
            apart = add is not None and not beside
            beside_sum = None if add is None else (
                lambda e, k, l=l: e.matmul(PS[4 + l][:, k * D:(k + 1) * D] if apart else PS[k][:, D:2 * D],
                                           hT[l][:, k * P:(k + 1) * P], wts["w1cat"][:, add, :], start=True, stop=True))
            sums(st, l, lambda k, l=l: G[l][:, k, 0, :], D, ["mask", "gather"] + (["hidden"] if add is not None else [])
                 + ([(l, "post", 1)] if apart else []), beside_sum, 2 * D if add is not None and not apart else D,
                 "post" if post else "store")
            if add is not None:
                st.step(l, "post", "vector", lambda e, r, l=l: e.tensor_tensor(
                    Z[l][:].rearrange("p (k d) -> p k d", k=TB),
                    PS[4 + l][:, 0:TB * D].rearrange("p (k d) -> p k d", k=TB) if apart else S[l][:, :, D:2 * D],
                    S[l][:, :, 0:D], ALU.add), [f"out{TB - 1}", (l, "store", 1)])
            elif scale is not None:
                st.step(l, "post", "vector", lambda e, r, l=l: e.tensor_tensor(
                    Z[l][:].rearrange("p (k d) -> p k d", k=TB), S[l][:, :, 0:D],
                    w_s[l][:].rearrange("p (k a) -> p k a", a=1).to_broadcast([P, TB, D]), ALU.mult),
                    [f"out{TB - 1}", (l, "store", 1)])
            direct = add is None and scale is None
            st.step(l, "store", "sync", lambda e, r, l=l: [e.dma_start(
                block_rows(target, l, r), S[l][:, :, 0:D] if direct else
                Z[l][:].rearrange("p (k d) -> p k d", k=TB))],
                [f"out{TB - 1}"] if direct else ["post"], dmas=1)
        finish(st, beside)

    def finish(st, beside):
        with ExitStack() as ctx:
            for rows_work in beside:
                rows_work(st, ctx)
            st.run()

    def place_nodes(beside=()):
        st = phase(LANES, ROUNDS, ahead=2)
        for l in range(LANES):
            def fe(e, r, l=l):
                t0 = r * (LANES * TB) + l * TB
                e.tensor_copy(G[l][:, :, 0, 0:2].bitcast(I32), own[:, ds(t0, TB), :])
                return e.tensor_copy(idx_s[l][:, 0, :], scat[:, ds(t0, TB)])
            st.step(l, "fetch", "vector", fe, [(l, "store_p", 1)], early=True)

            def sc(e, r, l=l):
                return [e.indirect_dma_start(
                    out=place, out_offset=bass.IndirectOffsetOnAxis(ap=idx_s[l][:, 0, k:k + 1], axis=0),
                    in_=G[l][:, k, 0, 0:2].bitcast(I32), in_offset=None, bounds_check=N - 1, oob_is_err=False)
                    for k in range(TB)]
            st.step(l, "store_p", "gpsimd", sc, ["fetch"], dmas=TB)
        finish(st, beside)

    def find_sources(beside=()):
        st = phase(LANES, ROUNDS, ahead=2)
        for l in range(LANES):
            st.step(l, "fetch", "vector", fetch_all(l, [srci, dsti]), [(l, "store", 1), (l, "keep", 1)], early=True)
            st.step(l, "gather2", "gpsimd", gather(l, [
                (place, lambda l, k: G[l][:, k, 1, 0:2].bitcast(I32), 0, N - 1),
                (x, lambda l, k: G[l][:, k, 0, :], 1, N - 1)]), ["fetch"], dmas=2 * TB, early=True)

            def keep(e, r, l=l):
                return e.tensor_copy(found[:, ds(r * (LANES * TB) + l * TB, TB), :], G[l][:, :, 1, 0:2].bitcast(I32))
            st.step(l, "keep", "vector", keep, ["gather2"])
            st.step(l, "store", "sync", lambda e, r, l=l: [e.dma_start(block_rows(xc, l, r), G[l][:, :, 0, :])],
                    ["gather2"], dmas=1)
        finish(st, beside)

    def finish_indices():
        with ExitStack() as ctx:
            st = phase()
            ln = Line(st, 0)
            pf, sf, v = (sb(ctx, n, [P, TILES]) for n in ("pf", "sf", "v"))

            def a(e, r):
                e.tensor_copy(pf[:], found[:, :, 0])
                e.tensor_copy(sf[:], srci[:])
                e.tensor_copy(posx[:], found[:, :, 0])
                return e.tensor_tensor(norm[:], wd[:], found[:, :, 1].bitcast(F32), ALU.mult)
            ln.on("vector", a)
            ln.on("vector", lambda e, r: e.tensor_scalar(v[:], pf[:], float(ABSENT), None, ALU.is_lt))
            ln.on("vector", lambda e, r: e.scalar_tensor_tensor(pf[:], pf[:], float(CB), sf[:], ALU.add, ALU.subtract))
            ln.on("vector", lambda e, r: e.tensor_tensor(pf[:], pf[:], v[:], ALU.mult))
            ln.on("vector", lambda e, r: e.tensor_tensor(comb[:], pf[:], sf[:], ALU.add))
            st.run()

    def logits(tab, v2):
        st = phase(LANES, ROUNDS, ahead=2)
        WZ = 2 * HEADS * D
        ctx = ExitStack()
        zbuf = [[sb(ctx, f"z{k}{j}", [P, WZ]) for j in range(2)] for k in range(2)]
        for l in range(LANES):
            st.step(l, "fetch", "vector", fetch_all(l, [comb, lastx]), [(l, "store", 1), (l, "tr3", 1)], early=True)
            st.step(l, "gather2", "gpsimd", gather(l, [
                (tab, lambda l, k: G[l][:, k, 0, :], 0, CB + EP - 1),
                (tab, lambda l, k: G[l][:, k, 1, :], 1, CB + EP - 1)]), ["fetch"], dmas=2 * TB, early=True)
            st.step(l, "store", "sync", lambda e, r, l=l: [e.dma_start(block_rows(hs_t, l, r), G[l][:, :, 0, :])],
                    ["gather2"], dmas=1)
            pv, bk = (l - 1) % LANES, (1 if l == 0 else 0)
            def front(k, l=l, pv=pv, bk=bk):
                def tr(e, r, k=k, l=l):
                    return e.transpose(PS[k][:, 0:P], G[l][:, k, :, :].rearrange("p a d -> p (a d)"), ident[:])
                st.step(l, f"tr{k}", "tensor", tr, (["gather2"] if k == 0 else []) + [(pv, f"cp{k}", bk)])
                st.step(l, f"cp{k}", "scalar", lambda e, r, k=k, l=l: e.copy(M[l][:, k, :], PS[k][:, 0:P]),
                        [f"tr{k}", (l, f"z{k}", 1)])

            def back_(k, l=l, pv=pv, bk=bk):
                def zmm(e, r, k=k, l=l):
                    if not v2:
                        return e.matmul(PS[4 + k][:, 0:2 * HEADS], M[l][:, k, :], wts["g3cols"][:], start=True, stop=True)
                    return e.matmul(PS[4 + k][:, 0:WZ], M[l][:, k, :],
                                    wts["glr"][:].rearrange("p a n -> p (a n)"), start=True, stop=True)
                st.step(l, f"z{k}", "tensor", zmm, [f"cp{k}", (pv, f"zc{k}", bk)])
                zb = zbuf[k % 2]
                if v2:
                    st.step(l, f"zc{k}", "vector", lambda e, r, k=k, zb=zb: e.tensor_tensor(
                        zb[0][:].rearrange("p (a n) -> p a n", a=2),
                        PS[4 + k][:, 0:WZ].rearrange("p (a n) -> p a n", a=2),
                        wts["bias_lr"][:].rearrange("p (a n) -> p a n", a=1).to_broadcast([P, 2, HEADS * D]), ALU.add),
                        [f"z{k}", (l, f"rd{k - 2}", 0) if k >= 2 else (pv, f"rd{k + 2}", bk)])
                    st.step(l, f"lr{k}", "vector", lambda e, r, zb=zb: e.scalar_tensor_tensor(
                        zb[1][:], zb[0][:], 0.2, zb[0][:], ALU.mult, ALU.max), [f"zc{k}"])
                    st.step(l, f"at{k}", "vector", lambda e, r, zb=zb: e.tensor_tensor(
                        zb[1][:], zb[1][:], wts["att_b"][:], ALU.mult), [f"lr{k}"])

                    def rd(e, r, k=k, l=l, zb=zb):
                        t = r * (LANES * TB) + (l * TB + k)
                        return e.tensor_reduce(LG[:, ds(t, 1), :].rearrange("p a h -> p (a h)"),
                                               zb[1][:].rearrange("p (h d) -> p h d", d=D), AX.X, ALU.add)
                    st.step(l, f"rd{k}", "vector", rd, [f"at{k}"])
                else:
                    st.step(l, f"zc{k}", "scalar", lambda e, r, k=k, l=l, zb=zb: e.copy(
                        zb[0][:, 0:2 * HEADS], PS[4 + k][:, 0:2 * HEADS]),
                        [f"z{k}", (l, f"rd{k - 2}", 0) if k >= 2 else (pv, f"rd{k + 2}", bk)])

                    def rd(e, r, k=k, l=l, zb=zb):
                        t = r * (LANES * TB) + (l * TB + k)
                        z = zb[0][:, 0:2 * HEADS]
                        return e.scalar_tensor_tensor(LG[:, ds(t, 1), :].rearrange("p a h -> p (a h)"), z, 0.2, z,
                                                      ALU.mult, ALU.max)
                    st.step(l, f"rd{k}", "vector", rd, [f"zc{k}"])
            front(0)
            for k in range(TB):
                if k + 1 < TB:
                    front(k + 1)
                back_(k)
        st.run()
        ctx.close()

    def softmax_terms():
        with ExitStack() as ctx:
            st = phase()
            ln = Line(st, 0)
            pen = sb(ctx, "pen", [AB, SC])
            a = [sb(ctx, f"smx_a{h}", [AB, SC]) for h in range(HEADS)]
            b = [sb(ctx, f"smx_b{h}", [AB, SC]) for h in range(HEADS)]
            mx = sb(ctx, "smx_m", [P, TILES, HEADS])
            ln.on("vector", lambda e, r: e.tensor_scalar(pen[:], cont[:], -1.0, -LOW, ALU.add, ALU.mult))
            for h in range(HEADS):
                to_scan(ln, h, LG[:, :, h], a[h][:])
            seg_scan(ln, ctx, "m", [x_[:] for x_ in a], [x_[:] for x_ in b], pen[:], "max")

            def only_last(e, r):
                for h in range(HEADS):
                    m = e.tensor_tensor(b[h][:], b[h][:], last[:], ALU.mult)
                return m
            ln.on("vector", only_last)
            seg_scan(ln, ctx, "n", [x_[:] for x_ in b], [x_[:] for x_ in a], nsame[:], "sum", reverse=True)
            for h in range(HEADS):
                from_scan(ln, h, a[h][:], mx[:, :, h])
            ln.on("vector", lambda e, r: e.tensor_tensor(mx[:], mx[:], LG[:, :, HEADS:], ALU.max))

            def sub(e, r):
                e.tensor_tensor(AE[:, :, 0:HEADS], LG[:, :, 0:HEADS], mx[:], ALU.subtract)
                return e.tensor_tensor(AE[:, :, HEADS:], LG[:, :, HEADS:], mx[:], ALU.subtract)
            ln.on("vector", sub)
            ln.on("scalar", lambda e, r: e.activation(AE[:], AE[:], ACT.Exp))
            st.run()

    def attend(tab, tiny, beside=()):
        with ExitStack() as ctx:
            R = [sb(ctx, f"weighted{k}", [P, TB, HEADS * D + HEADS]) for k in range(LANES)]
            ae = [sb(ctx, f"ae{l}", [P, TB, 2 * HEADS]) for l in range(LANES)]
            O = [sb(ctx, f"heads{l}", [P, TB, HEADS * D]) for l in range(LANES)]
            st = phase(LANES, ROUNDS, ahead=3)
            W = HEADS * D
            for l in range(LANES):
                def fe(e, r, l=l):
                    t0 = r * (LANES * TB) + l * TB
                    e.tensor_copy(ae[l][:], AE[:, ds(t0, TB), :])
                    return e.tensor_copy(dst_s[l][:, :], dstc[:, ds(t0, TB + 1)])
                st.step(l, "fetch", "vector", fe, [(l, "store", 1)], early=True)
                st.step(l, "rows", "sync", load_rows(l), [(l, "store", 1)], dmas=1, early=True)
                st.step(l, "feats", "sync", lambda e, r, l=l: [
                    e.dma_start(G[l][:, :, 0, :], block_rows(hs_t, l, r)),
                    e.dma_start(G[l][:, :, 1, :], block_rows(tab, l, r, base=CB))], [(l, "store", 1)], dmas=2, early=True)
                st.step(l, "mask", "vector", masks(l, False), ["fetch", "rows"], early="next")

                def weigh(e, r, l=l):
                    for k in range(TB):
                        e.tensor_tensor(
                            R[l][:, k, 0:W].rearrange("p (h d) -> p h d", h=HEADS),
                            G[l][:, k, 0:1, :].to_broadcast([P, HEADS, D]),
                            ae[l][:, k, 0:HEADS].rearrange("p (h a) -> p h a", a=1).to_broadcast([P, HEADS, D]), ALU.mult)
                    return e.tensor_copy(R[l][:, :, W:], ae[l][:, :, 0:HEADS])
                st.step(l, "weigh", "vector", weigh, ["fetch", "feats"], early="next")
                sums(st, l, lambda k, l=l: R[l][:, k, :], W + HEADS, ["mask", "weigh"])
                den = w4[l]
                st.step(l, "den", "vector", lambda e, r, l=l, den=den: e.tensor_tensor(
                    den[:], S[l][:, :, W:], ae[l][:, :, HEADS:], ALU.add), [f"out{TB - 1}"])
                st.step(l, "den2", "vector", lambda e, r, den=den: e.tensor_scalar(
                    den[:], den[:], tiny, None, ALU.add), ["den"])
                st.step(l, "inv", "vector", lambda e, r, den=den: e.reciprocal(den[:], den[:]), ["den2"])

                def own_term(e, r, l=l):
                    for k in range(TB):
                        m = e.tensor_tensor(
                            O[l][:, k, :].rearrange("p (h d) -> p h d", h=HEADS),
                            G[l][:, k, 1:2, :].to_broadcast([P, HEADS, D]),
                            ae[l][:, k, HEADS:].rearrange("p (h a) -> p h a", a=1).to_broadcast([P, HEADS, D]), ALU.mult)
                    return m
                st.step(l, "own", "vector", own_term, [f"out{TB - 1}"])
                st.step(l, "whole", "vector", lambda e, r, l=l: e.tensor_tensor(O[l][:], O[l][:], S[l][:, :, 0:W], ALU.add),
                        ["own"])

                def share(e, r, l=l, den=den):
                    for k in range(TB):
                        o = O[l][:, k, :].rearrange("p (h d) -> p h d", h=HEADS)
                        m = e.tensor_tensor(o, o, den[:, k, :].rearrange("p (h a) -> p h a", a=1)
                                            .to_broadcast([P, HEADS, D]), ALU.mult)
                    return m
                st.step(l, "share", "vector", share, ["whole", "inv"])
                st.step(l, "store", "sync", lambda e, r, l=l: [e.dma_start(block_rows(agg4, l, r), O[l][:])],
                        ["share"], dmas=1)
            finish(st, beside)

    w4 = [sb(stack, f"den{l}", [P, TB, HEADS]) for l in range(LANES)]

    FC = 4 * P

    def rows_phase(rounds, build, lanes):
        with ExitStack() as ctx:
            st = phase(len(lanes), rounds)
            step = 8 // len(lanes)
            add_rows(st, ctx, build, lanes, [PS[step * n:step * (n + 1)] for n in range(len(lanes))], rounds, True)
            st.run()

    def add_rows(st, ctx, build, lanes, banks, rounds, late, feeds=None):
        lines = []
        for n, l in enumerate(lanes):
            own_steps = Steps(nc, sems, len(lanes), rounds)
            line = Line(own_steps, l)
            build(line, n, ctx, banks[n])
            lines.append((own_steps.list, line.load_after or
                          [s[1] for s in own_steps.list if s[1].startswith("store")]))
        for a in range(len(lines[0][0])):
            for n in range(len(lanes)):
                lane, name, engine, fn, after, dmas, _, _ = lines[n][0][a]
                if a == 0:
                    after = [(lane, s, 1) for s in lines[n][1]] + (feeds(n) if feeds else [])
                st.step(lane, name, engine, fn, after, dmas, late=late)

    def make(ln, l, ctx, bank, block=None):
        if len(bank) == 2:
            bank = [bank[0], bank[1], bank[0]]
        block = block or (lambda r: r * 2 + l)
        made = {}

        def buf(name, cols=FC):
            if name not in made:
                made[name] = sb(ctx, f"{name}_{l}", [P, cols])
            return made[name][:, :]

        def rows_at(tab, r, base):
            return tab[ds(block(r) * (P * NB) + base, P * NB), :].rearrange("(p k) d -> p (k d)", k=NB)

        def load(pairs):
            ln.load(lambda e, r: [e.dma_start(b, rows_at(t, r, base)) for b, t, base in pairs], len(pairs))

        def turn(into, rowsb, step=P, at=0):
            def f(e, r):
                for q in range(4):
                    m = e.transpose(bank[0][:, q * P:(q + 1) * P], rowsb[:, q * step + at:q * step + at + P], ident[:])
                return m
            ln.on("tensor", f)
            ln.on("scalar", lambda e, r: e.copy(into, bank[0][:, :]))

        outs = []

        def unturn(cols, tab, base):
            n = len(outs)
            into = buf(f"out{n % 3}")

            def f(e, r):
                for q in range(4):
                    m = e.transpose(bank[0][:, q * P:(q + 1) * P], cols[:, q * P:(q + 1) * P], ident[:])
                return m
            ln.on("tensor", f)
            if n >= 3:
                ln.after = ln.after + [outs[n - 3]]
            ln.on("vector", lambda e, r: e.tensor_copy(into, bank[0][:, :]))
            outs.append(ln.store(lambda e, r: [e.dma_start(rows_at(tab, r, base), into)]))

        def mm(b, pairs):
            if not pairs:
                return
            def f(e, r):
                for n, (w, v) in enumerate(pairs):
                    m = e.matmul(bank[b][:, :], w, v, start=n == 0, stop=n == len(pairs) - 1)
                return m
            ln.on("tensor", f)

        def bias(into, b, v):
            ln.on("scalar", lambda e, r: e.activation(into, bank[b][:, :], ACT.Identity, bias=wts[v][:, 0:1]))

        def stt(o, a, s, b, o0, o1):
            ln.on("vector", lambda e, r: e.scalar_tensor_tensor(o, a, s, b, o0, o1))

        def tt(o, a, b, op):
            ln.on("vector", lambda e, r: e.tensor_tensor(o, a, b, op))

        def norm_to(o, y, affine=False, centred=False):
            t = buf("tmp")
            if centred:
                c = y
            else:
                mm(1, [(wts["center"][:], y)])
                c = bank[1][:, :]
            ln.on("scalar", lambda e, r: e.activation(t, c, ACT.Square))
            mm(2, [(wts["mean"][:], t)])
            ln.on("scalar", lambda e, r: e.activation(t, bank[2][:, :], ACT.Ln, bias=eps_col[:, 0:1]))
            ln.on("scalar", lambda e, r: e.activation(t, t, ACT.Exp, scale=-0.5))
            tt(o, c, t, ALU.mult)
            if affine:
                ln.on("vector", lambda e, r: e.tensor_scalar(o, o, wts["v_gamma"][:, 0:1], wts["v_beta"][:, 0:1],
                                                             ALU.mult, ALU.add))

        def sage(o, xT, aT=None):
            mm(1, [(wts["bd_sr"][:], xT)] + ([(wts["bd_sl"][:], aT)] if aT is not None else []))
            bias(o, 1, "v_bsl")

        def gat1(o, xT, pairs):
            a, b = buf("a"), buf("b")
            mm(1, pairs)
            bias(a, 1, "v_bg")
            norm_to(a, a, affine=True, centred=True)
            ln.on("vector", lambda e, r: e.tensor_scalar(b, a, 0.0, None, ALU.min))
            ln.on("scalar", lambda e, r: e.activation(b, b, ACT.Exp))
            stt(a, a, 0.0, b, ALU.max, ALU.add)
            stt(a, a, -1.0, xT, ALU.add, ALU.add)
            norm_to(o, a)

        def layer2(o, xT, aT=None):
            a = buf("a")
            mm(1, [(wts["bd_l2root"][:], xT)] + ([(wts["bd_l2w"][:], aT)] if aT is not None else []))
            ln.on("scalar", lambda e, r: e.activation(a, bank[1][:, :], ACT.Relu, bias=wts["v_bl2"][:, 0:1]))
            tt(a, a, xT, ALU.add)
            norm_to(o, a)

        def layer3(o, pairs):
            a = buf("a")
            mm(1, pairs)
            bias(a, 1, "v_bl3")
            norm_to(o, a, centred=True)

        def heads(stackw, more):
            g = buf("g", NB * HEADS * D)
            W = HEADS * D
            count = 4 + len(more)
            for n in range(4):
                q, c = n // 2, n % 2
                t = buf(f"gt{c}")
                turn(t, g, step=2 * W, at=q * W + c * P)
                ln.on("tensor", lambda e, r, n=n, q=q, c=c, t=t: e.matmul(
                    bank[1][:, :], wts[stackw][:, c, q, :], t, start=n == 0, stop=n == count - 1))
            for n, (w, v) in enumerate(more):
                ln.on("tensor", lambda e, r, n=n, w=w, v=v: e.matmul(
                    bank[1][:, :], w, v, start=False, stop=n == len(more) - 1))
            return []
        return dict(buf=buf, load=load, turn=turn, unturn=unturn, mm=mm, bias=bias, stt=stt, tt=tt, norm=norm_to,
                    sage=sage, gat1=gat1, layer2=layer2, layer3=layer3, heads=heads, bank=bank, rows_at=rows_at)

    def dense(st, ctx):
        def build(ln, l, ctx, bank):
            o = make(ln, l, ctx, bank, lambda r: r * 4 + l)
            buf = o["buf"]
            xT, yT, a, b = buf("xT"), buf("yT"), buf("a"), buf("b")
            o["load"]([(a, x0, 0)])
            o["turn"](xT, a)
            for q in range(2):
                o["mm"](1 + q, [(wts["w00"][:, q, :], xT)])
                h = (a, b)[q]
                o["bias"](h, 1 + q, "v_b0")
                o["stt"](h, h, 0.01, h, ALU.mult, ALU.max)
            o["mm"](1, [(wts["w10"][:, 0, :], a), (wts["w10"][:, 1, :], b)])
            o["bias"](a, 1, "v_b1")
            o["stt"](a, a, 0.01, a, ALU.mult, ALU.max)
            o["tt"](a, a, xT, ALU.add)
            o["norm"](yT, a)
            o["unturn"](yT, x1, 0)
            o["sage"](a, yT)
            o["unturn"](a, hh, 0)
            o["gat1"](xT, yT, [(wts["bd_gmean"][:], a)])
            o["unturn"](xT, x2, 0)
            o["layer2"](yT, xT)
            o["unturn"](yT, x3, 0)
            o["layer3"](xT, [(wts["bd_l3"][:], yT)])
            o["unturn"](xT, x4, 0)
        add_rows(st, ctx, build, (4, 5, 6, 7), [PS[2 * n:2 * n + 2] for n in range(4)], ROUNDS, True)

    def conv1():
        def build(ln, l, ctx, bank):
            o = make(ln, l, ctx, bank)
            buf = o["buf"]
            K6 = HOPS + 1
            cat = buf("cat", TB * K6 * D)
            catv = cat.rearrange("p (k m d) -> p k m d", k=TB, m=K6)
            ln.load(lambda e, r: [e.dma_start(catv[:, :, m, :], block_rows(tab, l, r)) for m, tab in enumerate(hop)], K6)
            lane = ln.lane
            ln.after = ln.after + [(lane, "y_copied", 1)]
            for c in range(3):
                t = buf(f"t{c % 2}")
                o["turn"](t, cat, step=K6 * D, at=c * P)
                ln.on("tensor", lambda e, r, c=c, t=t: e.matmul(bank[1][:, :], wts["w0cat"][:, c, :], t,
                                                                start=c == 0, stop=c == 2), f"product{c}")
            ln.load_after = ["product2"]
            h, y = buf("h"), buf("y", TB * D)
            ln.after = ln.after + [(lane, "store_soft1", 1)]
            o["bias"](h, 1, "v_b0")
            o["stt"](h, h, 0.01, h, ALU.mult, ALU.max)
            ln.store(lambda e, r: [e.dma_start(h1t[:, ds((r * LANES + l) * SC, SC)], h)], engine="gpsimd")

            def ymm(e, r):
                for k in range(TB):
                    m = e.matmul(bank[0][:, k * D:(k + 1) * D], h[:, k * P:(k + 1) * P], wts["w1cat"][:, HOPS, :],
                                 start=True, stop=True)
                return m
            ln.on("tensor", ymm)
            ln.after = ln.after + [(lane, "store_soft2", 1)]
            ln.on("vector", lambda e, r: e.tensor_copy(y, bank[0][:, 0:TB * D]), "y_copied")
            ln.store(lambda e, r: [e.dma_start(block_rows(utab[HOPS], l, r), y.rearrange("p (k d) -> p k d", k=TB))],
                     engine="gpsimd")
        rows_phase(ROUNDS, build, (4, 5, 6, 7))

    def compact(kind):
        def build(ln, l, ctx, bank):
            o = make(ln, l, ctx, bank)
            buf = o["buf"]
            xT, aT, a, b = buf("xT"), buf("aT"), buf("a"), buf("b")
            r1, r2 = buf("raw1"), buf("raw2")
            if kind == "x1":
                o["load"]([(r1, xc, 0), (r2, utab[0], 0)])
                o["turn"](xT, r1)
                o["turn"](aT, r2)
                ln.on("vector", lambda e, r: e.tensor_scalar(aT, aT, wts["v_b1"][:, 0:1], None, ALU.add))
                o["stt"](aT, aT, 0.01, aT, ALU.mult, ALU.max)
                o["tt"](aT, aT, xT, ALU.add)
                o["norm"](b, aT)
                o["unturn"](b, x1, CB)
            elif kind == "h":
                o["load"]([(r1, x1, CB), (r2, agg, 0)])
                o["turn"](xT, r1)
                o["turn"](aT, r2)
                o["sage"](b, xT, aT)
                o["unturn"](b, hh, CB)
            elif kind == "x3":
                o["load"]([(r1, x2, CB), (r2, agg, 0)])
                o["turn"](xT, r1)
                o["turn"](aT, r2)
                o["layer2"](b, xT, aT)
                o["unturn"](b, x3, CB)
            else:
                g = buf("g", NB * HEADS * D)
                tab, to, w = (x1, x2, "gl_stack") if kind == "x2" else (x3, x4, "g3_stack")
                o["load"]([(r1, tab, CB), (g, agg4, 0)])
                o["turn"](xT, r1)
                if kind == "x2":
                    o["gat1"](aT, xT, o["heads"](w, []))
                else:
                    o["layer3"](aT, o["heads"](w, [(wts["center"][:], xT)]))
                o["unturn"](aT, to, CB)
        return lambda st, ctx: add_rows(st, ctx, build, (4, 5), [PS[4:6], PS[6:8]], ROUNDS, True,
                                        lambda n: [(2 * n, "store", 0), (2 * n + 1, "store", 0)])

    def write_out():
        st = phase()
        ln = Line(st, 0)
        ln.load(lambda e, r: [e.dma_start(out.rearrange("(a n) d -> a (n d)", a=32),
                                          x4[0:N, :].rearrange("(a n) d -> a (n d)", a=32))], 1)
        ln.on("vector", lambda e, r: e.memset(Z[0][:], 0.0))
        st.run()
        st = phase(LANES, ROUNDS, ahead=2)
        for l in range(LANES):
            st.step(l, "fetch", "vector", fetch_all(l, [scat]), [(l, "store_p", 1)], early=True)
            st.step(l, "feats", "sync", lambda e, r, l=l: [e.dma_start(G[l][:, :, 0, :], block_rows(x4, l, r, base=CB))],
                    [(l, "store_p", 1)], dmas=1, early=True)

            def sc(e, r, l=l):
                return [e.indirect_dma_start(
                    out=out, out_offset=bass.IndirectOffsetOnAxis(ap=idx_s[l][:, 0, k:k + 1], axis=0),
                    in_=G[l][:, k, 0, :], in_offset=None, bounds_check=N - 1, oob_is_err=False) for k in range(TB)]
            st.step(l, "store_p", "gpsimd", sc, ["fetch", "feats"], dmas=TB)
        st.run()

    place_nodes()
    find_sources([dense])
    finish_indices()
    for k in range(HOPS):
        edge_sum(hop[k], EP - 1, posx, norm, None, hop[k + 1])
    conv1()
    with ExitStack() as ctx:
        hT = [sb(ctx, f"hidden_block{l}", [P, SC]) for l in range(LANES)]
        for k in range(HOPS - 1, -1, -1):
            edge_sum(utab[k + 1], EP - 1, posx, norm, None, utab[k], add=k, beside=[] if k else [compact("x1")])
    edge_sum(x1, CB + EP - 1, comb, None, rcnt, agg, beside=[compact("h")])
    logits(hh, True)
    softmax_terms()
    attend(hh, 0.0, beside=[compact("x2")])
    edge_sum(x2, CB + EP - 1, comb, None, rcnt, agg, beside=[compact("x3")])
    logits(x3, False)
    softmax_terms()
    attend(x3, 1e-16, beside=[compact("x4")])
    write_out()
    stack.close()


_INS = ["x", "src", "dst", "edge_weight", "edge_weight1", "L0_gnn_W0", "L0_gnn_b0", "L0_gnn_W1", "L0_gnn_b1",
        "L1_gnn_W_sl", "L1_gnn_b_sl", "L1_gnn_W_sr", "L1_gnn_Wg_l", "L1_gnn_bg_l", "L1_gnn_Wg_r", "L1_gnn_bg_r",
        "L1_gnn_att", "L1_gnn_b_gat", "L1_gnn_gamma", "L1_gnn_beta", "L2_gnn_W", "L2_gnn_root", "L2_gnn_bias",
        "L3_gnn_W", "L3_gnn_att_src", "L3_gnn_att_dst", "L3_gnn_bias", "L3_gnn_dense_w", "L3_gnn_dense_b"]


def kernel(**inputs):
    import numpy as _np
    import concourse.bacc as _bacc
    from concourse import mybir as _mybir
    from concourse.bass_utils import run_bass_kernel_spmd as _run

    nc = _bacc.Bacc("TRN2", target_bir_lowering=False, num_devices=1)
    arrays, args = {}, []
    for name in _INS:
        a = _np.ascontiguousarray(inputs[name])
        arrays[f"in_{name}_dram"] = a
        args.append(nc.dram_tensor(f"in_{name}_dram", a.shape, _mybir.dt.from_np(a.dtype), kind="ExternalInput").ap())
    args.append(nc.dram_tensor("out_0_dram", (N, D), _mybir.dt.float32, kind="ExternalOutput").ap())
    bass_gnn_resnorm(nc, *args)
    r = _run(nc, [arrays], core_ids=[0])
    return r.results[0]["out_0_dram"]
```
